# Optimizing a Trainium2 kernel written in Bass

```python
import numpy as np
import jax
import jax.numpy as jnp

def _softmax(x, axis=-1):
    return jax.nn.softmax(x, axis=axis)

def _gelu(x):
    return jax.nn.gelu(x, approximate=True)

def _silu(x):
    return jax.nn.silu(x)

def _sigmoid(x):
    return jax.nn.sigmoid(x)

def _layernorm(x, axis=-1, eps=1e-05):
    m = jnp.mean(x, axis=axis, keepdims=True)
    v = jnp.var(x, axis=axis, keepdims=True)
    return (x - m) / jnp.sqrt(v + eps)

def _scatter_add(tgt, idx, src, axis=0):
    return tgt.at[idx].add(src)

def _segment_sum(src, seg, n):
    return jax.ops.segment_sum(src, seg, n)
kernel_name = 'mk_flamingo_gated_d2_seqx_r4_0aa5ad'

def setup_inputs(seed: int=0):
    np.random.seed(seed)
    _w = jnp.asarray

    def _rec_inputs():
        import jax
        import jax.numpy as jnp
        _rk = jax.random.key(seed)
        x = -0.0002928 + 1 * jax.random.normal(jax.random.fold_in(_rk, 1), (16, 128, 256), jnp.float32)
        _lenS = 128 - jax.random.randint(jax.random.fold_in(_rk, 7), (16,), 0, max(1, 128 // 4) + 1, jnp.int32)
        _lenS2 = 128 - jax.random.randint(jax.random.fold_in(_rk, 8), (16,), 0, max(1, 128 // 4) + 1, jnp.int32)
        _ctx_1024P = jax.random.normal(jax.random.fold_in(_rk, 11), (16, 16, 256), jnp.float32)
        _ctx_1024c = jax.random.dirichlet(jax.random.fold_in(_rk, 511), 0.3 * jnp.ones((16,), jnp.float32), (16, 128))
        _ctx_1024t = jnp.einsum('bsk,bkd->bsd', _ctx_1024c, _ctx_1024P)
        _ctx_1024t = _ctx_1024t * jax.lax.rsqrt(jnp.mean(jnp.square(_ctx_1024t)) + 1e-12) * 0.953939
        ctx_1024 = -1.39393e-06 + 0.999914 * (_ctx_1024t + 0.3 * jax.random.normal(jax.random.fold_in(_rk, 611), (16, 128, 256), jnp.float32))
        _validS = jnp.arange(128)[None, :] < _lenS[:, None]
        _validS2 = jnp.arange(128)[None, :] < _lenS2[:, None]
        _causal = jnp.tril(jnp.ones((128, 128), dtype=bool))
        mask_BxS2_bf0 = jnp.logical_not(jnp.ones((16, 128), dtype=bool))
        mask_BxSxS2_ik0 = jnp.where(jnp.broadcast_to(_validS2[:, None, :], (16, 128, 128)), 0, 1).astype(jnp.int32)
        _g = jax.random.normal(jax.random.fold_in(_rk, 9001), (2, 2), jnp.float32)
        _g = jnp.sign(_g) * jnp.maximum(jnp.abs(_g), 1.0) + (_g == 0) * 1.0
        g_xattn = _g[0]
        g_ffn = _g[1]
        return (x, ctx_1024, mask_BxS2_bf0, mask_BxSxS2_ik0, g_xattn, g_ffn)
    x, ctx_1024, mask_BxS2_bf0, mask_BxSxS2_ik0, g_xattn, g_ffn = _rec_inputs()

    def _L0_xattn_setup():
        import jax, jax.numpy as jnp
        import numpy as np
        HEADS = 16
        key = jax.random.key(seed)
        ks = jax.random.split(key, 9)
        b, s, e = (2, 512, 256)
        w_scale = 1.0 / np.sqrt(e)
        return {'q': jax.random.normal(ks[0], (b, s, e), dtype=jnp.float32), 'k': jax.random.normal(ks[1], (b, s, e), dtype=jnp.float32), 'v': jax.random.normal(ks[2], (b, s, e), dtype=jnp.float32), 'keys_pad_mask': jnp.zeros((b, s), dtype=bool), 'Wq': jax.random.normal(ks[3], (e, e), dtype=jnp.float32) * w_scale, 'bq': jax.random.normal(ks[4], (e,), dtype=jnp.float32) * 0.01, 'Wk': jax.random.normal(ks[5], (e, e), dtype=jnp.float32) * w_scale, 'bk': jax.random.normal(ks[6], (e,), dtype=jnp.float32) * 0.01, 'Wv': jax.random.normal(ks[7], (e, e), dtype=jnp.float32) * w_scale, 'bv': jax.random.normal(ks[8], (e,), dtype=jnp.float32) * 0.01}
    _L0_xattn_all = _L0_xattn_setup()
    _L0_xattn_in = {k: v for k, v in _L0_xattn_all.items() if k in ('Wq', 'bq', 'Wk', 'bk', 'Wv', 'bv')}
    del _L0_xattn_all

    def _L0_ffn_setup():
        import jax, jax.numpy as jnp
        import numpy as np
        import math
        B, S, D = (4, 512, 256)
        E, DFF = (16, 512)
        CAP_FACTOR = 2.0
        ROUTER_HIDDEN = 128
        CAPACITY = int(math.ceil(S * CAP_FACTOR / E))
        key = jax.random.key(seed)
        ks = jax.random.split(key, 6)

        def uinit(k, shape, fan_in):
            bound = math.sqrt(3.0) * math.sqrt(1.0 / 3.0) / math.sqrt(fan_in)
            return jax.random.uniform(k, shape, jnp.float32, -bound, bound)
        return {'hidden_states': jax.random.normal(ks[0], (B, S, D), jnp.float32), 'router_w1': jax.random.normal(ks[1], (D, ROUTER_HIDDEN), jnp.float32) / math.sqrt(D), 'router_w2': jax.random.normal(ks[2], (ROUTER_HIDDEN, E), jnp.float32) / math.sqrt(ROUTER_HIDDEN), 'w1': uinit(ks[3], (E, D, DFF), D), 'w2': uinit(ks[4], (E, D, DFF), D), 'w3': uinit(ks[5], (E, DFF, D), DFF)}
    _L0_ffn_all = _L0_ffn_setup()
    _L0_ffn_in = {k: v for k, v in _L0_ffn_all.items() if k in ('router_w1', 'router_w2', 'w1', 'w2', 'w3')}
    del _L0_ffn_all

    def _L1_xattn_setup():
        import jax, jax.numpy as jnp
        import numpy as np
        D_MODEL = 256
        NUM_HEADS = 16
        D_K = D_MODEL // NUM_HEADS
        BATCH = 2
        SEQ = 512
        key = jax.random.key(seed)
        k = jax.random.split(key, 8)
        query = jax.random.normal(k[0], (BATCH, SEQ, D_MODEL), dtype=jnp.float32)
        key_t = jax.random.normal(k[1], (BATCH, SEQ, D_MODEL), dtype=jnp.float32)
        value = jax.random.normal(k[2], (BATCH, SEQ, D_MODEL), dtype=jnp.float32)
        mask = jnp.broadcast_to(jnp.tril(jnp.ones((SEQ, SEQ), dtype=jnp.int32)), (BATCH, SEQ, SEQ))
        scale = 1.0 / np.sqrt(D_MODEL)
        w_q = jax.random.normal(k[3], (D_MODEL, D_MODEL), dtype=jnp.float32) * scale
        w_k = jax.random.normal(k[4], (D_MODEL, D_MODEL), dtype=jnp.float32) * scale
        w_v = jax.random.normal(k[5], (D_MODEL, D_MODEL), dtype=jnp.float32) * scale
        w_o = jax.random.normal(k[6], (D_MODEL, D_MODEL), dtype=jnp.float32) * scale
        b_o = jnp.zeros((D_MODEL,), dtype=jnp.float32)
        return {'query': query, 'key': key_t, 'value': value, 'mask': mask, 'w_q': w_q, 'w_k': w_k, 'w_v': w_v, 'w_o': w_o, 'b_o': b_o}
    _L1_xattn_all = _L1_xattn_setup()
    _L1_xattn_in = {k: v for k, v in _L1_xattn_all.items() if k in ('w_q', 'w_k', 'w_v', 'w_o', 'b_o')}
    del _L1_xattn_all

    def _L1_ffn_setup():
        import jax, jax.numpy as jnp
        import numpy as np
        H = 256
        E = 32
        TOP_K = 4
        I = 192
        I_SH = 512
        SCALE = 0.02
        key = jax.random.key(seed)
        ks = jax.random.split(key, 9)
        inp = {'hidden_states': jax.random.normal(ks[0], (2, 128, H), dtype=jnp.float32), 'router_w': jax.random.normal(ks[1], (H, E), dtype=jnp.float32) * SCALE, 'w_gate': jax.random.normal(ks[2], (E, H, I), dtype=jnp.float32) * SCALE, 'w_up': jax.random.normal(ks[3], (E, H, I), dtype=jnp.float32) * SCALE, 'w_down': jax.random.normal(ks[4], (E, I, H), dtype=jnp.float32) * SCALE, 'sh_gate': jax.random.normal(ks[5], (H, I_SH), dtype=jnp.float32) * SCALE, 'sh_up': jax.random.normal(ks[6], (H, I_SH), dtype=jnp.float32) * SCALE, 'sh_down': jax.random.normal(ks[7], (I_SH, H), dtype=jnp.float32) * SCALE, 'sh_gate_w': jax.random.normal(ks[8], (H, 1), dtype=jnp.float32) * SCALE}
        return inp
    _L1_ffn_all = _L1_ffn_setup()
    _L1_ffn_in = {k: v for k, v in _L1_ffn_all.items() if k in ('router_w', 'w_gate', 'w_up', 'w_down', 'sh_gate', 'sh_up', 'sh_down', 'sh_gate_w')}
    del _L1_ffn_all
    return {'x': x, 'ctx_1024': ctx_1024, 'mask_BxS2_bf0': mask_BxS2_bf0, 'mask_BxSxS2_ik0': mask_BxSxS2_ik0, 'g_xattn': g_xattn, 'g_ffn': g_ffn, 'L0_xattn_Wq': _L0_xattn_in['Wq'], 'L0_xattn_bq': _L0_xattn_in['bq'], 'L0_xattn_Wk': _L0_xattn_in['Wk'], 'L0_xattn_bk': _L0_xattn_in['bk'], 'L0_xattn_Wv': _L0_xattn_in['Wv'], 'L0_xattn_bv': _L0_xattn_in['bv'], 'L0_ffn_router_w1': _L0_ffn_in['router_w1'], 'L0_ffn_router_w2': _L0_ffn_in['router_w2'], 'L0_ffn_w1': _L0_ffn_in['w1'], 'L0_ffn_w2': _L0_ffn_in['w2'], 'L0_ffn_w3': _L0_ffn_in['w3'], 'L1_xattn_w_q': _L1_xattn_in['w_q'], 'L1_xattn_w_k': _L1_xattn_in['w_k'], 'L1_xattn_w_v': _L1_xattn_in['w_v'], 'L1_xattn_w_o': _L1_xattn_in['w_o'], 'L1_xattn_b_o': _L1_xattn_in['b_o'], 'L1_ffn_router_w': _L1_ffn_in['router_w'], 'L1_ffn_w_gate': _L1_ffn_in['w_gate'], 'L1_ffn_w_up': _L1_ffn_in['w_up'], 'L1_ffn_w_down': _L1_ffn_in['w_down'], 'L1_ffn_sh_gate': _L1_ffn_in['sh_gate'], 'L1_ffn_sh_up': _L1_ffn_in['sh_up'], 'L1_ffn_sh_down': _L1_ffn_in['sh_down'], 'L1_ffn_sh_gate_w': _L1_ffn_in['sh_gate_w']}

def reference(x, ctx_1024, mask_BxS2_bf0, mask_BxSxS2_ik0, g_xattn, g_ffn, L0_xattn_Wq, L0_xattn_bq, L0_xattn_Wk, L0_xattn_bk, L0_xattn_Wv, L0_xattn_bv, L0_ffn_router_w1, L0_ffn_router_w2, L0_ffn_w1, L0_ffn_w2, L0_ffn_w3, L1_xattn_w_q, L1_xattn_w_k, L1_xattn_w_v, L1_xattn_w_o, L1_xattn_b_o, L1_ffn_router_w, L1_ffn_w_gate, L1_ffn_w_up, L1_ffn_w_down, L1_ffn_sh_gate, L1_ffn_sh_up, L1_ffn_sh_down, L1_ffn_sh_gate_w):
    import jax
    import jax.numpy as jnp

    def _L0_xattn_ref(q, k, v, keys_pad_mask, Wq, bq, Wk, bk, Wv, bv):
        import jax, jax.numpy as jnp
        import numpy as np
        HEADS = 16
        b, s_q, e = q.shape
        s_k = k.shape[1]
        h = HEADS
        Q = (q @ Wq.T + bq).reshape(b, h, s_q, -1)
        K = (k @ Wk.T + bk).reshape(b, h, s_k, -1)
        V = (v @ Wv.T + bv).reshape(b, h, s_k, -1)
        scale = jnp.sqrt(jnp.asarray(Q.shape[-1], Q.dtype))
        QK = jnp.einsum('bhqd,bhkd->bhqk', Q, K) * scale
        QK = jnp.where(keys_pad_mask[:, None, None, :], -jnp.inf, QK)
        causal = jnp.triu(jnp.ones((s_q, s_k), dtype=bool), 1)
        QK = jnp.where(causal[None, None], -jnp.inf, QK)
        attn = jax.nn.softmax(QK, axis=-1)
        out = jnp.einsum('bhqk,bhkd->bhqd', attn, V).reshape(b, s_q, -1)
        return out

    def _L0_ffn_ref(hidden_states, router_w1, router_w2, w1, w2, w3):
        import jax, jax.numpy as jnp
        import numpy as np
        import math
        B, S, D = (4, 512, 256)
        E, DFF = (16, 512)
        CAP_FACTOR = 2.0
        ROUTER_HIDDEN = 128
        CAPACITY = int(math.ceil(S * CAP_FACTOR / E))
        b, s, d = hidden_states.shape
        e = w1.shape[0]
        cap = CAPACITY
        router_logits = jax.nn.silu(hidden_states @ router_w1) @ router_w2
        expert_probs = jax.nn.softmax(router_logits.transpose(0, 2, 1), axis=-1)
        expert_weights, token_indices = jax.lax.top_k(expert_probs, cap)
        expert_weights = expert_weights / (expert_weights.sum(-1, keepdims=True) + 1e-09)
        expert_inputs = jax.vmap(lambda h, i: h[i])(hidden_states, token_indices)
        gate = jax.nn.silu(jnp.einsum('becd,edf->becf', expert_inputs, w1))
        value = jnp.einsum('becd,edf->becf', expert_inputs, w2)
        expert_out = jnp.einsum('becf,efd->becd', gate * value, w3)
        weighted = expert_out * expert_weights[..., None]

        def combine(idx, vals):
            return jnp.zeros((s, d), vals.dtype).at[idx.reshape(-1)].add(vals.reshape(-1, d))
        output = jax.vmap(combine)(token_indices, weighted)
        return output

    def _L1_xattn_ref(query, key, value, mask, w_q, w_k, w_v, w_o, b_o):
        import jax, jax.numpy as jnp
        import numpy as np
        D_MODEL = 256
        NUM_HEADS = 16
        D_K = D_MODEL // NUM_HEADS
        BATCH = 2
        SEQ = 512
        b, s, _ = query.shape

        def split_heads(x):
            return x.reshape(b, s, NUM_HEADS, D_K).transpose(0, 2, 1, 3)
        Q = split_heads(query @ w_q.T)
        K = split_heads(key @ w_k.T)
        V = split_heads(value @ w_v.T)
        scores = jnp.einsum('bhqd,bhkd->bhqk', Q, K) / jnp.sqrt(jnp.asarray(D_K, dtype=Q.dtype))
        scores = jnp.where(mask[:, None, :, :] == 0, -1000000000.0, scores)
        attn = jax.nn.softmax(scores, axis=-1)
        out = jnp.einsum('bhqk,bhkd->bhqd', attn, V)
        out = out.transpose(0, 2, 1, 3).reshape(b, s, D_MODEL)
        return out @ w_o.T + b_o

    def _L1_ffn_ref(hidden_states, router_w, w_gate, w_up, w_down, sh_gate, sh_up, sh_down, sh_gate_w):
        import jax, jax.numpy as jnp
        import numpy as np
        H = 256
        E = 32
        TOP_K = 4
        I = 192
        I_SH = 512
        SCALE = 0.02
        orig_shape = hidden_states.shape
        x = hidden_states.reshape(-1, H)
        logits = x @ router_w
        probs = jax.nn.softmax(logits, axis=-1)
        topk_w, topk_idx = jax.lax.top_k(probs, TOP_K)
        topk_w = topk_w / jnp.sum(topk_w, axis=-1, keepdims=True)
        combine = jnp.sum(jax.nn.one_hot(topk_idx, E, dtype=x.dtype) * topk_w[..., None], axis=1)
        g = jnp.einsum('th,ehi->tei', x, w_gate)
        u = jnp.einsum('th,ehi->tei', x, w_up)
        act = jax.nn.silu(g) * u
        eo = jnp.einsum('tei,eih->teh', act, w_down)
        routed = jnp.einsum('te,teh->th', combine, eo)
        sh = jax.nn.silu(x @ sh_gate) * (x @ sh_up) @ sh_down
        sh = sh * jax.nn.sigmoid(x @ sh_gate_w)
        return (routed + sh).reshape(orig_shape)
    x = x + jnp.tanh(g_xattn[0]) * _L0_xattn_ref(_layernorm(x, axis=-1), ctx_1024, ctx_1024, mask_BxS2_bf0, L0_xattn_Wq, L0_xattn_bq, L0_xattn_Wk, L0_xattn_bk, L0_xattn_Wv, L0_xattn_bv)
    x = x + jnp.tanh(g_ffn[0]) * _L0_ffn_ref(_layernorm(x, axis=-1), L0_ffn_router_w1, L0_ffn_router_w2, L0_ffn_w1, L0_ffn_w2, L0_ffn_w3)
    x = x + jnp.tanh(g_xattn[1]) * _L1_xattn_ref(_layernorm(x, axis=-1), ctx_1024, ctx_1024, mask_BxSxS2_ik0, L1_xattn_w_q, L1_xattn_w_k, L1_xattn_w_v, L1_xattn_w_o, L1_xattn_b_o)
    x = x + jnp.tanh(g_ffn[1]) * _L1_ffn_ref(_layernorm(x, axis=-1), L1_ffn_router_w, L1_ffn_w_gate, L1_ffn_w_up, L1_ffn_w_down, L1_ffn_sh_gate, L1_ffn_sh_up, L1_ffn_sh_down, L1_ffn_sh_gate_w)
    return x

_drawn_inputs = setup_inputs


def setup_inputs(seed=0):
    import zlib

    import numpy as np

    out = dict(_drawn_inputs(seed))
    spreads = {'g_ffn': (-1.0, 0.6), 'L1_xattn_b_o': (0.0, 0.1)}
    factors = {'L0_xattn_bq': 3.038,
     'L0_xattn_bk': 3.122,
     'L0_xattn_bv': 8.0,
     'L0_ffn_router_w1': 8.0,
     'L0_ffn_router_w2': 8.0,
     'L0_ffn_w1': 8.0,
     'L0_ffn_w2': 8.0,
     'L0_ffn_w3': 8.0,
     'L1_ffn_router_w': 8.0,
     'L1_ffn_w_gate': 8.0,
     'L1_ffn_w_up': 8.0,
     'L1_ffn_w_down': 8.0,
     'L1_ffn_sh_gate': 8.0,
     'L1_ffn_sh_up': 7.869,
     'L1_ffn_sh_down': 7.914,
     'L1_ffn_sh_gate_w': 8.0}
    for name, (base, spread) in spreads.items():
        noise = np.random.default_rng([zlib.crc32(name.encode()), seed]).standard_normal(out[name].shape)
        drawn = base * np.exp(spread * noise) if base else spread * noise
        out[name] = jnp.asarray(drawn.astype(out[name].dtype))
    for name, factor in factors.items():
        out[name] = (out[name] * factor).astype(out[name].dtype)
    return out
```

```python
import concourse.bass as bass
from concourse import mybir
from contextlib import ExitStack

ACT = mybir.ActivationFunctionType
ALU = mybir.AluOpType
AX_X = mybir.AxisListType.X
F32 = mybir.dt.float32
BF16 = mybir.dt.bfloat16
I32 = mybir.dt.int32
U8 = mybir.dt.uint8

B, S, D = 16, 128, 256
H, DH = 16, 16
KD = D // 128
STRIPS = 4
HS = H // STRIPS
EPS = 1e-5
MASKED = -2.0 ** 120


class Chain:

    def __init__(self, eng, sem, base=0):
        self.eng, self.sem, self.n, self.base = eng, sem, 0, base

    def link(self, ins):
        self.n += 1
        ins.then_inc(self.sem, 1)
        self.eng.wait_ge(self.sem, self.base + self.n)


class Resident:

    def __init__(self, nc, ctx):
        def sb(name, shape, dt=F32):
            return ctx.enter_context(nc.sbuf_tensor(name, shape, dt))

        self.X = sb("X", [128, B, D])
        self.XN = sb("XN", [128, B, D])
        self.ident = sb("ident", [128, 128])
        self.ident_bf = sb("ident_bf", [128, 128], BF16)
        self.gates = sb("gates", [128, 4])
        self.stats = sb("stats", [128, B, 6])
        self.mv = sb("mv", [128, B, 2])
        self.var = sb("var", [128, B])
        self.std = sb("std", [128, B])
        self.rstd = sb("rstd", [128, B])
        self.banks = [ctx.enter_context(nc.psum_tensor(f"bank{i}", [128, 512], F32)) for i in range(8)]


def load_phase(nc, r, a):
    with ExitStack() as ctx:
        s_x, s_g, s_zero, s_ident, s_gates = (ctx.enter_context(nc.semaphore(n)) for n in (
            "x_loaded", "g_loaded", "ident_zeroed", "ident_made", "gates_made"))
        block = ctx.enter_context(nc.Block())

        @block.sync
        def _(sp):
            sp.dma_start(r.X[:, :, :], a["x"].rearrange("b s d -> s b d")).then_inc(s_x, 16)
            sp.dma_start(r.gates[:, 0:2], a["g_xattn"].partition_broadcast(128)).then_inc(s_g, 16)
            sp.dma_start(r.gates[:, 2:4], a["g_ffn"].partition_broadcast(128)).then_inc(s_g, 16)
            sp.wait_ge(s_x, 16)

        @block.gpsimd
        def _(pool):
            nc.gpsimd.memset(r.ident[:, :], 0.0).then_inc(s_zero, 1)
            nc.gpsimd.memset(r.ident_bf[:, :], 0.0).then_inc(s_zero, 1)
            pool.wait_ge(s_zero, 2)
            for t in (r.ident, r.ident_bf):
                nc.gpsimd.affine_select(out=t[:, :], in_=t[:, :], compare_op=ALU.not_equal, fill=1.0, base=0,
                                        pattern=[[-1, 128]], channel_multiplier=1).then_inc(s_ident, 1)
            pool.wait_ge(s_ident, 2)

        @block.scalar
        def _(act):
            act.wait_ge(s_g, 32)
            nc.scalar.activation(r.gates[:, :], r.gates[:, :], ACT.Tanh).then_inc(s_gates, 1)
            act.wait_ge(s_gates, 1)


def stats_phase(nc, r, name, added=None, gate=None, clear=None):
    with ExitStack() as ctx:
        s_chain, s_var, s_std = (ctx.enter_context(nc.semaphore(f"{name}_{n}")) for n in
                                 ("dve_chain", "var_ready", "std_ready"))
        block = ctx.enter_context(nc.Block())

        @block.vector
        def _(dve):
            ch = Chain(dve, s_chain)
            if added is not None:
                for b in range(B):
                    last = nc.vector.scalar_tensor_tensor(out=r.X[:, b, :], in0=added[:, b, :], scalar=gate,
                                                          in1=r.X[:, b, :], op0=ALU.mult, op1=ALU.add)
                ch.link(last)
            for b in range(B):
                last = nc.vector.bn_stats(r.stats[:, b, :], r.X[:, b, :])
            ch.link(last)
            for b in range(B):
                last = nc.vector.bn_aggr(r.mv[:, b, :], r.stats[:, b, :])
            ch.link(last)
            nc.vector.tensor_scalar(r.var[:, :], r.mv[:, :, 1], EPS, None, ALU.add).then_inc(s_var, 1)
            dve.wait_ge(s_std, 1)
            ch.link(nc.vector.reciprocal(r.rstd[:, :], r.std[:, :]))

        @block.scalar
        def _(act):
            act.wait_ge(s_var, 1)
            nc.scalar.activation(r.std[:, :], r.var[:, :], ACT.Sqrt).then_inc(s_std, 1)

        if clear is not None:
            @block.sync
            def _(sp):
                sp.sem_clear(range(min(clear.numbers), max(clear.numbers) + 1))


class AttentionSignals:

    def __init__(self, nc, ctx):
        self.numbers = []

        def sem(name):
            s = ctx.enter_context(nc.semaphore("attn_" + name))
            self.numbers.append(s.num)
            return s

        def pair(name):
            return [sem(name + "0"), sem(name + "1")]

        self.w_in = sem("w_in")
        self.w_made = sem("w_made")
        self.causal_made = sem("causal_made")
        self.zeroed = sem("zeroed")
        self.mask_sb = sem("mask_sb")
        self.xb_sb = sem("xb_sb")
        self.xt_ps = sem("xt_ps")
        self.xt_sb = sem("xt_sb")
        self.q_ps = sem("q_ps")
        self.kv_ps = sem("kv_ps")
        self.q_sb = sem("q_sb")
        self.qk_sb = sem("qk_sb")
        self.v_sb = sem("v_sb")
        self.s_ps = sem("s_ps")
        self.max_sb = sem("max_sb")
        self.p_sb = sem("p_sb")
        self.pt_ps = sem("pt_ps")
        self.pt_sb = sem("pt_sb")
        self.pv_ps = sem("pv_ps")
        self.o_sb = sem("o_sb")
        self.o_in = sem("o_in")
        self.k_ps = sem("k_ps")
        self.ot_ps = sem("ot_ps")
        self.ot_sb = sem("ot_sb")
        self.y_ps = sem("y_ps")
        self.y_sb = sem("y_sb")
        self.chain = sem("chain")
        self.sp_held = sem("sp_held")
        self.v_out = pair("v_out")
        self.v_in = pair("v_in")
        self.o_out = pair("o_out")


def attention_phase(nc, r, a, layer, signals):
    pre = f"a{layer}_"
    S_BANKS, PT_BANKS, KV, QO = r.banks[0:4], r.banks[4:6], r.banks[6], r.banks[7]
    NJ = STRIPS
    AHEAD = 5
    FIRST, FIRST_DMA = 1, 16

    def head(j, g):
        return HS * j + g if layer == 0 else STRIPS * g + j

    with ExitStack() as ctx:
        def sb(name, shape, dt=F32):
            return ctx.enter_context(nc.sbuf_tensor(pre + name, shape, dt))

        xb = [sb(f"xb{u}", [128, D]) for u in range(2)]
        xT = [sb(f"xT{u}", [128, KD, S]) for u in range(2)]
        cT = [sb(f"cT{u}", [128, KD, S]) for u in range(2)]
        qT = [sb(f"qT{u}", [128, HS, S]) for u in range(2)]
        kT = [sb(f"kT{u}", [128, HS, S]) for u in range(2)]
        vtok = [sb(f"vtok{u}", [128, H, DH]) for u in range(2)]
        mask = [sb(f"mask{u}", [128, S], BF16) for u in range(2)]
        negmax = [sb(f"negmax{u}", [128, NJ, HS]) for u in range(2)]
        rowsum = [sb(f"rowsum{u}", [128, H]) for u in range(2)]
        rinv = [sb(f"rinv{u}", [128, H]) for u in range(2)]
        osb = [sb(f"osb{u}", [128, H, DH]) for u in range(2)]
        P = sb("P", [128, NJ, HS, S])
        pT = [sb(f"pT{u}", [128, HS, S]) for u in range(2)]
        if layer == 0:
            padmask = [sb(f"padmask{u}", [128, S], U8) for u in range(2)]
            causal = sb("causal", [128, S])
            qpad = sb("qpad", [128, H, 2 * DH])
            kpad = sb("kpad", [128, H, 2 * DH])
            vs = [sb(f"vs{u}", [128, H, DH]) for u in range(2)]
            wq = sb("wq", [128, KD, D])
            wkv = sb("wkv", [128, KD, 2 * D])
            bq4 = sb("bq4", [128, D])
            bkv = sb("bkv", [128, 2 * D])
            poison = [sb(f"poison{u}", [128, H]) for u in range(2)]
            v_dram = nc.dram_tensor(pre + "v_dram", (B * S * D,), F32, kind="Internal").ap()
            o_dram = nc.dram_tensor(pre + "o_dram", (B * S * D,), F32, kind="Internal").ap()
        else:
            imask = [sb(f"imask{u}", [128, S], I32) for u in range(2)]
            wdense = sb("wdense", [128, KD, 2 * D])
            wqp = sb("wqp", [128, KD, H, 2 * DH])
            wkp = sb("wkp", [128, KD, H, 2 * DH])
            wv = sb("wv", [128, KD, D])
            wo = sb("wo", [128, KD, D])
            bo = sb("bo", [128, D])
            oT = [sb(f"oT{u}", [128, KD, S]) for u in range(2)]
            proj = [sb(f"proj{u}", [128, D]) for u in range(2)]
            vs = vtok

        q = signals
        mask_in, ctx_in = ([ctx.enter_context(nc.semaphore(f"{pre}{n}{u}")) for u in range(2)] for n in ("mask_in", "ctx_in"))
        block = ctx.enter_context(nc.Block())

        @block.sync
        def _(sp):
            def hold(sp, sem, value):
                sp.wait_ge(sem, value)
                sp.sem_inc(q.sp_held, 1)

            def weights(dst, name):
                sp.dma_start(dst, a[name].rearrange("(k p) n -> p k n", p=128)).then_inc(q.w_in, 16)

            if layer == 0:
                weights(wq[:, :, :], "L0_wq_t")
                weights(wkv[:, :, 0:D], "L0_wk_t")
                weights(wkv[:, :, D:2 * D], "L0_wv_t")
                sp.dma_start(bq4[:, :], a["L0_xattn_bq"].partition_broadcast(128)).then_inc(q.w_in, 16)
                sp.dma_start(bkv[:, 0:D], a["L0_xattn_bk"].partition_broadcast(128)).then_inc(q.w_in, 16)
                sp.dma_start(bkv[:, D:2 * D], a["L0_xattn_bv"].partition_broadcast(128)).then_inc(q.w_in, 16)
                with sp.Fori(0, B // 2) as i:
                    for u in range(2):
                        b = i * 2 + u
                        vd = v_dram[bass.ds(sp.snap(b * (S * D)), S * D)]
                        hold(sp, q.v_sb, b + 1)
                        sp.dma_start(vd.rearrange("(s d) -> s d", d=D), vtok[u][:, :, :].rearrange("p h e -> p (h e)")
                                     ).then_inc(q.v_out[u], 16)
                        hold(sp, q.v_out[u], i * 16 + 16 + FIRST_DMA)
                        hold(sp, q.pv_ps, (b - 1) * NJ + AHEAD)
                        sp.dma_start(vs[u][:, :, :], vd.rearrange("(h p e) -> p h e", h=H, e=DH)).then_inc(q.v_in[u], 16)
                    for u in range(2):
                        b = i * 2 + u
                        od = o_dram[bass.ds(sp.snap(b * (S * D)), S * D)]
                        hold(sp, q.o_sb, b + 1 + FIRST)
                        sp.dma_start(od.rearrange("(h p e) -> p h e", h=H, e=DH), osb[u][:, :, :]).then_inc(q.o_out[u], 16)
                for u in range(2):
                    sp.wait_ge(q.o_out[u], 16 * B // 2 + FIRST_DMA)
                sp.dma_start(r.XN[:, :, :], o_dram.rearrange("(b s d) -> s b d", b=B, s=S)).then_inc(q.o_in, 16)
                sp.wait_ge(q.o_in, 16)
            else:
                weights(wdense[:, :, 0:D], "L1_wq_t")
                weights(wdense[:, :, D:2 * D], "L1_wk_t")
                weights(wv[:, :, :], "L1_wv_t")
                weights(wo[:, :, :], "L1_wo_t")
                sp.dma_start(bo[:, :], a["L1_xattn_b_o"].partition_broadcast(128)).then_inc(q.w_in, 16)

        @block.gpsimd
        def _(pool):
            if layer == 0:
                for t in (causal[:, :], qpad[:, :, :], kpad[:, :, :]):
                    nc.gpsimd.memset(t, 0.0).then_inc(q.zeroed, 1)
                pool.wait_ge(q.zeroed, 3)
                nc.gpsimd.affine_select(out=causal[:, :], in_=causal[:, :], compare_op=ALU.is_ge, fill=MASKED, base=0,
                                        pattern=[[-1, S]], channel_multiplier=1).then_inc(q.causal_made, 1)
            else:
                for t in (wqp, wkp):
                    nc.gpsimd.memset(t[:, :, :, :], 0.0).then_inc(q.zeroed, 1)
                pool.wait_ge(q.zeroed, 2)
                pool.wait_ge(q.w_in, 16 * 5)
                for n, t in enumerate((wqp, wkp)):
                    for k in range(KD):
                        src = wdense[:, k, n * D:(n + 1) * D].rearrange("p (h e) -> p h e", h=H)
                        nc.gpsimd.tensor_copy(t[:, k, :, 0:DH], src).then_inc(q.w_made, 1)
            with pool.Fori(0, B // 2) as i:
                for u in range(2):
                    b = i * 2 + u
                    pool.wait_ge(q.mask_sb, b + FIRST)
                    pool.wait_ge(q.kv_ps, b + FIRST)
                    if layer == 0:
                        src = a["mask_pad"][bass.ds(b, 1), :].rearrange("o s -> (o s)").partition_broadcast(128)
                        pool.dma_start(padmask[u][:, :], src).then_inc(mask_in[u], 16)
                    else:
                        src = a["mask_BxSxS2_ik0"][bass.ds(b, 1), :, :].rearrange("o q k -> (o q) k")
                        pool.dma_start(imask[u][:, :], src).then_inc(mask_in[u], 16)
                    src = a["ctx_t"][bass.ds(b, 1), :, :].rearrange("o (k p) s -> p (o k) s", p=128)
                    pool.dma_start(cT[u][:, :, :], src).then_inc(ctx_in[u], 16)

        @block.tensor
        def _(pe):
            pe.wait_ge(q.w_in, 16 * (6 if layer == 0 else 5))
            if layer == 1:
                pe.wait_ge(q.w_made, 2 * KD)

            def project(i, u):
                b = i * 2 + u
                pe.wait_ge(q.o_sb, i * 2 + FIRST)
                pe.wait_ge(q.qk_sb, b + FIRST)
                pe.wait_ge(q.xb_sb, b + 1)
                for k in range(KD):
                    last = nc.tensor.transpose(QO[:, k * S:(k + 1) * S], xb[u][:, k * 128:(k + 1) * 128], r.ident[:, :])
                last.then_inc(q.xt_ps, 1)
                pe.wait_ge(ctx_in[u], i * 16 + 16)
                if layer == 0:
                    for k in range(KD):
                        last = nc.tensor.matmul(KV[:, :], cT[u][:, k, :], wkv[:, k, :], start=k == 0, stop=k == KD - 1)
                    last.then_inc(q.kv_ps, 1)
                    pe.wait_ge(q.xt_sb, b + 1)
                    for k in range(KD):
                        last = nc.tensor.matmul(QO[:, D:2 * D], xT[u][:, k, :], wq[:, k, :], start=k == 0, stop=k == KD - 1)
                    last.then_inc(q.q_ps, 1)
                else:
                    pe.wait_ge(q.y_sb, i * 2 + FIRST)
                    pe.wait_ge(q.xt_sb, b + 1)
                    for k in range(KD):
                        last = nc.tensor.matmul(QO[:, D:2 * D], cT[u][:, k, :], wv[:, k, :], start=k == 0, stop=k == KD - 1)
                    last.then_inc(q.kv_ps, 1)
                    for g in range(HS):
                        for k in range(KD):
                            w = wqp[:, k, STRIPS * g:STRIPS * g + STRIPS, :].rearrange("p h e -> p (h e)")
                            last = nc.tensor.matmul(KV[:, g * S:(g + 1) * S], w, xT[u][:, k, :],
                                                    start=k == 0, stop=k == KD - 1)
                    last.then_inc(q.q_ps, 1)
                    pe.wait_ge(q.q_sb, b + 1)
                    for g in range(HS):
                        for k in range(KD):
                            w = wkp[:, k, STRIPS * g:STRIPS * g + STRIPS, :].rearrange("p h e -> p (h e)")
                            last = nc.tensor.matmul(KV[:, g * S:(g + 1) * S], w, cT[u][:, k, :],
                                                    start=k == 0, stop=k == KD - 1)
                    last.then_inc(q.k_ps, 1)

            def scores(i, u):
                b = i * 2 + u
                pe.wait_ge(q.mask_sb, b + 1 + FIRST)
                pe.wait_ge(q.p_sb, b * NJ + FIRST)
                for j in range(NJ):
                    m = mask[u][:, :].rearrange("p (o s) -> p o s", o=1).broadcast_to((128, HS, S))
                    nc.tensor.matmul(S_BANKS[j][:, :], r.ident_bf[:, :], m, start=True, stop=False)
                pe.wait_ge(q.qk_sb, b + 1 + FIRST)
                for g in range(HS):
                    for j in range(NJ):
                        rows = slice(32 * j, 32 * j + DH)
                        last = nc.tensor.matmul(S_BANKS[j][:, g * S:(g + 1) * S], qT[u][rows, g, :], kT[u][rows, g, :],
                                                start=False, stop=g == HS - 1)
                        if g == HS - 1:
                            last.then_inc(q.s_ps, 1)

            def attend(i, u):
                b = i * 2 + u

                def transpose_p(j):
                    n = b * NJ + j
                    pe.wait_ge(q.p_sb, n + 1 + FIRST)
                    pe.wait_ge(q.pt_sb, n - 1 + AHEAD)
                    for g in range(HS):
                        last = nc.tensor.transpose(PT_BANKS[j % 2][:, g * S:(g + 1) * S], P[:, j, g, :], r.ident[:, :])
                    last.then_inc(q.pt_ps, 1)

                def values(j):
                    n = b * NJ + j
                    pe.wait_ge(q.pt_sb, n + 1 + AHEAD)
                    for g in range(HS):
                        h = head(j, g)
                        last = nc.tensor.matmul(QO[:, h * DH:(h + 1) * DH], pT[j % 2][:, g, :], vs[u][:, h, :],
                                                start=True, stop=True)
                    last.then_inc(q.pv_ps, 1)

                transpose_p(0)
                if layer == 0:
                    pe.wait_ge(q.v_in[u], i * 16 + 16)
                pe.wait_ge(q.o_sb, b + FIRST)
                pe.wait_ge(q.qk_sb, i * 2 + 2 + FIRST)
                for j in range(1, NJ):
                    transpose_p(j)
                    values(j - 1)
                values(NJ - 1)

            def project_out(i, u):
                b = i * 2 + u
                pe.wait_ge(q.o_sb, b + 1 + FIRST)
                pe.wait_ge(q.y_sb, b + FIRST)
                for k in range(KD):
                    last = nc.tensor.transpose(KV[:, k * S:(k + 1) * S],
                                               osb[u][:, :, :].rearrange("p h e -> p (h e)")[:, k * 128:(k + 1) * 128],
                                               r.ident[:, :])
                last.then_inc(q.ot_ps, 1)
                pe.wait_ge(q.ot_sb, b + 1)
                for k in range(KD):
                    last = nc.tensor.matmul(KV[:, D:2 * D], oT[u][:, k, :], wo[:, k, :], start=k == 0, stop=k == KD - 1)
                last.then_inc(q.y_ps, 1)

            with pe.Fori(0, B // 2) as i:
                project(i, 0)
                scores(i, 0)
                project(i, 1)
                attend(i, 0)
                scores(i, 1)
                if layer == 1:
                    project_out(i, 0)
                attend(i, 1)
                if layer == 1:
                    project_out(i, 1)

        @block.scalar
        def _(act):
            for s in (q.pt_ps, q.pt_sb, q.pv_ps):
                act.sem_inc(s, AHEAD)
            for s in (q.mask_sb, q.kv_ps, q.o_sb, q.qk_sb, q.y_sb, q.p_sb):
                act.sem_inc(s, FIRST)
            for s in (*q.v_out, *q.o_out):
                act.sem_inc(s, FIRST_DMA)
            with act.Fori(0, B // 2) as i:
                for u in range(2):
                    b = i * 2 + u
                    for j in range(NJ):
                        n = b * NJ + j
                        act.wait_ge(q.max_sb, n + 1)
                        act.wait_ge(q.pt_ps, n - NJ + 1 + AHEAD)
                        for g in range(HS):
                            h = head(j, g)
                            last = nc.scalar.activation(P[:, j, g, :], S_BANKS[j][:, g * S:(g + 1) * S], ACT.Exp,
                                                        bias=negmax[u][:, j, g:g + 1],
                                                        accum_out=rowsum[u][:, h:h + 1])
                        last.then_inc(q.p_sb, 1)
                    for j in range(NJ):
                        n = b * NJ + j
                        act.wait_ge(q.pt_ps, n + 1 + AHEAD)
                        act.wait_ge(q.pv_ps, n - 1 + AHEAD)
                        nc.scalar.copy(pT[j % 2][:, :, :].rearrange("p g s -> p (g s)"), PT_BANKS[j % 2][:, :]
                                       ).then_inc(q.pt_sb, 1)

        PER_TURN = 4 if layer == 0 else 4

        @block.vector
        def _(dve):
            setup = 0
            if layer == 0:
                dve.wait_ge(q.w_in, 16 * 6)
                dve.wait_ge(q.causal_made, 1)
                ch = Chain(dve, q.chain)
                ch.link(nc.vector.tensor_scalar(bq4[:, :], bq4[:, :], 4.0, None, ALU.mult))
                setup = ch.n
            else:
                dve.wait_ge(q.w_in, 16 * 5)

            def prepare(i, u, ch):
                b = i * 2 + u
                dve.wait_ge(mask_in[u], i * 16 + 16)
                if layer == 0:
                    nc.vector.scalar_tensor_tensor(out=mask[u][:, :], in0=padmask[u][:, :], scalar=MASKED,
                                                   in1=causal[:, :], op0=ALU.mult, op1=ALU.add).then_inc(q.mask_sb, 1)
                else:
                    nc.vector.tensor_scalar(mask[u][:, :], imask[u][:, :], 0.0, MASKED, ALU.is_equal, ALU.mult
                                            ).then_inc(q.mask_sb, 1)
                nc.vector.tensor_scalar(xb[u][:, :], r.X[:, bass.ds(b, 1), :].rearrange("p o d -> p (o d)"),
                                        r.mv[:, bass.ds(b, 1), 0:1].rearrange("p o s -> p (o s)"),
                                        r.rstd[:, bass.ds(b, 1)], ALU.subtract, ALU.mult).then_inc(q.xb_sb, 1)
                dve.wait_ge(q.xt_ps, b + 1)
                nc.vector.tensor_copy(xT[u][:, :, :].rearrange("p k s -> p (k s)"), QO[:, 0:D]).then_inc(q.xt_sb, 1)
                if layer == 0:
                    dve.wait_ge(q.kv_ps, b + 1 + FIRST)
                    dve.wait_ge(q.v_out[u], i * 16 + FIRST_DMA)
                    nc.vector.tensor_tensor(vtok[u][:, :, :].rearrange("p h e -> p (h e)"), KV[:, D:2 * D],
                                            bkv[:, D:2 * D], ALU.add).then_inc(q.v_sb, 1)
                    ch.link(nc.vector.tensor_tensor(kpad[:, :, 0:DH], KV[:, 0:D].rearrange("p (c e) -> p c e", e=DH),
                                                    bkv[:, 0:D].rearrange("p (c e) -> p c e", e=DH), ALU.add))
                    nc.vector.transpose(kT[u][:, :, :].rearrange("p g s -> p (g s)").rearrange("p (s c) -> p c s", c=H),
                                        kpad[:, :, :])
                    dve.wait_ge(q.q_ps, b + 1)
                    ch.link(nc.vector.scalar_tensor_tensor(out=qpad[:, :, 0:DH],
                                                           in0=QO[:, D:2 * D].rearrange("p (c e) -> p c e", e=DH),
                                                           scalar=4.0, in1=bq4[:, :].rearrange("p (c e) -> p c e", e=DH),
                                                           op0=ALU.mult, op1=ALU.add))
                    nc.vector.transpose(qT[u][:, :, :].rearrange("p g s -> p (g s)").rearrange("p (s c) -> p c s", c=H),
                                        qpad[:, :, :]).then_inc(q.qk_sb, 1)
                else:
                    dve.wait_ge(q.kv_ps, b + 1 + FIRST)
                    nc.vector.tensor_copy(vtok[u][:, :, :].rearrange("p h e -> p (h e)"), QO[:, D:2 * D])
                    dve.wait_ge(q.q_ps, b + 1)
                    nc.vector.tensor_scalar(qT[u][:, :, :].rearrange("p g s -> p (g s)"), KV[:, :], 0.25, None, ALU.mult
                                            ).then_inc(q.q_sb, 1)
                    dve.wait_ge(q.k_ps, b + 1)
                    nc.vector.tensor_copy(kT[u][:, :, :].rearrange("p g s -> p (g s)"), KV[:, :]).then_inc(q.qk_sb, 1)

            def maxima(i, u, ch):
                b = i * 2 + u
                for j in range(NJ):
                    dve.wait_ge(q.s_ps, b * NJ + j + 1)
                    nc.vector.tensor_reduce(negmax[u][:, j, :], S_BANKS[j][:, :].rearrange("p (g s) -> p g s", g=HS),
                                            AX_X, ALU.max, negate=True).then_inc(q.max_sb, 1)

            def output(i, u, ch):
                b = i * 2 + u
                dve.wait_ge(q.pv_ps, b * NJ + NJ + AHEAD)
                ch.link(nc.vector.reciprocal(rinv[u][:, :], rowsum[u][:, :]))
                if layer == 0:
                    dve.wait_ge(q.o_out[u], i * 16 + FIRST_DMA)
                nc.vector.tensor_tensor(osb[u][:, :, :], QO[:, 0:D].rearrange("p (h e) -> p h e", h=H),
                                        rinv[u][:, :].rearrange("p (h o) -> p h o", o=1).broadcast_to((128, H, DH)),
                                        ALU.mult).then_inc(q.o_sb, 1)

            def take_out(i, u, ch):
                b = i * 2 + u
                dve.wait_ge(q.ot_ps, b + 1)
                nc.vector.tensor_copy(oT[u][:, :, :].rearrange("p k s -> p (k s)"), KV[:, 0:D]).then_inc(q.ot_sb, 1)
                dve.wait_ge(q.y_ps, b + 1)
                nc.vector.tensor_tensor(proj[u][:, :], KV[:, D:2 * D], bo[:, :], ALU.add).then_inc(q.y_sb, 1)
                dve.wait_ge(q.y_sb, b + 1 + FIRST)
                xrow = r.X[:, bass.ds(b, 1), :].rearrange("p o d -> p (o d)")
                nc.vector.scalar_tensor_tensor(out=xrow, in0=proj[u][:, :], scalar=r.gates[:, 1:2], in1=xrow,
                                               op0=ALU.mult, op1=ALU.add)

            per_turn = 6 if layer == 0 else 2
            with dve.Fori(0, B // 2) as i:
                ch = Chain(dve, q.chain, i * per_turn + setup)
                prepare(i, 0, ch)
                maxima(i, 0, ch)
                prepare(i, 1, ch)
                output(i, 0, ch)
                maxima(i, 1, ch)
                if layer == 1:
                    take_out(i, 0, ch)
                output(i, 1, ch)
                if layer == 1:
                    take_out(i, 1, ch)
                assert ch.n == per_turn
            if layer == 0:
                dve.wait_ge(q.o_sb, B + FIRST)


E0, F0, CAP, RH = 16, 512, 64, 128
KF0 = F0 // 128
TIE = 2.0 ** -100


def router0_phase(nc, r, a, R, W):
    NB, NT = 4, B // 4
    with ExitStack() as ctx:
        def sb(name, shape, dt=F32):
            return ctx.enter_context(nc.sbuf_tensor("r0_" + name, shape, dt))

        def sem(name):
            return ctx.enter_context(nc.semaphore("r0_" + name))

        w1 = sb("w1", [128, KD, RH])
        w2 = sb("w2", [RH, E0])
        tie = sb("tie", [128, S])
        ones = sb("ones", [128, 128])
        xb = sb("xb", [128, NB, D])
        xT = sb("xT", [128, KD, NB * S])
        hid = sb("hid", [RH, NB * S])
        negmax = sb("negmax", [E0, NB])
        ex = sb("ex", [E0, NB, S])
        sums = sb("sums", [E0, NB])
        rs = sb("rs", [E0, NB])
        probs = sb("probs", [E0, NB, S])
        row = sb("row", [128, E0, NB * S])
        col = sb("col", [128, NB, E0])
        taken = sb("taken", [128, NB, E0])
        total = sb("total", [128, NB, E0])
        inv = sb("inv", [128, NB, E0])
        p_dram = nc.dram_tensor("r0_p_dram", (NT * E0 * NB * S,), F32, kind="Internal").ap()
        (w_in, consts, xb_sb, xt_ps, xt_sb, h_ps, h_sb, l_ps, max_sb, ex_sb, probs_sb, p_out, row_in, col_ps, taken_sb,
         total_ps, pe_held, chain, held) = (sem(n) for n in (
             "w_in", "consts", "xb_sb", "xt_ps", "xt_sb", "h_ps", "h_sb", "l_ps", "max_sb", "ex_sb", "probs_sb",
             "p_out", "row_in", "col_ps", "taken_sb", "total_ps", "pe_held", "dve_chain", "held"))
        banks = r.banks
        block = ctx.enter_context(nc.Block())

        @block.sync
        def _(sp):
            sp.dma_start(w1[:, :, :], a["L0_ffn_router_w1"].rearrange("(k p) n -> p k n", p=128)).then_inc(w_in, 16)
            sp.dma_start(w2[:, :], a["L0_ffn_router_w2"]).then_inc(w_in, 16)
            with sp.Fori(0, NT) as i:
                sp.wait_ge(probs_sb, i + 1)
                sp.sem_inc(held, 1)
                pd = p_dram[bass.ds(i * (E0 * NB * S), E0 * NB * S)]
                sp.dma_start(pd.rearrange("(e n) -> e n", e=E0), probs[:, :, :].rearrange("e b s -> e (b s)")
                             ).then_inc(p_out, 16)
                sp.wait_ge(p_out, i * 16 + 16)
                sp.sem_inc(held, 1)
                sp.dma_start(row[:, :, :].rearrange("p e n -> p (e n)"), pd.partition_broadcast(128)).then_inc(row_in, 16)

        @block.gpsimd
        def _(pool):
            nc.gpsimd.memset(tie[:, :], -TIE).then_inc(consts, 1)
            nc.gpsimd.memset(ones[:, :], 1.0).then_inc(consts, 1)
            nc.gpsimd.memset(R[:, :, :], 0.0).then_inc(consts, 1)
            nc.gpsimd.memset(W[:, :, :], 0.0).then_inc(consts, 1)
            pool.wait_ge(consts, 4)
            nc.gpsimd.affine_select(out=tie[:, :], in_=tie[:, :], compare_op=ALU.is_gt, fill=0.0, base=0,
                                    pattern=[[-1, S]], channel_multiplier=1).then_inc(consts, 1)

        @block.tensor
        def _(pe):
            pe.wait_ge(w_in, 32)
            pe.wait_ge(consts, 5)
            with pe.Fori(0, NT) as i:
                pe.wait_ge(xb_sb, i + 1)
                for k in range(KD):
                    for n in range(NB):
                        last = nc.tensor.transpose(banks[k][:, n * S:(n + 1) * S], xb[:, n, k * 128:(k + 1) * 128],
                                                   r.ident[:, :])
                last.then_inc(xt_ps, 1)
                pe.wait_ge(xt_sb, i + 1)
                for k in range(KD):
                    last = nc.tensor.matmul(banks[2][:, :], w1[:, k, :], xT[:, k, :], start=k == 0, stop=k == KD - 1)
                last.then_inc(h_ps, 1)
                pe.wait_ge(h_sb, i + 1)
                nc.tensor.matmul(banks[3][0:E0, :], w2[:, :], hid[:, :], start=True, stop=True).then_inc(l_ps, 1)
                pe.wait_ge(probs_sb, i + 1)
                pe.sem_inc(pe_held, 1)
                for n in range(NB):
                    last = nc.tensor.transpose(banks[4][:, n * E0:(n + 1) * E0], probs[:, n, :], r.ident[0:E0, 0:E0])
                last.then_inc(col_ps, 1)
                pe.wait_ge(taken_sb, i + 1)
                nc.tensor.matmul(banks[5][:, 0:NB * E0], ones[:, :], taken[:, :, :].rearrange("p b e -> p (b e)"),
                                 start=True, stop=True).then_inc(total_ps, 1)

        @block.scalar
        def _(act):
            with act.Fori(0, NT) as i:
                act.wait_ge(h_ps, i + 1)
                nc.scalar.activation(hid[:, :], banks[2][:, :], ACT.Silu).then_inc(h_sb, 1)
                act.wait_ge(max_sb, i + 1)
                for n in range(NB):
                    last = nc.scalar.activation(ex[:, n, :], banks[3][0:E0, n * S:(n + 1) * S], ACT.Exp,
                                                bias=negmax[:, n:n + 1], accum_out=sums[:, n:n + 1])
                last.then_inc(ex_sb, 1)

        PER_TURN = 5

        @block.vector
        def _(dve):
            dve.wait_ge(consts, 5)
            with dve.Fori(0, NT) as i:
                ch = Chain(dve, chain, i * PER_TURN)
                for n in range(NB):
                    b = i * NB + n
                    last = nc.vector.tensor_scalar(xb[:, n, :], r.X[:, bass.ds(b, 1), :].rearrange("p o d -> p (o d)"),
                                                   r.mv[:, bass.ds(b, 1), 0:1].rearrange("p o s -> p (o s)"),
                                                   r.rstd[:, bass.ds(b, 1)], ALU.subtract, ALU.mult)
                last.then_inc(xb_sb, 1)
                dve.wait_ge(xt_ps, i + 1)
                for k in range(KD):
                    last = nc.vector.tensor_copy(xT[:, k, :], banks[k][:, :])
                last.then_inc(xt_sb, 1)
                nc.vector.tensor_copy(r.XN[:, bass.ds(i * NB, NB), :], xb[:, :, :])
                dve.wait_ge(l_ps, i + 1)
                nc.vector.tensor_reduce(negmax[:, :], banks[3][0:E0, :].rearrange("e (b s) -> e b s", b=NB), AX_X,
                                        ALU.max, negate=True).then_inc(max_sb, 1)
                dve.wait_ge(ex_sb, i + 1)
                ch.link(nc.vector.reciprocal(rs[:, :], sums[:, :]))
                nc.vector.tensor_tensor(probs[:, :, :], ex[:, :, :], rs[:, :].rearrange("e (b o) -> e b o", o=1)
                                        .broadcast_to((E0, NB, S)), ALU.mult).then_inc(probs_sb, 1)
                dve.wait_ge(col_ps, i + 1)
                ch.link(nc.vector.tensor_copy(col[:, :, :].rearrange("p b e -> p (b e)"), banks[4][:, 0:NB * E0]))
                dve.wait_ge(row_in, i * 16 + 16)
                for n in range(NB):
                    for e in range(E0):
                        rank = R[:, bass.ds(i * NB + n, 1), e:e + 1].rearrange("p o s -> p (o s)")
                        last = nc.vector.scalar_tensor_tensor(
                            out=row[:, e, n * S:(n + 1) * S], in0=row[:, e, n * S:(n + 1) * S], scalar=col[:, n, e:e + 1],
                            in1=tie[:, :], op0=ALU.subtract, op1=ALU.is_gt, accum_out=rank)
                ch.link(last)
                nc.vector.scalar_tensor_tensor(out=taken[:, :, :], in0=R[:, bass.ds(i * NB, NB), 0:E0],
                                               scalar=float(CAP), in1=col[:, :, :], op0=ALU.is_lt, op1=ALU.mult
                                               ).then_inc(taken_sb, 1)
                dve.wait_ge(total_ps, i + 1)
                ch.link(nc.vector.tensor_scalar(total[:, :, :].rearrange("p b e -> p (b e)"), banks[5][:, 0:NB * E0],
                                                1e-9, None, ALU.add))
                ch.link(nc.vector.reciprocal(inv[:, :, :], total[:, :, :]))
                nc.vector.tensor_tensor(W[:, bass.ds(i * NB, NB), 0:E0], taken[:, :, :], inv[:, :, :], ALU.mult)
                assert ch.n == PER_TURN


def experts0_phase(nc, r, a, R, W, ACC, xs_dram):
    NH, NPAIR, SLOTS = 2, 4, 8 * CAP
    with ExitStack() as ctx:
        def sb(name, shape, dt=F32):
            return ctx.enter_context(nc.sbuf_tensor("e0_" + name, shape, dt))

        def sem(name):
            return ctx.enter_context(nc.semaphore("e0_" + name))

        w1 = [sb(f"w1_{v}", [128, KD, F0]) for v in range(2)]
        w2 = [sb(f"w2_{v}", [128, KD, F0]) for v in range(2)]
        w3 = [sb(f"w3_{v}", [128, KF0, D]) for v in range(2)]
        slot = sb("slot", [128, B, CAP])
        pick = [sb(f"pick{v}", [128, B, CAP]) for v in range(2)]
        put = [sb(f"put{v}", [128, B, CAP]) for v in range(2)]
        xg = [sb(f"xg{v}", [128, KD, B * CAP]) for v in range(2)]
        putT = [sb(f"putT{v}", [128, B // 2, S]) for v in range(2)]
        sg = [sb(f"sg{n}", [128, SLOTS]) for n in range(2)]
        hidden = [sb(f"hidden{h}", [128, KF0, SLOTS]) for h in range(NH)]
        eo = [sb(f"eo{n}", [128, D]) for n in range(2)]
        (made, pick_sb, put_sb, xg_ps, xg_sb, put_ps, putT_sb, g_ps, sg_sb, u_ps, hid_sb, eo_ps, eo_sb, sum_ps, acc_sb,
         held, chain) = (sem(n) for n in (
             "made", "pick_sb", "put_sb", "xg_ps", "xg_sb", "put_ps", "putT_sb", "g_ps", "sg_sb", "u_ps", "hid_sb",
             "eo_ps", "eo_sb", "sum_ps", "acc_sb", "held", "dve_chain"))
        w_in, zero_made, cleared = [sem(f"w_in{v}") for v in range(2)], sem("zero_made"), sem("cleared")
        zero = sb("zero", [128, D])
        A_PUTT, A_SG, A_HID, A_EO, A_SUM, A_ACC = 2, 1, 2, 2, 2, 1
        G_BANK, U_BANK, XK, EO, OUT = r.banks[2], r.banks[3], r.banks[0:2], r.banks[4:6], r.banks[6:8]
        block = ctx.enter_context(nc.Block())

        @block.sync
        def _(sp):
            def load(e, v):
                for t, name in ((w1[v], "L0_ffn_w1"), (w2[v], "L0_ffn_w2"), (w3[v], "L0_ffn_w3")):
                    src = a[name][bass.ds(e, 1), :, :].rearrange("o (k p) n -> p (o k) n", p=128)
                    sp.dma_start(t[:, :, :], src).then_inc(w_in[v], 16)

            load(0, 0)
            load(1, 1)
            with sp.Fori(0, E0 // 2 - 1) as i:
                for v in range(2):
                    sp.wait_ge(eo_ps, i * 16 + 8 * v + 8)
                    sp.sem_inc(held, 1)
                    load(i * 2 + v + 2, v)

        @block.gpsimd
        def _(pool):
            nc.gpsimd.iota(slot[:, :, :], pattern=[[0, B], [1, CAP]], base=0, channel_multiplier=0,
                           allow_small_or_imprecise_dtypes=True).then_inc(made, 1)
            nc.gpsimd.memset(ACC[:, :, :], 0.0).then_inc(made, 1)
            nc.gpsimd.memset(zero[:, :], 0.0).then_inc(zero_made, 1)
            pool.wait_ge(zero_made, 1)
            pool.dma_start(xs_dram.rearrange("(t p) d -> p t d", p=TT),
                           zero[:, :].rearrange("p (o d) -> p o d", o=1).broadcast_to((128, TILES, D))).then_inc(cleared, 16)
            pool.wait_ge(cleared, 16)

        @block.tensor
        def _(pe):
            def gather(i, v):
                e = i * 2 + v
                pe.wait_ge(pick_sb, e + 1)
                pe.wait_ge(putT_sb, e * 2 + A_PUTT)
                for h in range(NH):
                    if h == 1:
                        pe.wait_ge(xg_sb, e * 4 + 2)
                    for k in range(KD):
                        for n in range(B // NH):
                            b = h * (B // NH) + n
                            last = nc.tensor.matmul(XK[k][:, n * CAP:(n + 1) * CAP], r.XN[:, b, k * 128:(k + 1) * 128],
                                                    pick[v][:, b, :], start=True, stop=True)
                    last.then_inc(xg_ps, 1)
                pe.wait_ge(put_sb, e + 1)
                pe.wait_ge(xg_sb, e * 4 + 4)
                for p in range(B // 2):
                    last = nc.tensor.transpose(XK[p // 4][:, (p % 4) * S:(p % 4 + 1) * S],
                                               put[v][:, 2 * p:2 * p + 2, :].rearrange("p b c -> p (b c)"), r.ident[:, :])
                last.then_inc(put_ps, 1)

            def up(i, v, h):
                for f in range(KF0):
                    n = (i * 2 + v) * 8 + h * KF0 + f
                    pe.wait_ge(sg_sb, n + A_SG)
                    for k in range(KD):
                        last = nc.tensor.matmul(G_BANK[:, :], w1[v][:, k, f * 128:(f + 1) * 128],
                                                xg[v][:, k, h * SLOTS:(h + 1) * SLOTS], start=k == 0, stop=k == KD - 1)
                    last.then_inc(g_ps, 1)
                    pe.wait_ge(hid_sb, n + A_HID)
                    for k in range(KD):
                        last = nc.tensor.matmul(U_BANK[:, :], w2[v][:, k, f * 128:(f + 1) * 128],
                                                xg[v][:, k, h * SLOTS:(h + 1) * SLOTS], start=k == 0, stop=k == KD - 1)
                    last.then_inc(u_ps, 1)

            def down(i, v, q):
                h, p = q // NPAIR, q % NPAIR
                n = (i * 2 + v) * 8 + q
                pe.wait_ge(hid_sb, (i * 2 + v) * 8 + (h + 1) * KF0 + A_HID)
                pe.wait_ge(eo_sb, n - 1 + A_EO)
                for f in range(KF0):
                    last = nc.tensor.matmul(EO[q % 2][:, 0:D], hidden[h][:, f, p * 128:(p + 1) * 128], w3[v][:, f, :],
                                            start=f == 0, stop=f == KF0 - 1)
                last.then_inc(eo_ps, 1)

            def scatter(i, v, q):
                n = (i * 2 + v) * 8 + q
                pe.wait_ge(eo_sb, n + 1 + A_EO)
                pe.wait_ge(acc_sb, n + A_ACC)
                for t in range(2):
                    rows = slice(t * CAP, (t + 1) * CAP)
                    last = nc.tensor.matmul(OUT[t][:, 0:D], putT[v][rows, q, :], eo[q % 2][rows, :], start=True, stop=True)
                last.then_inc(sum_ps, 1)

            pe.wait_ge(made, 2)
            with pe.Fori(0, E0 // 2) as i:
                for v in range(2):
                    gather(i, v)
                    pe.wait_ge(w_in[v], i * 48 + 48)
                    pe.wait_ge(xg_sb, (i * 2 + v) * 4 + 4)
                    for h in range(NH):
                        up(i, v, h)
                    pe.wait_ge(putT_sb, (i * 2 + v) * 2 + 2 + A_PUTT)
                    down(i, v, 0)
                    for q in range(1, 2 * NPAIR):
                        down(i, v, q)
                        scatter(i, v, q - 1)
                    scatter(i, v, 2 * NPAIR - 1)

        @block.scalar
        def _(act):
            for s, ahead in ((putT_sb, A_PUTT), (sg_sb, A_SG), (eo_sb, A_EO), (hid_sb, A_HID), (sum_ps, A_SUM),
                             (acc_sb, A_ACC)):
                act.sem_inc(s, ahead)
            with act.Fori(0, E0 // 2) as i:
                for v in range(2):
                    e = i * 2 + v
                    for h in range(NH):
                        act.wait_ge(xg_ps, e * 2 + h + 1)
                        nc.scalar.copy(xg[v][:, 0, h * SLOTS:(h + 1) * SLOTS], XK[0][:, :]).then_inc(xg_sb, 1)
                    act.wait_ge(put_ps, e + 1)
                    nc.scalar.copy(putT[v][:, 0:4, :].rearrange("p q s -> p (q s)"), XK[0][:, :]).then_inc(putT_sb, 1)
                    for n in range(NH * KF0):
                        act.wait_ge(g_ps, e * 8 + n + 1)
                        act.wait_ge(hid_sb, e * 8 + n - 1 + A_HID)
                        nc.scalar.activation(sg[n % 2][:, :], G_BANK[:, :], ACT.Silu).then_inc(sg_sb, 1)
                    for q in range(2 * NPAIR):
                        act.wait_ge(eo_ps, e * 8 + q + 1)
                        act.wait_ge(sum_ps, e * 8 + q - 1 + A_SUM)
                        nc.scalar.copy(eo[q % 2][:, :], EO[q % 2][:, 0:D]).then_inc(eo_sb, 1)

        @block.vector
        def _(dve):
            dve.wait_ge(made, 2)

            def one_hots(e, v):
                rank = R[:, :, bass.ds(e, 1)].broadcast_to((128, B, CAP))
                nc.vector.tensor_tensor(pick[v][:, :, :], slot[:, :, :], rank, ALU.is_equal).then_inc(pick_sb, 1)
                dve.wait_ge(pick_sb, e + 1)
                nc.vector.tensor_tensor(put[v][:, :, :], pick[v][:, :, :], W[:, :, bass.ds(e, 1)]
                                        .broadcast_to((128, B, CAP)), ALU.mult).then_inc(put_sb, 1)

            one_hots(0, 0)
            with dve.Fori(0, E0 // 2) as i:
                for v in range(2):
                    e = i * 2 + v
                    for h in range(NH):
                        dve.wait_ge(xg_ps, e * 2 + h + 1)
                        nc.vector.tensor_copy(xg[v][:, 1, h * SLOTS:(h + 1) * SLOTS], XK[1][:, :]).then_inc(xg_sb, 1)
                    dve.wait_ge(put_ps, e + 1)
                    nc.vector.tensor_copy(putT[v][:, 4:8, :].rearrange("p q s -> p (q s)"), XK[1][:, :]).then_inc(putT_sb, 1)
                    one_hots(e + 1, 1 - v)
                    for n in range(NH * KF0):
                        dve.wait_ge(u_ps, e * 8 + n + 1)
                        dve.wait_ge(sg_sb, e * 8 + n + 1 + A_SG)
                        nc.vector.tensor_tensor(hidden[n // KF0][:, n % KF0, :], sg[n % 2][:, :], U_BANK[:, :], ALU.mult
                                                ).then_inc(hid_sb, 1)
                    dve.wait_ge(acc_sb, e * 8 + A_ACC)
                    for q in range(2 * NPAIR):
                        dve.wait_ge(sum_ps, e * 8 + q + 1 + A_SUM)
                        for t in range(2):
                            last = nc.vector.tensor_tensor(ACC[:, 2 * q + t, :], OUT[t][:, 0:D], ACC[:, 2 * q + t, :], ALU.add)
                        last.then_inc(acc_sb, 1)


E1, F1, TOPK, FS = 32, 192, 4, 512
FH = F1 // 2
KFS = FS // 128
TT = 128
TILES = (B * S * TOPK + E1 * (TT - 1)) // TT // 2 * 2 + 2


def router1_phase(nc, r, a, LG, SH):
    NB, NT = 4, B // 4
    with ExitStack() as ctx:
        def sb(name, shape, dt=F32):
            return ctx.enter_context(nc.sbuf_tensor("r1_" + name, shape, dt))

        def sem(name):
            return ctx.enter_context(nc.semaphore("r1_" + name))

        wr = sb("wr", [128, KD, E1 + 1])
        wg = sb("wg", [128, KD, FS])
        wu = sb("wu", [128, KD, FS])
        wd = sb("wd", [128, KFS, D])
        xb = sb("xb", [128, NB, D])
        xT = sb("xT", [128, KD, NB * S])
        sg = [sb(f"sg{n}", [128, NB * S]) for n in range(2)]
        hidden = sb("hidden", [128, KFS, NB * S])
        names = ("w_in", "xb_sb", "xt_ps", "xt_sb", "l_ps", "l_sb", "g_ps", "sg_sb", "u_ps", "hid_sb", "y_ps", "y_sb")
        w_in, xb_sb, xt_ps, xt_sb, l_ps, l_sb, g_ps, sg_sb, u_ps, hid_sb, y_ps, y_sb = (sem(n) for n in names)
        A_SG, A_HID, A_Y, A_XT, A_L = 1, 2, 2, 1, 1
        XK, LOG, G_BANK, U_BANK, Y = r.banks[0:2], r.banks[2], r.banks[3], r.banks[4], r.banks[5:7]
        block = ctx.enter_context(nc.Block())

        @block.sync
        def _(sp):
            def load(dst, name):
                sp.dma_start(dst, a[name].rearrange("(k p) n -> p k n", p=128)).then_inc(w_in, 16)

            load(wr[:, :, :], "L1_router_and_gate_w")
            load(wg[:, :, :], "L1_ffn_sh_gate")
            load(wu[:, :, :], "L1_ffn_sh_up")
            load(wd[:, :, :], "L1_ffn_sh_down")

        @block.tensor
        def _(pe):
            pe.wait_ge(w_in, 16 * 4)
            with pe.Fori(0, NT) as i:
                pe.wait_ge(xb_sb, i + 1)
                for k in range(KD):
                    for n in range(NB):
                        last = nc.tensor.transpose(XK[k][:, n * S:(n + 1) * S], xb[:, n, k * 128:(k + 1) * 128], r.ident[:, :])
                last.then_inc(xt_ps, 1)
                pe.wait_ge(xt_sb, i + 1 + A_XT)
                pe.wait_ge(l_sb, i + A_L)
                for n in range(NB):
                    for k in range(KD):
                        last = nc.tensor.matmul(LOG[:, n * (E1 + 1):(n + 1) * (E1 + 1)], xT[:, k, n * S:(n + 1) * S],
                                                wr[:, k, :], start=k == 0, stop=k == KD - 1)
                last.then_inc(l_ps, 1)
                for f in range(KFS):
                    m = i * KFS + f
                    pe.wait_ge(sg_sb, m + A_SG)
                    for k in range(KD):
                        last = nc.tensor.matmul(G_BANK[:, :], wg[:, k, f * 128:(f + 1) * 128], xT[:, k, :],
                                                start=k == 0, stop=k == KD - 1)
                    last.then_inc(g_ps, 1)
                    pe.wait_ge(hid_sb, m + A_HID)
                    for k in range(KD):
                        last = nc.tensor.matmul(U_BANK[:, :], wu[:, k, f * 128:(f + 1) * 128], xT[:, k, :],
                                                start=k == 0, stop=k == KD - 1)
                    last.then_inc(u_ps, 1)
                pe.wait_ge(hid_sb, i * KFS + KFS + A_HID)
                for n in range(NB):
                    pe.wait_ge(y_sb, i * NB + n - 1 + A_Y)
                    for f in range(KFS):
                        last = nc.tensor.matmul(Y[n % 2][:, 0:D], hidden[:, f, n * S:(n + 1) * S], wd[:, f, :],
                                                start=f == 0, stop=f == KFS - 1)
                    last.then_inc(y_ps, 1)

        @block.scalar
        def _(act):
            for s, ahead in ((sg_sb, A_SG), (hid_sb, A_HID), (y_sb, A_Y), (xt_sb, A_XT), (l_sb, A_L)):
                act.sem_inc(s, ahead)
            with act.Fori(0, NT) as i:
                for f in range(KFS):
                    m = i * KFS + f
                    act.wait_ge(g_ps, m + 1)
                    act.wait_ge(hid_sb, m - 1 + A_HID)
                    nc.scalar.activation(sg[f % 2][:, :], G_BANK[:, :], ACT.Silu).then_inc(sg_sb, 1)
                for n in range(NB):
                    act.wait_ge(y_ps, i * NB + n + 1)
                    nc.scalar.copy(SH[:, bass.ds(i * NB + n, 1), :].rearrange("p o d -> p (o d)"), Y[n % 2][:, 0:D]
                                   ).then_inc(y_sb, 1)

        @block.vector
        def _(dve):
            with dve.Fori(0, NT) as i:
                for n in range(NB):
                    b = i * NB + n
                    last = nc.vector.tensor_scalar(xb[:, n, :], r.X[:, bass.ds(b, 1), :].rearrange("p o d -> p (o d)"),
                                                   r.mv[:, bass.ds(b, 1), 0:1].rearrange("p o s -> p (o s)"),
                                                   r.rstd[:, bass.ds(b, 1)], ALU.subtract, ALU.mult)
                last.then_inc(xb_sb, 1)
                dve.wait_ge(xt_ps, i + 1)
                for k in range(KD):
                    last = nc.vector.tensor_copy(xT[:, k, :], XK[k][:, :])
                last.then_inc(xt_sb, 1)
                nc.vector.tensor_copy(r.XN[:, bass.ds(i * NB, NB), :], xb[:, :, :])
                dve.wait_ge(l_ps, i + 1)
                nc.vector.tensor_copy(LG[:, bass.ds(i * NB, NB), :],
                                      LOG[:, 0:NB * (E1 + 1)].rearrange("p (b e) -> p b e", b=NB)).then_inc(l_sb, 1)
                for f in range(KFS):
                    m = i * KFS + f
                    dve.wait_ge(u_ps, m + 1)
                    dve.wait_ge(sg_sb, m + 1 + A_SG)
                    nc.vector.tensor_tensor(hidden[:, f, :], sg[f % 2][:, :], U_BANK[:, :], ALU.mult).then_inc(hid_sb, 1)


def dispatch1_phase(nc, r, LG, w4, slots, sig, tile_expert, xs_dram):
    with ExitStack() as ctx:
        def sb(name, shape, dt=F32):
            return ctx.enter_context(nc.sbuf_tensor("d1_" + name, shape, dt))

        def sem(name):
            return ctx.enter_context(nc.semaphore("d1_" + name))

        negmax = sb("negmax", [128, B])
        ex = sb("ex", [128, B, E1])
        sums = sb("sums", [128, B])
        rs = sb("rs", [128, B])
        probs = sb("probs", [128, B, E1])
        ez = sb("ez", [128, B])
        ez1 = sb("ez1", [128, B])
        top = sb("top", [128, B, 8])
        top_at = sb("top_at", [128, B, 8], mybir.dt.uint32)
        at = sb("at", [128, B, TOPK])
        s4 = sb("s4", [128, B])
        i4 = sb("i4", [128, B])
        expert = sb("expert", [128, B, E1])
        choice = [sb(f"choice{k}", [128, B, E1]) for k in range(TOPK)]
        member = sb("member", [128, B, E1])
        earlier = sb("earlier", [128, 128])
        ones = sb("ones", [128, 128])
        before = sb("before", [128, B, E1])
        totals = sb("totals", [128, B, E1])
        upto = sb("upto", [128, B + 1, E1])
        edge = sb("edge", [128, E1, B * S // TT])
        over = sb("over", [128, E1, B * S // TT])
        ntiles = sb("ntiles", [128, E1])
        zeros = sb("zeros", [128, E1])
        ends = sb("ends", [128, E1])
        first = sb("first", [128, E1])
        slot = sb("slot", [128, B, E1])
        mine = sb("mine", [128, B, E1])
        slotf = sb("slotf", [128, TOPK, B])
        tile_at = sb("tile_at", [128, 1])
        done = sb("done", [128, E1])
        te = sb("te", [128, 1])
        (made, max_sb, ex_sb, mem_sb, cnt_ps, te_sb, te_ps, slots_sb, sent, chain) = (sem(n) for n in (
            "made", "max_sb", "ex_sb", "mem_sb", "cnt_ps", "te_sb", "te_ps", "slots_sb", "sent", "dve_chain"))
        BEFORE, TOTALS, TE = r.banks[0], r.banks[1], r.banks[2]
        block = ctx.enter_context(nc.Block())

        @block.gpsimd
        def _(pool):
            def iota(t, pattern, multiplier=0):
                nc.gpsimd.iota(t, pattern=pattern, base=0, channel_multiplier=multiplier,
                               allow_small_or_imprecise_dtypes=True).then_inc(made, 1)

            iota(expert[:, :, :], [[0, B], [1, E1]])
            iota(edge[:, :, :], [[0, E1], [TT, B * S // TT]])
            iota(tile_at[:, :], [[0, 1]], 1)
            nc.gpsimd.memset(ones[:, :], 1.0).then_inc(made, 1)
            nc.gpsimd.memset(earlier[:, :], 1.0).then_inc(made, 1)
            nc.gpsimd.memset(zeros[:, :], 0.0).then_inc(made, 1)
            pool.wait_ge(made, 6)
            nc.gpsimd.affine_select(out=earlier[:, :], in_=earlier[:, :], compare_op=ALU.is_gt, fill=0.0, base=0,
                                    pattern=[[1, 128]], channel_multiplier=-1).then_inc(made, 1)
            pool.wait_ge(slots_sb, 1)
            for b in range(B):
                for k in range(TOPK):
                    nc.gpsimd.indirect_dma_start(
                        out=xs_dram[:, :], out_offset=bass.IndirectOffsetOnAxis(ap=slots[:, b, k:k + 1], axis=0),
                        in_=r.XN[:, b, :], in_offset=None).then_inc(sent, 16)
            pool.wait_ge(sent, 16 * B * TOPK)

        @block.scalar
        def _(act):
            act.wait_ge(max_sb, 1)
            nc.scalar.activation(ex[:, :, :], ex[:, :, :], ACT.Exp)
            nc.scalar.activation(ez[:, :], LG[:, :, E1], ACT.Exp, scale=-1.0).then_inc(ex_sb, 1)

        @block.tensor
        def _(pe):
            pe.wait_ge(made, 7)
            pe.wait_ge(mem_sb, 1)
            m = member[:, :, :].rearrange("p b e -> p (b e)")
            nc.tensor.matmul(BEFORE[:, :], earlier[:, :], m, start=True, stop=True)
            nc.tensor.matmul(TOTALS[:, :], ones[:, :], m, start=True, stop=True).then_inc(cnt_ps, 1)
            pe.wait_ge(te_sb, 1)
            nc.tensor.matmul(TE[0:1, 0:128], te[:, :], r.ident[:, :], start=True, stop=True).then_inc(te_ps, 1)

        @block.vector
        def _(dve):
            ch = Chain(dve, chain)
            logits = LG[:, :, 0:E1]

            def along(t, n):
                return t.rearrange("p (b o) -> p b o", o=1).broadcast_to((128, B, n))

            dve.wait_ge(made, 7)
            ch.link(nc.vector.tensor_reduce(negmax[:, :], logits, AX_X, ALU.max, negate=True))
            nc.vector.tensor_tensor(ex[:, :, :], logits, along(negmax[:, :], E1), ALU.add).then_inc(max_sb, 1)
            dve.wait_ge(ex_sb, 1)
            ch.link(nc.vector.tensor_reduce(sums[:, :], ex[:, :, :], AX_X, ALU.add))
            ch.link(nc.vector.reciprocal(rs[:, :], sums[:, :]))
            nc.vector.tensor_scalar(ez1[:, :], ez[:, :], 1.0, None, ALU.add)
            ch.link(nc.vector.tensor_tensor(probs[:, :, :], ex[:, :, :], along(rs[:, :], E1), ALU.mult))
            nc.vector.reciprocal(sig[:, :], ez1[:, :])
            for b in range(B):
                last = nc.vector.max(top[:, b, :], probs[:, b, :])
            ch.link(last)
            for b in range(B):
                last = nc.vector.max_index(top_at[:, b, :], top[:, b, :], probs[:, b, :])
            ch.link(last)
            nc.vector.tensor_reduce(s4[:, :], top[:, :, 0:TOPK], AX_X, ALU.add)
            ch.link(nc.vector.tensor_copy(at[:, :, :], top_at[:, :, 0:TOPK]))
            nc.vector.reciprocal(i4[:, :], s4[:, :])
            for k in range(TOPK):
                last = nc.vector.tensor_tensor(choice[k][:, :, :], expert[:, :, :],
                                               at[:, :, k:k + 1].broadcast_to((128, B, E1)), ALU.is_equal)
            ch.link(last)
            nc.vector.tensor_tensor(w4[:, :, :], top[:, :, 0:TOPK], along(i4[:, :], TOPK), ALU.mult)
            ch.link(nc.vector.tensor_tensor(member[:, :, :], choice[0][:, :, :], choice[1][:, :, :], ALU.add))
            ch.link(nc.vector.tensor_tensor(member[:, :, :], member[:, :, :], choice[2][:, :, :], ALU.add))
            nc.vector.tensor_tensor(member[:, :, :], member[:, :, :], choice[3][:, :, :], ALU.add).then_inc(mem_sb, 1)
            ch.link(nc.vector.tensor_copy(upto[:, 0, :], zeros[:, :]))
            dve.wait_ge(cnt_ps, 1)
            nc.vector.tensor_copy(before[:, :, :].rearrange("p b e -> p (b e)"), BEFORE[:, :])
            ch.link(nc.vector.tensor_copy(totals[:, :, :].rearrange("p b e -> p (b e)"), TOTALS[:, :]))
            for b in range(B):
                ch.link(nc.vector.tensor_tensor(upto[:, b + 1, :], upto[:, b, :], totals[:, b, :], ALU.add))
            count = upto[:, B, :].rearrange("p (e o) -> p e o", o=1).broadcast_to((128, E1, B * S // TT))
            ch.link(nc.vector.tensor_tensor(over[:, :, :], count, edge[:, :, :], ALU.is_gt))
            ch.link(nc.vector.tensor_reduce(ntiles[:, :], over[:, :, :], AX_X, ALU.add))
            ch.link(nc.vector.tensor_tensor_scan(ends[:, :], ntiles[:, :], zeros[:, :], 0.0, ALU.add, ALU.add))
            ch.link(nc.vector.tensor_scalar(done[:, :], ends[:, :], tile_at[:, 0:1], None, ALU.is_le))
            ch.link(nc.vector.tensor_reduce(te[:, :], done[:, :], AX_X, ALU.add))
            nc.vector.tensor_scalar(te[:, :], te[:, :], float(E1 - 1), None, ALU.min).then_inc(te_sb, 1)
            ch.link(nc.vector.tensor_tensor(first[:, :], ends[:, :], ntiles[:, :], ALU.subtract))
            ch.link(nc.vector.tensor_scalar(first[:, :], first[:, :], float(TT), None, ALU.mult))
            ch.link(nc.vector.tensor_tensor(slot[:, :, :], before[:, :, :], upto[:, 0:B, :], ALU.add))
            ch.link(nc.vector.tensor_tensor(slot[:, :, :], slot[:, :, :],
                                            first[:, :].rearrange("p (o e) -> p o e", o=1).broadcast_to((128, B, E1)), ALU.add))
            for k in range(TOPK):
                ch.link(nc.vector.tensor_tensor(mine[:, :, :], choice[k][:, :, :], slot[:, :, :], ALU.mult))
                ch.link(nc.vector.tensor_reduce(slotf[:, k, :], mine[:, :, :], AX_X, ALU.add))
            nc.vector.tensor_copy(slots[:, :, :], slotf[:, :, :].rearrange("p k b -> p b k")).then_inc(slots_sb, 1)
            dve.wait_ge(te_ps, 1)
            ch.link(nc.vector.tensor_copy(tile_expert[:, :], TE[0:1, 0:TILES]))


def experts1_phase(nc, r, a, tile_expert, xs_dram, ys_dram):
    with ExitStack() as ctx:
        def sb(name, shape, dt=F32):
            return ctx.enter_context(nc.sbuf_tensor("e1_" + name, shape, dt))

        def sem(name):
            return ctx.enter_context(nc.semaphore("e1_" + name))

        wg = [sb(f"wg{v}", [128, KD, F1]) for v in range(2)]
        wu = [sb(f"wu{v}", [128, KD, F1]) for v in range(2)]
        wd = [sb(f"wd{v}", [FH, 2, D]) for v in range(2)]
        xt = [sb(f"xt{v}", [128, D]) for v in range(2)]
        xT = [sb(f"xT{v}", [128, KD, TT]) for v in range(2)]
        sg = [sb(f"sg{v}", [FH, 2, TT]) for v in range(2)]
        hidden = [sb(f"hidden{v}", [FH, 2, TT]) for v in range(2)]
        yt = [sb(f"yt{v}", [128, D]) for v in range(2)]
        x_in, w_in, y_out = ([sem(f"{n}{v}") for v in range(2)] for n in ("x_in", "w_in", "y_out"))
        xt_ps, xt_sb, g_ps, sg_sb, u_ps, hid_sb, y_ps, y_sb, held = (sem(n) for n in (
            "xt_ps", "xt_sb", "g_ps", "sg_sb", "u_ps", "hid_sb", "y_ps", "y_sb", "held"))
        AHEAD = 2
        XT, G, U, Y = r.banks[0:2], r.banks[2:4], r.banks[4:6], r.banks[6:8]
        block = ctx.enter_context(nc.Block())

        @block.sync
        def _(sp):
            with sp.Fori(0, TILES // 2) as i:
                for v in range(2):
                    t = i * 2 + v
                    sp.wait_ge(y_ps, t - 1 + AHEAD)
                    sp.sem_inc(held, 1)
                    sp.dma_start(xt[v][:, :], xs_dram[bass.ds(t * TT, TT), :]).then_inc(x_in[v], 16)
                    e = sp.value_load(tile_expert[0:1, bass.ds(t, 1)], min_val=0, max_val=E1 - 1)
                    for w, name in ((wg[v], "L1_ffn_w_gate"), (wu[v], "L1_ffn_w_up")):
                        sp.dma_start(w[:, :, :], a[name][bass.ds(e, 1), :, :].rearrange("o (k p) n -> p (o k) n", p=128)
                                     ).then_inc(w_in[v], 16)
                    sp.dma_start(wd[v][:, :, :], a["L1_ffn_w_down"][bass.ds(e, 1), :, :]
                                 .rearrange("o (k p) n -> p (o k) n", p=FH)).then_inc(w_in[v], 16)

        @block.tensor
        def _(pe):
            def turn(i, v):
                t = i * 2 + v
                pe.wait_ge(x_in[v], i * 16 + 16)
                pe.wait_ge(xt_sb, t - 1 + AHEAD)
                for k in range(KD):
                    last = nc.tensor.transpose(XT[v][:, k * TT:(k + 1) * TT], xt[v][:, k * 128:(k + 1) * 128], r.ident[:, :])
                last.then_inc(xt_ps, 1)

            def up(i, v):
                t = i * 2 + v
                pe.wait_ge(xt_sb, t + 1 + AHEAD)
                pe.wait_ge(w_in[v], i * 48 + 48)
                for free, bank, w, full in ((sg_sb, G, wg, g_ps), (hid_sb, U, wu, u_ps)):
                    pe.wait_ge(free, t - 1 + AHEAD)
                    for m in range(2):
                        for k in range(KD):
                            last = nc.tensor.matmul(bank[v][0:FH, m * TT:(m + 1) * TT], w[v][:, k, m * FH:(m + 1) * FH],
                                                    xT[v][:, k, :], start=k == 0, stop=k == KD - 1)
                    last.then_inc(full, 1)

            def down(i, v):
                t = i * 2 + v
                pe.wait_ge(hid_sb, t + 1 + AHEAD)
                pe.wait_ge(y_sb, t - 1 + AHEAD)
                for m in range(2):
                    last = nc.tensor.matmul(Y[v][:, 0:D], hidden[v][:, m, :], wd[v][:, m, :], start=m == 0, stop=m == 1)
                last.then_inc(y_ps, 1)

            with pe.Fori(0, TILES // 2) as i:
                for stage in (turn, up, down):
                    for v in range(2):
                        stage(i, v)

        @block.scalar
        def _(act):
            for s in (xt_sb, sg_sb, hid_sb, y_ps, y_sb):
                act.sem_inc(s, AHEAD)
            for v in range(2):
                act.sem_inc(y_out[v], 16)
            with act.Fori(0, TILES // 2) as i:
                for v in range(2):
                    t = i * 2 + v
                    act.wait_ge(g_ps, t + 1)
                    nc.scalar.activation(sg[v][:, :, :].rearrange("p m t -> p (m t)"), G[v][0:FH, 0:2 * TT], ACT.Silu
                                         ).then_inc(sg_sb, 1)
                for v in range(2):
                    t = i * 2 + v
                    act.wait_ge(y_ps, t + 1 + AHEAD)
                    act.wait_ge(y_out[v], i * 16 + 16)
                    nc.scalar.copy(yt[v][:, :], Y[v][:, 0:D]).then_inc(y_sb, 1)
                    act.wait_ge(y_sb, t + 1 + AHEAD)
                    act.dma_start(ys_dram[bass.ds(t * TT, TT), :], yt[v][:, :]).then_inc(y_out[v], 16)
            for v in range(2):
                act.wait_ge(y_out[v], (1 + TILES // 2) * 16)

        @block.vector
        def _(dve):
            with dve.Fori(0, TILES // 2) as i:
                for v in range(2):
                    t = i * 2 + v
                    dve.wait_ge(xt_ps, t + 1)
                    nc.vector.tensor_copy(xT[v][:, :, :].rearrange("p k t -> p (k t)"), XT[v][:, 0:D]).then_inc(xt_sb, 1)
                for v in range(2):
                    t = i * 2 + v
                    dve.wait_ge(u_ps, t + 1)
                    dve.wait_ge(sg_sb, t + 1 + AHEAD)
                    nc.vector.tensor_tensor(hidden[v][:, :, :].rearrange("p m t -> p (m t)"),
                                            sg[v][:, :, :].rearrange("p m t -> p (m t)"), U[v][0:FH, 0:2 * TT], ALU.mult
                                            ).then_inc(hid_sb, 1)


def combine1_phase(nc, r, w4, slots, sig, SH, ys_dram, out):
    NBUF = 4
    with ExitStack() as ctx:
        def sb(name, shape, dt=F32):
            return ctx.enter_context(nc.sbuf_tensor("c1_" + name, shape, dt))

        def sem(name):
            return ctx.enter_context(nc.semaphore("c1_" + name))

        y = [sb(f"y{n}", [128, TOPK, D]) for n in range(NBUF)]
        y_in = [sem(f"y_in{n}") for n in range(NBUF)]
        x_sb, stored, chain = sem("x_sb"), sem("stored"), sem("dve_chain")
        block = ctx.enter_context(nc.Block())

        @block.gpsimd
        def _(pool):
            for b in range(B):
                if b >= NBUF:
                    pool.wait_ge(x_sb, b - NBUF + 1)
                for k in range(TOPK):
                    nc.gpsimd.indirect_dma_start(
                        out=y[b % NBUF][:, k, :], out_offset=None, in_=ys_dram[:, :],
                        in_offset=bass.IndirectOffsetOnAxis(ap=slots[:, b, k:k + 1], axis=0)).then_inc(y_in[b % NBUF], 16)

        @block.vector
        def _(dve):
            ch = Chain(dve, chain)
            for b in range(B):
                acc = SH[:, b, :]
                ch.link(nc.vector.tensor_scalar(acc, acc, sig[:, b:b + 1], None, ALU.mult))
                dve.wait_ge(y_in[b % NBUF], (b // NBUF + 1) * 16 * TOPK)
                for k in range(TOPK):
                    ch.link(nc.vector.scalar_tensor_tensor(out=acc, in0=y[b % NBUF][:, k, :], scalar=w4[:, b, k:k + 1],
                                                           in1=acc, op0=ALU.mult, op1=ALU.add))
                nc.vector.scalar_tensor_tensor(out=r.X[:, b, :], in0=acc, scalar=r.gates[:, 3:4], in1=r.X[:, b, :],
                                               op0=ALU.mult, op1=ALU.add).then_inc(x_sb, 1)

        @block.sync
        def _(sp):
            for b in range(B):
                sp.wait_ge(x_sb, b + 1)
                sp.dma_start(out[b, :, :], r.X[:, b, :]).then_inc(stored, 16)
            sp.wait_ge(stored, 16 * B)


def build(nc, a, out):
    with ExitStack() as ctx:
        r = Resident(nc, ctx)
        signals = AttentionSignals(nc, ctx)
        xs_dram = nc.dram_tensor("xs_dram", (TILES * TT, D), F32, kind="Internal").ap()
        load_phase(nc, r, a)
        stats_phase(nc, r, "ln_xattn0")
        attention_phase(nc, r, a, 0, signals)
        stats_phase(nc, r, "ln_ffn0", added=r.XN, gate=r.gates[:, 0:1], clear=signals)
        with ExitStack() as ffn:
            ACC = ffn.enter_context(nc.sbuf_tensor("ACC", [128, B, D], F32))
            R = ffn.enter_context(nc.sbuf_tensor("R", [128, B, E0 + 1], F32))
            W = ffn.enter_context(nc.sbuf_tensor("W", [128, B, E0 + 1], F32))
            router0_phase(nc, r, a, R, W)
            experts0_phase(nc, r, a, R, W, ACC, xs_dram)
            stats_phase(nc, r, "ln_xattn1", added=ACC, gate=r.gates[:, 2:3])
        attention_phase(nc, r, a, 1, signals)
        stats_phase(nc, r, "ln_ffn1")
        LG, SH, w4, sig = (ctx.enter_context(nc.sbuf_tensor(n, s, F32)) for n, s in (
            ("LG", [128, B, E1 + 1]), ("SH", [128, B, D]), ("w4", [128, B, TOPK]), ("sig", [128, B])))
        slots = ctx.enter_context(nc.sbuf_tensor("slots", [128, B, TOPK], I32))
        tile_expert = ctx.enter_context(nc.sbuf_tensor("tile_expert", [1, TILES], I32))
        ys_dram = nc.dram_tensor("ys_dram", (TILES * TT, D), F32, kind="Internal").ap()
        router1_phase(nc, r, a, LG, SH)
        dispatch1_phase(nc, r, LG, w4, slots, sig, tile_expert, xs_dram)
        experts1_phase(nc, r, a, tile_expert, xs_dram, ys_dram)
        combine1_phase(nc, r, w4, slots, sig, SH, ys_dram, out)


def kernel(**inputs):
    import numpy as np
    import concourse.bacc as bacc
    from concourse.bass_utils import run_bass_kernel_spmd as run

    laid_out = {
        "x": inputs["x"],
        "ctx_t": np.asarray(inputs["ctx_1024"]).transpose(0, 2, 1),
        "mask_pad": np.asarray(inputs["mask_BxS2_bf0"]),
        "mask_BxSxS2_ik0": inputs["mask_BxSxS2_ik0"],
        "L0_wq_t": np.asarray(inputs["L0_xattn_Wq"]).T,
        "L0_wk_t": np.asarray(inputs["L0_xattn_Wk"]).T,
        "L0_wv_t": np.asarray(inputs["L0_xattn_Wv"]).T,
        "L1_wq_t": np.asarray(inputs["L1_xattn_w_q"]).T,
        "L1_wk_t": np.asarray(inputs["L1_xattn_w_k"]).T,
        "L1_wv_t": np.asarray(inputs["L1_xattn_w_v"]).T,
        "L1_router_and_gate_w": np.concatenate([np.asarray(inputs["L1_ffn_router_w"]),
                                                np.asarray(inputs["L1_ffn_sh_gate_w"])], axis=1),
        "L1_wo_t": np.asarray(inputs["L1_xattn_w_o"]).T,
    }
    for name in ("g_xattn", "g_ffn", "L0_xattn_bq", "L0_xattn_bk", "L0_xattn_bv", "L1_xattn_b_o", "L0_ffn_router_w1", "L0_ffn_router_w2",
                 "L0_ffn_w1", "L0_ffn_w2", "L0_ffn_w3", "L1_ffn_w_gate", "L1_ffn_w_up", "L1_ffn_w_down",
                 "L1_ffn_sh_gate", "L1_ffn_sh_up", "L1_ffn_sh_down"):
        laid_out[name] = inputs[name]

    nc = bacc.Bacc("TRN2", target_bir_lowering=False, num_devices=1)
    arrays, args = {}, {}
    for name, value in laid_out.items():
        value = np.ascontiguousarray(value)
        arrays[f"in_{name}"] = value
        args[name] = nc.dram_tensor(f"in_{name}", value.shape, U8 if value.dtype == bool else mybir.dt.from_np(value.dtype), kind="ExternalInput").ap()
    out = nc.dram_tensor("out", (B, S, D), F32, kind="ExternalOutput").ap()
    build(nc, args, out)
    return run(nc, [arrays], core_ids=[0]).results[0]["out"]
```

```python
import concourse.bass as bass
from concourse import mybir
from contextlib import ExitStack

ACT = mybir.ActivationFunctionType
ALU = mybir.AluOpType
AX_X = mybir.AxisListType.X
F32 = mybir.dt.float32
BF16 = mybir.dt.bfloat16
F32R = mybir.dt.float32r
I32 = mybir.dt.int32
U8 = mybir.dt.uint8

B, S, D = 16, 128, 256
H, DH = 16, 16
KD = D // 128
STRIPS = 4
HS = H // STRIPS
EPS = 1e-5
MASKED = -2.0 ** 120


class Chain:

    def __init__(self, eng, sem, base=0):
        self.eng, self.sem, self.n, self.base = eng, sem, 0, base

    def link(self, ins):
        self.n += 1
        ins.then_inc(self.sem, 1)
        self.eng.wait_ge(self.sem, self.base + self.n)


class Resident:

    def __init__(self, nc, ctx):
        def sb(name, shape, dt=F32):
            return ctx.enter_context(nc.sbuf_tensor(name, shape, dt))

        self.X = sb("X", [128, B, D])
        self.XN = None
        self.ident = sb("ident", [128, 128])
        self.ident_bf = sb("ident_bf", [128, 128], BF16)
        self.gates = sb("gates", [128, 4])
        self.stats = sb("stats", [128, B, 6])
        self.mv = sb("mv", [128, B, 2])
        self.var = sb("var", [128, B])
        self.std = sb("std", [128, B])
        self.rstd = sb("rstd", [128, B])
        self.held = ctx.enter_context(nc.semaphore("held"))
        self.banks = [ctx.enter_context(nc.psum_tensor(f"bank{i}", [128, 512], F32)) for i in range(8)]


def load_phase(nc, r, a):
    with ExitStack() as ctx:
        s_x, s_g, s_zero, s_ident, s_gates = (ctx.enter_context(nc.semaphore(n)) for n in (
            "x_loaded", "g_loaded", "ident_zeroed", "ident_made", "gates_made"))
        block = ctx.enter_context(nc.Block())

        @block.sync
        def _(sp):
            sp.dma_start(r.X[:, :, :], a["x"].rearrange("b s d -> s b d")).then_inc(s_x, 16)
            sp.dma_start(r.gates[:, 0:2], a["g_xattn"].partition_broadcast(128)).then_inc(s_g, 16)
            sp.dma_start(r.gates[:, 2:4], a["g_ffn"].partition_broadcast(128)).then_inc(s_g, 16)
            sp.wait_ge(s_x, 16)

        @block.gpsimd
        def _(pool):
            nc.gpsimd.memset(r.ident[:, :], 0.0).then_inc(s_zero, 1)
            nc.gpsimd.memset(r.ident_bf[:, :], 0.0).then_inc(s_zero, 1)
            pool.wait_ge(s_zero, 2)
            for t in (r.ident, r.ident_bf):
                nc.gpsimd.affine_select(out=t[:, :], in_=t[:, :], compare_op=ALU.not_equal, fill=1.0, base=0,
                                        pattern=[[-1, 128]], channel_multiplier=1).then_inc(s_ident, 1)
            pool.wait_ge(s_ident, 2)

        @block.scalar
        def _(act):
            act.wait_ge(s_g, 32)
            nc.scalar.activation(r.gates[:, :], r.gates[:, :], ACT.Tanh).then_inc(s_gates, 1)
            act.wait_ge(s_gates, 1)


def stats_phase(nc, r, name, added=None, gate=None, clear=None):
    with ExitStack() as ctx:
        s_chain, s_var, s_std = (ctx.enter_context(nc.semaphore(f"{name}_{n}")) for n in
                                 ("dve_chain", "var_ready", "std_ready"))
        block = ctx.enter_context(nc.Block())

        @block.vector
        def _(dve):
            ch = Chain(dve, s_chain)
            if added is not None:
                for b in range(B):
                    last = nc.vector.scalar_tensor_tensor(out=r.X[:, b, :], in0=added[:, b, :], scalar=gate,
                                                          in1=r.X[:, b, :], op0=ALU.mult, op1=ALU.add)
                ch.link(last)
            for b in range(B):
                last = nc.vector.bn_stats(r.stats[:, b, :], r.X[:, b, :])
            ch.link(last)
            for b in range(B):
                last = nc.vector.bn_aggr(r.mv[:, b, :], r.stats[:, b, :])
            ch.link(last)
            nc.vector.tensor_scalar(r.var[:, :], r.mv[:, :, 1], EPS, None, ALU.add).then_inc(s_var, 1)
            dve.wait_ge(s_std, 1)
            ch.link(nc.vector.reciprocal(r.rstd[:, :], r.std[:, :]))

        @block.scalar
        def _(act):
            act.wait_ge(s_var, 1)
            nc.scalar.activation(r.std[:, :], r.var[:, :], ACT.Sqrt).then_inc(s_std, 1)

        if clear is not None:
            @block.sync
            def _(sp):
                sp.sem_clear(range(min(clear.numbers), max(clear.numbers) + 1))


class AttentionSignals:

    def __init__(self, nc, ctx):
        self.numbers = []

        def sem(name):
            s = ctx.enter_context(nc.semaphore("attn_" + name))
            self.numbers.append(s.num)
            return s

        def pair(name):
            return [sem(name + "0"), sem(name + "1")]

        self.w_in = sem("w_in")
        self.w_made = sem("w_made")
        self.causal_made = sem("causal_made")
        self.zeroed = sem("zeroed")
        self.mask_sb = sem("mask_sb")
        self.k_tok_sb = sem("k_tok_sb")
        self.q_tok_sb = sem("q_tok_sb")
        self.k_hi_sb = sem("k_hi_sb")
        self.q_hi_sb = sem("q_hi_sb")
        self.xb_sb = sem("xb_sb")
        self.xt_ps = sem("xt_ps")
        self.xt_sb = sem("xt_sb")
        self.q_ps = sem("q_ps")
        self.kv_ps = sem("kv_ps")
        self.q_sb = sem("q_sb")
        self.qk_sb = sem("qk_sb")
        self.v_sb = sem("v_sb")
        self.s_ps = sem("s_ps")
        self.max_sb = sem("max_sb")
        self.p_sb = sem("p_sb")
        self.pt_ps = sem("pt_ps")
        self.pt_sb = sem("pt_sb")
        self.pv_ps = sem("pv_ps")
        self.o_sb = sem("o_sb")
        self.o_in = sem("o_in")
        self.k_ps = sem("k_ps")
        self.ot_ps = sem("ot_ps")
        self.ot_sb = sem("ot_sb")
        self.y_ps = sem("y_ps")
        self.y_sb = sem("y_sb")
        self.chain = sem("chain")
        self.v_out = pair("v_out")
        self.v_in = pair("v_in")
        self.o_out = pair("o_out")


def attention_phase(nc, r, a, layer, signals):
    pre = f"a{layer}_"
    S_BANKS, PT_BANKS, KV, XQ = r.banks[0:4], r.banks[4:6], r.banks[6], r.banks[7]
    O = S_BANKS[0]
    BANK_ORDER = (1, 2, 3, 0)
    NJ = STRIPS
    AHEAD = 5
    FIRST, FIRST_DMA = 1, 16

    def head(j, g):
        return HS * j + g if layer == 0 else STRIPS * g + j

    with ExitStack() as ctx:
        def sb(name, shape, dt=F32):
            return ctx.enter_context(nc.sbuf_tensor(pre + name, shape, dt))

        xb = [sb(f"xb{u}", [128, D]) for u in range(2)]
        xT = [sb(f"xT{u}", [128, KD, S]) for u in range(2)]
        cT = [sb(f"cT{u}", [128, KD, S]) for u in range(2)]
        qT = [sb(f"qT{u}", [128, HS, S], F32R) for u in range(2)]
        kA = [sb(f"kA{u}", [128, HS, S], F32R) for u in range(2)]
        kB = [sb(f"kB{u}", [128, HS, S], F32R) for u in range(2)]
        vtok = [sb(f"vtok{u}", [128, H, DH + 1]) for u in range(2)]
        mask = [sb(f"mask{u}", [128, S], BF16) for u in range(2)]
        negmax = [sb(f"negmax{u}", [128, NJ, HS]) for u in range(2)]
        rinv = [sb(f"rinv{u}", [128, H]) for u in range(2)]
        osb = [sb(f"osb{u}", [128, H, DH]) for u in range(2)]
        P = sb("P", [128, NJ, HS, S])
        pT = [sb(f"pT{u}", [128, HS, S]) for u in range(2)]
        qhi = sb("qhi", [128, HS, S], F32R)
        low_cols = sb("low_cols", [128, STRIPS, DH])
        low_rows = sb("low_rows", [128, 1])
        if layer == 0:
            padmask = [sb(f"padmask{u}", [128, S], U8) for u in range(2)]
            causal = sb("causal", [128, S])
            q_tok = sb("q_tok", [128, H, 2, DH])
            k_tok = sb("k_tok", [128, H, 2, DH])
            q_strips = sb("q_strips", [128, HS, S])
            k_strips = sb("k_strips", [128, HS, S])
            vs = [sb(f"vs{u}", [128, H, DH + 1]) for u in range(2)]
            wq = sb("wq", [128, KD, D])
            wkv = sb("wkv", [128, KD, 2 * D])
            bq = sb("bq", [128, D])
            bkv = sb("bkv", [128, 2 * D])
            v_dram = nc.dram_tensor(pre + "v_dram", (B * S * D,), F32, kind="Internal").ap()
            o_dram = nc.dram_tensor(pre + "o_dram", (B * S * D,), F32, kind="Internal").ap()
        else:
            imask = [sb(f"imask{u}", [128, S], I32) for u in range(2)]
            wdense = sb("wdense", [128, KD, 2 * D])
            wqp = sb("wqp", [128, KD, H, 2 * DH])
            wkp = sb("wkp", [128, KD, H, 2 * DH])
            wv = sb("wv", [128, KD, D])
            wo = sb("wo", [128, KD, D])
            bo = sb("bo", [128, D])
            oT = [sb(f"oT{u}", [128, KD, S]) for u in range(2)]
            proj = [sb(f"proj{u}", [128, D]) for u in range(2)]
            vs = vtok

        q = signals
        mask_in, ctx_in = ([ctx.enter_context(nc.semaphore(f"{pre}{n}{u}")) for u in range(2)] for n in ("mask_in", "ctx_in"))
        block = ctx.enter_context(nc.Block())

        @block.sync
        def _(sp):
            def hold(sp, sem, value):
                sp.wait_ge(sem, value)
                sp.sem_inc(r.held, 1)

            def weights(dst, name):
                sp.dma_start(dst, a[name].rearrange("(k p) n -> p k n", p=128)).then_inc(q.w_in, 16)

            if layer == 0:
                weights(wq[:, :, :], "L0_wq_t")
                weights(wkv[:, :, 0:D], "L0_wk_t")
                weights(wkv[:, :, D:2 * D], "L0_wv_t")
                sp.dma_start(bq[:, :], a["L0_xattn_bq"].partition_broadcast(128)).then_inc(q.w_in, 16)
                sp.dma_start(bkv[:, 0:D], a["L0_xattn_bk"].partition_broadcast(128)).then_inc(q.w_in, 16)
                sp.dma_start(bkv[:, D:2 * D], a["L0_xattn_bv"].partition_broadcast(128)).then_inc(q.w_in, 16)
                sp.wait_ge(q.zeroed, 2)
                with sp.Fori(0, B // 2) as i:
                    for u in range(2):
                        b = i * 2 + u
                        vd = v_dram[bass.ds(sp.snap(b * (S * D)), S * D)]
                        hold(sp, q.v_sb, b + 1)
                        sp.dma_start(vd.rearrange("(s h e) -> s h e", h=H, e=DH), vtok[u][:, :, 0:DH]).then_inc(q.v_out[u], 16)
                        hold(sp, q.v_out[u], i * 16 + 16 + FIRST_DMA)
                        hold(sp, q.pv_ps, (b - 1) * NJ + AHEAD)
                        sp.dma_start(vs[u][:, :, 0:DH], vd.rearrange("(h p e) -> p h e", h=H, e=DH)).then_inc(q.v_in[u], 16)
                    for u in range(2):
                        b = i * 2 + u
                        od = o_dram[bass.ds(sp.snap(b * (S * D)), S * D)]
                        hold(sp, q.o_sb, b + 1 + FIRST)
                        sp.dma_start(od.rearrange("(h p e) -> p h e", h=H, e=DH), osb[u][:, :, :]).then_inc(q.o_out[u], 16)
                for u in range(2):
                    sp.wait_ge(q.o_out[u], 16 * B // 2 + FIRST_DMA)
                sp.dma_start(r.XN[:, :, :], o_dram.rearrange("(b s d) -> s b d", b=B, s=S)).then_inc(q.o_in, 16)
                sp.wait_ge(q.o_in, 16)
            else:
                weights(wdense[:, :, 0:D], "L1_wq_t")
                weights(wdense[:, :, D:2 * D], "L1_wk_t")
                weights(wv[:, :, :], "L1_wv_t")
                weights(wo[:, :, :], "L1_wo_t")
                sp.dma_start(bo[:, :], a["L1_xattn_b_o"].partition_broadcast(128)).then_inc(q.w_in, 16)

        @block.gpsimd
        def _(pool):
            for u in range(2):
                nc.gpsimd.memset(vs[u][:, :, :], 1.0).then_inc(q.zeroed, 1)
            nc.gpsimd.tensor_copy(low_cols[:, :, :], r.ident[:, :].rearrange("p (j n) -> p j n", j=STRIPS)[:, :, DH:2 * DH]
                                  ).then_inc(q.zeroed, 1)
            if layer == 0:
                nc.gpsimd.memset(causal[:, :], 0.0).then_inc(q.zeroed, 1)
                pool.wait_ge(q.zeroed, 4)
                nc.gpsimd.affine_select(out=causal[:, :], in_=causal[:, :], compare_op=ALU.is_ge, fill=MASKED, base=0,
                                        pattern=[[-1, S]], channel_multiplier=1).then_inc(q.causal_made, 1)
            else:
                pool.wait_ge(q.w_in, 16 * 5)
                for k in range(KD):
                    for half in range(2):
                        for n, (t, scale) in enumerate(((wqp, DH ** -0.5), (wkp, 1.0))):
                            src = wdense[:, k, n * D:(n + 1) * D].rearrange("p (h e) -> p h e", h=H)
                            nc.gpsimd.tensor_scalar(t[:, k, :, half * DH:(half + 1) * DH], src, scale, None, ALU.mult
                                                    ).then_inc(q.w_made, 1)
            with pool.Fori(0, B // 2) as i:
                for u in range(2):
                    b = i * 2 + u
                    pool.wait_ge(q.mask_sb, b + FIRST)
                    pool.wait_ge(q.kv_ps, b + FIRST)
                    if layer == 0:
                        src = a["mask_pad"][bass.ds(b, 1), :].rearrange("o s -> (o s)").partition_broadcast(128)
                        pool.dma_start(padmask[u][:, :], src).then_inc(mask_in[u], 16)
                    else:
                        src = a["mask_BxSxS2_ik0"][bass.ds(b, 1), :, :].rearrange("o q k -> (o q) k")
                        pool.dma_start(imask[u][:, :], src).then_inc(mask_in[u], 16)
                    src = a["ctx_t"][bass.ds(b, 1), :, :].rearrange("o (k p) s -> p (o k) s", p=128)
                    pool.dma_start(cT[u][:, :, :], src).then_inc(ctx_in[u], 16)
                    if layer == 0:
                        pool.wait_ge(q.k_tok_sb, b + 1)
                        pool.sem_inc(r.held, 1)
                        nc.gpsimd.tensor_copy(kA[u][:, :, :].rearrange("p g s -> p (g s)"),
                                              k_strips[:, :, :].rearrange("p g s -> p (g s)")).then_inc(q.k_hi_sb, 1)
                        pool.wait_ge(q.q_tok_sb, b + 1)
                        pool.sem_inc(r.held, 1)
                        nc.gpsimd.tensor_copy(qhi[:, :, :].rearrange("p g s -> p (g s)"),
                                              q_strips[:, :, :].rearrange("p g s -> p (g s)")).then_inc(q.q_hi_sb, 1)

        @block.tensor
        def _(pe):
            pe.wait_ge(q.w_in, 16 * (6 if layer == 0 else 5))
            pe.wait_ge(q.w_made, 1 if layer == 0 else 4 * KD)

            def project(i, u):
                b = i * 2 + u
                pe.wait_ge(q.xb_sb, b + 1)
                for k in range(KD):
                    last = nc.tensor.transpose(XQ[:, k * S:(k + 1) * S], xb[u][:, k * 128:(k + 1) * 128], r.ident[:, :])
                last.then_inc(q.xt_ps, 1)
                pe.wait_ge(ctx_in[u], i * 16 + 16)
                if layer == 0:
                    for k in range(KD):
                        last = nc.tensor.matmul(KV[:, :], cT[u][:, k, :], wkv[:, k, :], start=k == 0, stop=k == KD - 1)
                    last.then_inc(q.kv_ps, 1)
                    pe.wait_ge(q.xt_sb, b + 1)
                    for k in range(KD):
                        last = nc.tensor.matmul(XQ[:, D:2 * D], xT[u][:, k, :], wq[:, k, :], start=k == 0, stop=k == KD - 1)
                    last.then_inc(q.q_ps, 1)
                else:
                    pe.wait_ge(q.y_sb, b - 1 + FIRST)
                    pe.wait_ge(q.xt_sb, b + 1)
                    for k in range(KD):
                        last = nc.tensor.matmul(XQ[:, D:2 * D], cT[u][:, k, :], wv[:, k, :], start=k == 0, stop=k == KD - 1)
                    last.then_inc(q.kv_ps, 1)
                    for g in range(HS):
                        for k in range(KD):
                            w = wqp[:, k, STRIPS * g:STRIPS * g + STRIPS, :].rearrange("p h e -> p (h e)")
                            last = nc.tensor.matmul(KV[:, g * S:(g + 1) * S], w, xT[u][:, k, :],
                                                    start=k == 0, stop=k == KD - 1)
                    last.then_inc(q.q_ps, 1)
                    pe.wait_ge(q.q_sb, b + 1 + FIRST)
                    for g in range(HS):
                        for k in range(KD):
                            w = wkp[:, k, STRIPS * g:STRIPS * g + STRIPS, :].rearrange("p h e -> p (h e)")
                            last = nc.tensor.matmul(KV[:, g * S:(g + 1) * S], w, cT[u][:, k, :],
                                                    start=k == 0, stop=k == KD - 1)
                    last.then_inc(q.k_ps, 1)

            def scores(i, u):
                b = i * 2 + u
                pe.wait_ge(q.mask_sb, b + 1 + FIRST)
                pe.wait_ge(q.p_sb, b * NJ + FIRST)
                for j in BANK_ORDER:
                    if j == 0:
                        pe.wait_ge(q.o_sb, b + FIRST)
                    m = mask[u][:, :].rearrange("p (o s) -> p o s", o=1).broadcast_to((128, HS, S))
                    nc.tensor.matmul(S_BANKS[j][:, :], r.ident_bf[:, :], m, start=True, stop=False)
                pe.wait_ge(q.qk_sb, b + 1 + FIRST)
                for g in range(HS):
                    for part in (kA, kB):
                        for j in BANK_ORDER:
                            rows = slice(32 * j, 32 * j + 2 * DH)
                            last = nc.tensor.matmul(S_BANKS[j][:, g * S:(g + 1) * S], qT[u][rows, g, :],
                                                    part[u][rows, g, :], start=False, stop=g == HS - 1 and part is kB)
                            if g == HS - 1 and part is kB:
                                last.then_inc(q.s_ps, 1)

            def attend(i, u):
                b = i * 2 + u

                def transpose_p(m):
                    n, j = b * NJ + m, BANK_ORDER[m]
                    pe.wait_ge(q.p_sb, n + 1 + FIRST)
                    pe.wait_ge(q.pt_sb, n - 1 + AHEAD)
                    for g in range(HS):
                        last = nc.tensor.transpose(PT_BANKS[m % 2][:, g * S:(g + 1) * S], P[:, j, g, :], r.ident[:, :])
                    last.then_inc(q.pt_ps, 1)

                def values(m):
                    n, j = b * NJ + m, BANK_ORDER[m]
                    pe.wait_ge(q.pt_sb, n + 1 + AHEAD)
                    for g in range(HS):
                        h = head(j, g)
                        last = nc.tensor.matmul(O[:, h * (DH + 1):(h + 1) * (DH + 1)], pT[m % 2][:, g, :], vs[u][:, h, :],
                                                start=True, stop=True)
                    last.then_inc(q.pv_ps, 1)

                transpose_p(0)
                if layer == 0:
                    pe.wait_ge(q.v_in[u], i * 16 + 16)
                pe.wait_ge(q.p_sb, b * NJ + NJ + FIRST)
                for m in range(1, NJ):
                    transpose_p(m)
                    values(m - 1)
                values(NJ - 1)

            def project_out(i, u):
                b = i * 2 + u
                pe.wait_ge(q.o_sb, b + 1 + FIRST)
                pe.wait_ge(q.y_sb, b + FIRST)
                for k in range(KD):
                    last = nc.tensor.transpose(KV[:, k * S:(k + 1) * S],
                                               osb[u][:, :, :].rearrange("p h e -> p (h e)")[:, k * 128:(k + 1) * 128],
                                               r.ident[:, :])
                last.then_inc(q.ot_ps, 1)
                pe.wait_ge(q.ot_sb, b + 1)
                for k in range(KD):
                    last = nc.tensor.matmul(KV[:, D:2 * D], oT[u][:, k, :], wo[:, k, :], start=k == 0, stop=k == KD - 1)
                last.then_inc(q.y_ps, 1)

            def turn(i, last_turn):
                for u in range(2):
                    last_batch = last_turn and u == 1
                    scores(i, u)
                    if not last_batch:
                        project(i + u, 1 - u)
                    attend(i, u)
                    if layer == 1:
                        project_out(i, u)

            project(0, 0)
            with pe.Fori(0, B // 2 - 1) as i:
                turn(i, False)
            turn(B // 2 - 1, True)

        @block.scalar
        def _(act):
            for s in (q.pt_ps, q.pt_sb, q.pv_ps):
                act.sem_inc(s, AHEAD)
            for s in (q.mask_sb, q.kv_ps, q.o_sb, q.qk_sb, q.y_sb, q.p_sb, q.q_sb):
                act.sem_inc(s, FIRST)
            for s in (*q.v_out, *q.o_out):
                act.sem_inc(s, FIRST_DMA)

            def high_parts(i, u):
                b = i * 2 + u
                act.wait_ge(q.q_ps, b + 1)
                act.wait_ge(q.q_sb, b + FIRST)
                nc.scalar.copy(qhi[:, :, :].rearrange("p g s -> p (g s)"), KV[:, :]).then_inc(q.q_hi_sb, 1)
                act.wait_ge(q.k_ps, b + 1)
                nc.scalar.copy(kA[u][:, :, :].rearrange("p g s -> p (g s)"), KV[:, :]).then_inc(q.k_hi_sb, 1)

            def turn(i, last_turn):
                for u in range(2):
                    b = i * 2 + u
                    for m, j in enumerate(BANK_ORDER):
                        n = b * NJ + m
                        act.wait_ge(q.max_sb, n + 1)
                        act.wait_ge(q.pt_ps, n - NJ + 1 + AHEAD)
                        for g in range(HS):
                            last = nc.scalar.activation(P[:, j, g, :], S_BANKS[j][:, g * S:(g + 1) * S], ACT.Exp,
                                                        bias=negmax[u][:, j, g:g + 1])
                        last.then_inc(q.p_sb, 1)
                    if layer == 1 and not (last_turn and u == 1):
                        high_parts(i + u, 1 - u)
                    for m, j in enumerate(BANK_ORDER):
                        n = b * NJ + m
                        act.wait_ge(q.pt_ps, n + 1 + AHEAD)
                        act.wait_ge(q.pv_ps, n - 1 + AHEAD)
                        nc.scalar.copy(pT[m % 2][:, :, :].rearrange("p g s -> p (g s)"), PT_BANKS[m % 2][:, :]
                                       ).then_inc(q.pt_sb, 1)

            if layer == 1:
                high_parts(0, 0)
            with act.Fori(0, B // 2 - 1) as i:
                turn(i, False)
            turn(B // 2 - 1, True)

        @block.vector
        def _(dve):
            if layer == 0:
                dve.wait_ge(q.w_in, 16 * 6)
                dve.wait_ge(q.causal_made, 1)
                ch = Chain(dve, q.chain)
                nc.vector.tensor_scalar(bq[:, :], bq[:, :], DH ** 0.5, None, ALU.mult)
                ch.link(nc.vector.tensor_scalar(wq[:, :, :], wq[:, :, :], DH ** 0.5, None, ALU.mult))
                dve.sem_inc(q.w_made, 1)
            else:
                ch = Chain(dve, q.chain)
            dve.wait_ge(q.zeroed, 3)
            ch.link(nc.vector.tensor_reduce(low_rows[:, :], low_cols[:, :, :].rearrange("p j e -> p (j e)"), AX_X,
                                            ALU.add, negate=True))
            setup = ch.n

            def prepare_early(i, u, ch):
                b = i * 2 + u
                dve.wait_ge(mask_in[u], i * 16 + 16)
                if layer == 0:
                    nc.vector.scalar_tensor_tensor(out=mask[u][:, :], in0=padmask[u][:, :], scalar=MASKED,
                                                   in1=causal[:, :], op0=ALU.mult, op1=ALU.add).then_inc(q.mask_sb, 1)
                else:
                    nc.vector.tensor_scalar(mask[u][:, :], imask[u][:, :], 0.0, MASKED, ALU.is_equal, ALU.mult
                                            ).then_inc(q.mask_sb, 1)
                nc.vector.tensor_scalar(xb[u][:, :], r.X[:, bass.ds(b, 1), :].rearrange("p o d -> p (o d)"),
                                        r.mv[:, bass.ds(b, 1), 0:1].rearrange("p o s -> p (o s)"),
                                        r.rstd[:, bass.ds(b, 1)], ALU.subtract, ALU.mult).then_inc(q.xb_sb, 1)

            def strips(t):
                return t[:, :, :].rearrange("p g s -> p (g s)").rearrange("p (s c) -> p c s", c=H)

            def padded(t):
                return t[:, :, :, :].rearrange("p c o e -> p c (o e)")

            def prepare(i, u, ch):
                b = i * 2 + u
                dve.wait_ge(q.xt_ps, b + 1)
                nc.vector.tensor_copy(xT[u][:, :, :].rearrange("p k s -> p (k s)"), XQ[:, 0:D]).then_inc(q.xt_sb, 1)
                if layer == 0:
                    def twice(t):
                        return t.rearrange("p (c o e) -> p c o e", o=1, e=DH).broadcast_to((128, H, 2, DH))

                    dve.wait_ge(q.kv_ps, b + 1 + FIRST)
                    ch.link(nc.vector.tensor_tensor(k_tok[:, :, :, :], twice(KV[:, 0:D]), twice(bkv[:, 0:D]), ALU.add))
                    nc.vector.transpose(strips(k_strips), padded(k_tok)).then_inc(q.k_tok_sb, 1)
                    dve.wait_ge(q.v_out[u], i * 16 + FIRST_DMA)
                    nc.vector.tensor_tensor(vtok[u][:, :, 0:DH], KV[:, D:2 * D].rearrange("p (h e) -> p h e", h=H),
                                            bkv[:, D:2 * D].rearrange("p (h e) -> p h e", h=H), ALU.add).then_inc(q.v_sb, 1)
                    dve.wait_ge(q.q_ps, b + 1)
                    ch.link(nc.vector.tensor_tensor(q_tok[:, :, :, :], twice(XQ[:, D:2 * D]), twice(bq[:, :]), ALU.add))
                    nc.vector.transpose(strips(q_strips), padded(q_tok)).then_inc(q.q_tok_sb, 1)
                    dve.wait_ge(q.k_hi_sb, b + 1)
                    nc.vector.tensor_tensor(kB[u][:, :, :].rearrange("p g s -> p (g s)"),
                                            k_strips[:, :, :].rearrange("p g s -> p (g s)"),
                                            kA[u][:, :, :].rearrange("p g s -> p (g s)").bitcast(F32), ALU.subtract)
                    dve.wait_ge(q.q_hi_sb, b + 1)
                    nc.vector.scalar_tensor_tensor(out=qT[u][:, :, :].rearrange("p g s -> p (g s)"),
                                                   in0=qhi[:, :, :].rearrange("p g s -> p (g s)").bitcast(F32),
                                                   scalar=low_rows[:, 0:1],
                                                   in1=q_strips[:, :, :].rearrange("p g s -> p (g s)"),
                                                   op0=ALU.mult, op1=ALU.add).then_inc(q.qk_sb, 1)
                else:
                    dve.wait_ge(q.kv_ps, b + 1 + FIRST)
                    nc.vector.tensor_copy(vtok[u][:, :, 0:DH], XQ[:, D:2 * D].rearrange("p (h e) -> p h e", h=H))
                    dve.wait_ge(q.q_hi_sb, b + 1)
                    nc.vector.scalar_tensor_tensor(out=qT[u][:, :, :].rearrange("p g s -> p (g s)"),
                                                   in0=qhi[:, :, :].rearrange("p g s -> p (g s)").bitcast(F32),
                                                   scalar=low_rows[:, 0:1], in1=KV[:, :], op0=ALU.mult, op1=ALU.add
                                                   ).then_inc(q.q_sb, 1)
                    dve.wait_ge(q.k_hi_sb, b + 1)
                    nc.vector.tensor_tensor(kB[u][:, :, :].rearrange("p g s -> p (g s)"), KV[:, :],
                                            kA[u][:, :, :].rearrange("p g s -> p (g s)").bitcast(F32), ALU.subtract
                                            ).then_inc(q.qk_sb, 1)

            def maxima(i, u, ch):
                b = i * 2 + u
                for m, j in enumerate(BANK_ORDER):
                    dve.wait_ge(q.s_ps, b * NJ + m + 1)
                    nc.vector.tensor_reduce(negmax[u][:, j, :], S_BANKS[j][:, :].rearrange("p (g s) -> p g s", g=HS),
                                            AX_X, ALU.max, negate=True).then_inc(q.max_sb, 1)

            def output(i, u, ch):
                b = i * 2 + u
                dve.wait_ge(q.pv_ps, b * NJ + NJ + AHEAD)
                sums = O[:, 0:H * (DH + 1)].rearrange("p (h e) -> p h e", h=H)
                ch.link(nc.vector.reciprocal(rinv[u][:, :], sums[:, :, DH]))
                if layer == 0:
                    dve.wait_ge(q.o_out[u], i * 16 + FIRST_DMA)
                nc.vector.tensor_tensor(osb[u][:, :, :], sums[:, :, 0:DH],
                                        rinv[u][:, :].rearrange("p (h o) -> p h o", o=1).broadcast_to((128, H, DH)),
                                        ALU.mult).then_inc(q.o_sb, 1)

            def take_out(i, u, ch):
                b = i * 2 + u
                dve.wait_ge(q.ot_ps, b + 1)
                nc.vector.tensor_copy(oT[u][:, :, :].rearrange("p k s -> p (k s)"), KV[:, 0:D]).then_inc(q.ot_sb, 1)
                dve.wait_ge(q.y_ps, b + 1)
                nc.vector.tensor_tensor(proj[u][:, :], KV[:, D:2 * D], bo[:, :], ALU.add).then_inc(q.y_sb, 1)
                dve.wait_ge(q.y_sb, b + 1 + FIRST)
                xrow = r.X[:, bass.ds(b, 1), :].rearrange("p o d -> p (o d)")
                nc.vector.scalar_tensor_tensor(out=xrow, in0=proj[u][:, :], scalar=r.gates[:, 1:2], in1=xrow,
                                               op0=ALU.mult, op1=ALU.add)

            per_batch = 3 if layer == 0 else 1

            def turn(i, last_turn):
                for u in range(2):
                    ch = Chain(dve, q.chain, (i * 2 + u) * per_batch + setup + prepared)
                    more = not (last_turn and u == 1)
                    if more:
                        prepare_early(i + u, 1 - u, ch)
                    maxima(i, u, ch)
                    if more:
                        prepare(i + u, 1 - u, ch)
                    output(i, u, ch)
                    if layer == 1:
                        take_out(i, u, ch)
                    assert last_turn or ch.n == per_batch

            ch = Chain(dve, q.chain, setup)
            prepare_early(0, 0, ch)
            prepare(0, 0, ch)
            prepared = ch.n
            with dve.Fori(0, B // 2 - 1) as i:
                turn(i, False)
            turn(B // 2 - 1, True)
            if layer == 0:
                dve.wait_ge(q.o_sb, B + FIRST)


E0, F0, CAP, RH = 16, 512, 64, 128
KF0 = F0 // 128
TIE = 2.0 ** -100


def router0_phase(nc, r, a, R, W, xn_hi, xn_lo):
    NB, NT = 4, B // 4
    with ExitStack() as ctx:
        def sb(name, shape, dt=F32):
            return ctx.enter_context(nc.sbuf_tensor("r0_" + name, shape, dt))

        def sem(name):
            return ctx.enter_context(nc.semaphore("r0_" + name))

        w1 = sb("w1", [128, KD, RH])
        w2 = sb("w2", [RH, E0])
        tie = sb("tie", [128, S])
        ones = sb("ones", [128, 128])
        xb = sb("xb", [128, NB, D])
        xT = sb("xT", [128, KD, NB * S])
        hid = sb("hid", [RH, NB * S])
        negmax = sb("negmax", [E0, NB])
        ex = sb("ex", [E0, NB, S])
        sums = sb("sums", [E0, NB])
        rs = sb("rs", [E0, NB])
        probs = sb("probs", [E0, NB, S])
        row = sb("row", [128, E0, NB * S])
        col = sb("col", [128, NB, E0])
        taken = sb("taken", [128, NB, E0])
        total = sb("total", [128, NB, E0])
        inv = sb("inv", [128, NB, E0])
        p_dram = nc.dram_tensor("r0_p_dram", (NT * E0 * NB * S,), F32, kind="Internal").ap()
        (w_in, consts, xb_sb, xt_ps, xt_sb, h_ps, h_sb, l_ps, max_sb, ex_sb, probs_sb, p_out, row_in, col_ps, taken_sb,
         total_ps, chain, hi_sb, split_sb) = (sem(n) for n in (
             "w_in", "consts", "xb_sb", "xt_ps", "xt_sb", "h_ps", "h_sb", "l_ps", "max_sb", "ex_sb", "probs_sb",
             "p_out", "row_in", "col_ps", "taken_sb", "total_ps", "dve_chain", "hi_sb", "split_sb"))
        banks = r.banks
        block = ctx.enter_context(nc.Block())

        @block.sync
        def _(sp):
            sp.dma_start(w1[:, :, :], a["L0_ffn_router_w1"].rearrange("(k p) n -> p k n", p=128)).then_inc(w_in, 16)
            sp.dma_start(w2[:, :], a["L0_ffn_router_w2"]).then_inc(w_in, 16)
            with sp.Fori(0, NT) as i:
                sp.wait_ge(probs_sb, i + 1)
                sp.sem_inc(r.held, 1)
                pd = p_dram[bass.ds(i * (E0 * NB * S), E0 * NB * S)]
                sp.dma_start(pd.rearrange("(e n) -> e n", e=E0), probs[:, :, :].rearrange("e b s -> e (b s)")
                             ).then_inc(p_out, 16)
                sp.wait_ge(p_out, i * 16 + 16)
                sp.sem_inc(r.held, 1)
                sp.dma_start(row[:, :, :].rearrange("p e n -> p (e n)"), pd.partition_broadcast(128)).then_inc(row_in, 16)

        @block.gpsimd
        def _(pool):
            nc.gpsimd.memset(tie[:, :], -TIE).then_inc(consts, 1)
            nc.gpsimd.memset(ones[:, :], 1.0).then_inc(consts, 1)
            nc.gpsimd.memset(R[:, :, :], 0.0).then_inc(consts, 1)
            nc.gpsimd.memset(W[:, :, :], 0.0).then_inc(consts, 1)
            pool.wait_ge(consts, 4)
            nc.gpsimd.affine_select(out=tie[:, :], in_=tie[:, :], compare_op=ALU.is_gt, fill=0.0, base=0,
                                    pattern=[[-1, S]], channel_multiplier=1).then_inc(consts, 1)
            with pool.Fori(0, NT) as i:
                turn = bass.ds(i * NB, NB)
                pool.wait_ge(xb_sb, i + 1)
                pool.sem_inc(r.held, 1)
                nc.gpsimd.tensor_copy(xn_hi[:, turn, :], xb[:, :, :]).then_inc(hi_sb, 1)
                pool.wait_ge(hi_sb, i + 1)
                nc.gpsimd.tensor_tensor(xn_lo[:, turn, :], xb[:, :, :], xn_hi[:, turn, :].bitcast(F32), ALU.subtract
                                        ).then_inc(split_sb, 1)

        @block.tensor
        def _(pe):
            pe.wait_ge(w_in, 32)
            pe.wait_ge(consts, 5)
            with pe.Fori(0, NT) as i:
                pe.wait_ge(xb_sb, i + 1)
                for k in range(KD):
                    for n in range(NB):
                        last = nc.tensor.transpose(banks[k][:, n * S:(n + 1) * S], xb[:, n, k * 128:(k + 1) * 128],
                                                   r.ident[:, :])
                last.then_inc(xt_ps, 1)
                pe.wait_ge(xt_sb, i + 1)
                for k in range(KD):
                    last = nc.tensor.matmul(banks[2][:, :], w1[:, k, :], xT[:, k, :], start=k == 0, stop=k == KD - 1)
                last.then_inc(h_ps, 1)
                pe.wait_ge(h_sb, i + 1)
                nc.tensor.matmul(banks[3][0:E0, :], w2[:, :], hid[:, :], start=True, stop=True).then_inc(l_ps, 1)
                pe.wait_ge(probs_sb, i + 1)
                pe.sem_inc(r.held, 1)
                for n in range(NB):
                    last = nc.tensor.transpose(banks[4][:, n * E0:(n + 1) * E0], probs[:, n, :], r.ident[0:E0, 0:E0])
                last.then_inc(col_ps, 1)
                pe.wait_ge(taken_sb, i + 1)
                nc.tensor.matmul(banks[5][:, 0:NB * E0], ones[:, :], taken[:, :, :].rearrange("p b e -> p (b e)"),
                                 start=True, stop=True).then_inc(total_ps, 1)

        @block.scalar
        def _(act):
            with act.Fori(0, NT) as i:
                act.wait_ge(h_ps, i + 1)
                nc.scalar.activation(hid[:, :], banks[2][:, :], ACT.Silu).then_inc(h_sb, 1)
                act.wait_ge(max_sb, i + 1)
                for n in range(NB):
                    last = nc.scalar.activation(ex[:, n, :], banks[3][0:E0, n * S:(n + 1) * S], ACT.Exp,
                                                bias=negmax[:, n:n + 1], accum_out=sums[:, n:n + 1])
                last.then_inc(ex_sb, 1)

        PER_TURN = 5

        @block.vector
        def _(dve):
            dve.wait_ge(consts, 5)
            dve.sem_inc(split_sb, 1)
            with dve.Fori(0, NT) as i:
                ch = Chain(dve, chain, i * PER_TURN)
                dve.wait_ge(split_sb, i + 1)
                for n in range(NB):
                    b = i * NB + n
                    last = nc.vector.tensor_scalar(xb[:, n, :], r.X[:, bass.ds(b, 1), :].rearrange("p o d -> p (o d)"),
                                                   r.mv[:, bass.ds(b, 1), 0:1].rearrange("p o s -> p (o s)"),
                                                   r.rstd[:, bass.ds(b, 1)], ALU.subtract, ALU.mult)
                last.then_inc(xb_sb, 1)
                dve.wait_ge(xt_ps, i + 1)
                for k in range(KD):
                    last = nc.vector.tensor_copy(xT[:, k, :], banks[k][:, :])
                last.then_inc(xt_sb, 1)
                dve.wait_ge(l_ps, i + 1)
                nc.vector.tensor_reduce(negmax[:, :], banks[3][0:E0, :].rearrange("e (b s) -> e b s", b=NB), AX_X,
                                        ALU.max, negate=True).then_inc(max_sb, 1)
                dve.wait_ge(ex_sb, i + 1)
                ch.link(nc.vector.reciprocal(rs[:, :], sums[:, :]))
                nc.vector.tensor_tensor(probs[:, :, :], ex[:, :, :], rs[:, :].rearrange("e (b o) -> e b o", o=1)
                                        .broadcast_to((E0, NB, S)), ALU.mult).then_inc(probs_sb, 1)
                dve.wait_ge(col_ps, i + 1)
                ch.link(nc.vector.tensor_copy(col[:, :, :].rearrange("p b e -> p (b e)"), banks[4][:, 0:NB * E0]))
                dve.wait_ge(row_in, i * 16 + 16)
                for n in range(NB):
                    for e in range(E0):
                        rank = R[:, bass.ds(i * NB + n, 1), e:e + 1].rearrange("p o s -> p (o s)")
                        last = nc.vector.scalar_tensor_tensor(
                            out=row[:, e, n * S:(n + 1) * S], in0=row[:, e, n * S:(n + 1) * S], scalar=col[:, n, e:e + 1],
                            in1=tie[:, :], op0=ALU.subtract, op1=ALU.is_gt, accum_out=rank)
                ch.link(last)
                nc.vector.scalar_tensor_tensor(out=taken[:, :, :], in0=R[:, bass.ds(i * NB, NB), 0:E0],
                                               scalar=float(CAP), in1=col[:, :, :], op0=ALU.is_lt, op1=ALU.mult
                                               ).then_inc(taken_sb, 1)
                dve.wait_ge(total_ps, i + 1)
                ch.link(nc.vector.tensor_scalar(total[:, :, :].rearrange("p b e -> p (b e)"), banks[5][:, 0:NB * E0],
                                                1e-9, None, ALU.add))
                ch.link(nc.vector.reciprocal(inv[:, :, :], total[:, :, :]))
                nc.vector.tensor_tensor(W[:, bass.ds(i * NB, NB), 0:E0], taken[:, :, :], inv[:, :, :], ALU.mult)
                assert ch.n == PER_TURN


def experts0_phase(nc, r, a, R, W, xn_hi, xn_lo, xs_dram):
    NH, NPAIR, SLOTS = 2, 4, 8 * CAP
    NQ, NF = NH * NPAIR, NH * KF0
    with ExitStack() as ctx:
        def sb(name, shape, dt=F32):
            return ctx.enter_context(nc.sbuf_tensor("e0_" + name, shape, dt))

        def sem(name):
            return ctx.enter_context(nc.semaphore("e0_" + name))

        def parts(name, shape):
            return [sb(f"{name}_{part}", shape, F32R) for part in ("hi", "lo")]

        w_raw = [sb(f"w{n}", [128, KD * F0]) for n in range(3)]
        w_parts = [[parts(f"w{n}_{v}", [128, KD * F0]) for n in range(3)] for v in range(2)]
        slot = sb("slot", [128, 1, CAP])
        pick = sb("pick", [128, B, CAP], F32R)
        pickT = [sb(f"pickT{v}", [128, NQ, S], F32R) for v in range(2)]
        weight = [sb(f"weight{v}", [128, NQ]) for v in range(2)]
        xg = parts("xg", [128, KD, B * CAP])
        sg = [sb(f"sg{n}", [128, SLOTS]) for n in range(2)]
        hid = [sb(f"hid{n}", [128, SLOTS]) for n in range(2)]
        hidden = parts("hidden", [128, NF, SLOTS])
        eo = [parts(f"eo{n}", [128, D]) for n in range(2)]
        zero = sb("zero", [128, D])
        (made, pick_sb, xg_ps, xg_hi, xg_sb, put_ps, putT_sb, g_ps, sg_sb, u_ps, hid_sb, hi_sb, hidden_sb, eo_ps, eo_hi, eo_sb,
         sum_ps, acc_sb, w_in, w_hi, w_sb) = (sem(n) for n in (
             "made", "pick_sb", "xg_ps", "xg_hi", "xg_sb", "put_ps", "putT_sb", "g_ps", "sg_sb", "u_ps", "hid_sb", "hi_sb",
             "hidden_sb", "eo_ps", "eo_hi", "eo_sb", "sum_ps", "acc_sb", "w_in", "w_hi", "w_sb"))
        zero_made, cleared = sem("zero_made"), sem("cleared")
        A_SG, A_HID, A_EO, A_SUM, A_ACC, A_EOPS, A_PUT, A_UP = 1, 1, 2, 2, 1, 2 * NQ, 1, 1
        G_BANK, U_BANK, XK, EO, OUT = r.banks[2], r.banks[3], r.banks[0:2], r.banks[4:6], r.banks[6:8]
        WEIGHTS = G_BANK[:, 0:2 * NQ]
        block = ctx.enter_context(nc.Block())

        @block.sync
        def _(sp):
            def load(e):
                for t, name in zip(w_raw, ("L0_ffn_w1", "L0_ffn_w2", "L0_ffn_w3")):
                    src = a[name][bass.ds(e, 1), :, :].rearrange("o (k p) n -> p (o k) n", p=128)
                    sp.dma_start(t[:, :].rearrange("p (k n) -> p k n", n=src.shape[2]), src).then_inc(w_in, 16)

            load(0)
            with sp.Fori(0, E0 - 1) as e:
                sp.wait_ge(w_sb, e * 3 + 3)
                sp.sem_inc(r.held, 1)
                load(e + 1)

        @block.gpsimd
        def _(pool):
            nc.gpsimd.iota(slot[:, :, :], pattern=[[0, 1], [1, CAP]], base=0, channel_multiplier=0,
                           allow_small_or_imprecise_dtypes=True).then_inc(made, 1)
            nc.gpsimd.memset(zero[:, :], 0.0).then_inc(zero_made, 1)
            pool.wait_ge(zero_made, 1)
            pool.dma_start(xs_dram.rearrange("(t p) d -> p t d", p=TT),
                           zero[:, :].rearrange("p (o d) -> p o d", o=1).broadcast_to((128, TILES, D))).then_inc(cleared, 16)
            with pool.Fori(0, E0 // 2) as i:
                for v in range(2):
                    e = i * 2 + v
                    pool.wait_ge(w_in, e * 48 + 48)
                    pool.wait_ge(eo_ps, (e - 1) * NQ + A_EOPS)
                    pool.sem_inc(r.held, 1)
                    for n in range(3):
                        nc.gpsimd.tensor_copy(w_parts[v][n][0][:, :], w_raw[n][:, :]).then_inc(w_hi, 1)
                    for n in range(3):
                        pool.wait_ge(w_hi, e * 3 + n + 1)
                        nc.gpsimd.tensor_tensor(w_parts[v][n][1][:, :], w_raw[n][:, :], w_parts[v][n][0][:, :].bitcast(F32),
                                                ALU.subtract).then_inc(w_sb, 1)
            pool.wait_ge(cleared, 16)

        @block.tensor
        def _(pe):
            def gather(e, h):
                if h == 0:
                    pe.wait_ge(pick_sb, e + 1)
                    pe.wait_ge(putT_sb, e * 4 + A_PUT)
                else:
                    pe.wait_ge(xg_sb, e * 4 + 2)
                for k in range(KD):
                    for n in range(B // NH):
                        b = h * (B // NH) + n
                        for part in (xn_hi, xn_lo):
                            last = nc.tensor.matmul(XK[k][:, n * CAP:(n + 1) * CAP], part[:, b, k * 128:(k + 1) * 128],
                                                    pick[:, b, :], start=part is xn_hi, stop=part is xn_lo)
                last.then_inc(xg_ps, 1)

            def turn_over(e):
                pe.wait_ge(xg_sb, e * 4 + 4)
                pe.wait_ge(sg_sb, e * NF + A_SG)
                for q in range(NQ):
                    pair = pick[:, 2 * q:2 * q + 2, :].rearrange("p b c -> p (b c)").bitcast(F32)
                    nc.tensor.matmul(WEIGHTS[:, 2 * q:2 * q + 2], pair,
                                     W[:, 2 * q:2 * q + 2, bass.ds(e, 1)].rearrange("p b o -> p (b o)"),
                                     start=True, stop=True)
                for q in range(NQ):
                    pair = pick[:, 2 * q:2 * q + 2, :].rearrange("p b c -> p (b c)").bitcast(F32)
                    last = nc.tensor.transpose(XK[q // 4][:, (q % 4) * S:(q % 4 + 1) * S], pair, r.ident[:, :])
                last.then_inc(put_ps, 1)

            def up(e, v, h):
                for f in range(KF0):
                    n = e * NF + h * KF0 + f
                    for m, (free, bank, full) in enumerate(((sg_sb, G_BANK, g_ps), (hid_sb, U_BANK, u_ps))):
                        pe.wait_ge(free, n + A_SG)
                        hi, lo = w_parts[v][m]
                        terms = [(w, x, k) for w, x in ((hi, xg[0]), (lo, xg[0]), (hi, xg[1])) for k in range(KD)]
                        for w, x, k in terms:
                            last = nc.tensor.matmul(bank[:, :], w[:, k * F0 + f * 128:k * F0 + (f + 1) * 128],
                                                    x[:, k, h * SLOTS:(h + 1) * SLOTS],
                                                    start=(w, x, k) == terms[0], stop=(w, x, k) == terms[-1])
                        last.then_inc(full, 1)

            def down(e, v, q):
                h, p = q // NPAIR, q % NPAIR
                n = e * NQ + q
                if p == 0:
                    pe.wait_ge(hidden_sb, e * NF + (h + 1) * KF0)
                pe.wait_ge(eo_sb, n - 1 + A_EO)
                hi, lo = w_parts[v][2]
                terms = [(x, w, f) for x, w in ((hidden[0], hi), (hidden[1], hi), (hidden[0], lo)) for f in range(KF0)]
                for x, w, f in terms:
                    last = nc.tensor.matmul(EO[q % 2][:, 0:D], x[:, h * KF0 + f, p * 128:(p + 1) * 128],
                                            w[:, f * D:(f + 1) * D],
                                            start=(x, w, f) == terms[0], stop=(x, w, f) == terms[-1])
                last.then_inc(eo_ps, 1)

            def scatter(e, v, q):
                n = e * NQ + q
                pe.wait_ge(eo_sb, n + 1 + A_EO)
                pe.wait_ge(acc_sb, n + A_ACC)
                for t in range(2):
                    rows = slice(t * CAP, (t + 1) * CAP)
                    for part in eo[q % 2]:
                        last = nc.tensor.matmul(OUT[t][:, 0:D], pickT[v][rows, q, :], part[rows, :],
                                                start=part is eo[q % 2][0], stop=part is eo[q % 2][1])
                last.then_inc(sum_ps, 1)

            def turn(i, last_turn):
                for v in range(2):
                    e = i * 2 + v
                    more = not (last_turn and v == 1)
                    pe.wait_ge(w_sb, e * 3 + 3)
                    pe.wait_ge(xg_sb, e * 4 + 4)
                    pe.wait_ge(putT_sb, e * 4 + 4 + A_PUT)
                    for h in range(NH):
                        up(e, v, h)
                    for q in range(NQ):
                        if more and q in (0, 2):
                            gather(e + 1, q // 2)
                        if more and q == 4:
                            turn_over(e + 1)
                        down(e, v, q)
                        if q > 0:
                            scatter(e, v, q - 1)
                    scatter(e, v, NQ - 1)

            pe.wait_ge(made, 1)
            pe.sem_inc(putT_sb, A_PUT)
            gather(0, 0)
            gather(0, 1)
            turn_over(0)
            with pe.Fori(0, E0 // 2 - 1) as i:
                turn(i, False)
            turn(E0 // 2 - 1, True)

        @block.scalar
        def _(act):
            for s, ahead in ((sg_sb, A_SG), (eo_sb, A_EO), (hid_sb, A_HID), (sum_ps, A_SUM), (acc_sb, A_ACC),
                             (eo_ps, A_EOPS)):
                act.sem_inc(s, ahead)

            def take_tokens(e, h):
                act.wait_ge(xg_ps, e * 2 + h + 1)
                for k in range(KD):
                    nc.scalar.copy(xg[0][:, k, h * SLOTS:(h + 1) * SLOTS], XK[k][:, :]).then_inc(xg_hi, 1)

            def take_one_hots(e, v):
                act.wait_ge(put_ps, e + 1)
                nc.scalar.copy(pickT[v][:, 0:4, :].rearrange("p q s -> p (q s)"), XK[0][:, :]).then_inc(putT_sb, 1)

            def turn(i, last_turn):
                for v in range(2):
                    e = i * 2 + v
                    more = not (last_turn and v == 1)
                    for f in range(NF):
                        n = e * NF + f
                        act.wait_ge(g_ps, n + 1)
                        nc.scalar.activation(sg[f % 2][:, :], G_BANK[:, :], ACT.Silu).then_inc(sg_sb, 1)
                        act.wait_ge(hid_sb, n + 1 + A_HID)
                        nc.scalar.copy(hidden[0][:, f, :], hid[f % 2][:, :]).then_inc(hi_sb, 1)
                    for q in range(NQ):
                        if more and q in (0, 2):
                            take_tokens(e + 1, q // 2)
                        if more and q == 4:
                            take_one_hots(e + 1, 1 - v)
                        n = e * NQ + q
                        act.wait_ge(eo_ps, n + 1 + A_EOPS)
                        act.wait_ge(sum_ps, n - 1 + A_SUM)
                        nc.scalar.activation(eo[q % 2][0][:, :], EO[q % 2][:, 0:D], ACT.Copy, scale=weight[v][:, q:q + 1]
                                             ).then_inc(eo_hi, 1)

            take_tokens(0, 0)
            take_tokens(0, 1)
            take_one_hots(0, 0)
            with act.Fori(0, E0 // 2 - 1) as i:
                turn(i, False)
            turn(E0 // 2 - 1, True)

        @block.vector
        def _(dve):
            dve.wait_ge(made, 1)

            def one_hots(e):
                rank = R[:, :, bass.ds(e, 1)].broadcast_to((128, B, CAP))
                nc.vector.tensor_tensor(pick[:, :, :], slot[:, :, :].broadcast_to((128, B, CAP)), rank, ALU.is_equal
                                        ).then_inc(pick_sb, 1)

            def take_tokens(e, h):
                for k in range(KD):
                    dve.wait_ge(xg_hi, e * 4 + h * 2 + k + 1)
                    part = slice(h * SLOTS, (h + 1) * SLOTS)
                    nc.vector.tensor_tensor(xg[1][:, k, part], XK[k][:, :], xg[0][:, k, part].bitcast(F32), ALU.subtract
                                            ).then_inc(xg_sb, 1)

            def take_one_hots(e, v):
                dve.wait_ge(put_ps, e + 1)
                nc.vector.tensor_copy(pickT[v][:, 4:8, :].rearrange("p q s -> p (q s)"), XK[1][:, :]).then_inc(putT_sb, 1)
                for t in range(2):
                    rows = slice(t * CAP, (t + 1) * CAP)
                    nc.vector.tensor_copy(weight[v][rows, :], WEIGHTS[rows, :].rearrange("p (q t) -> p q t", t=2)[:, :, t]
                                          ).then_inc(putT_sb, 1)

            def add(e, q):
                dve.wait_ge(sum_ps, e * NQ + q + 1 + A_SUM)
                for t in range(2):
                    b = 2 * q + t
                    last = nc.vector.scalar_tensor_tensor(out=r.X[:, b, :], in0=OUT[t][:, 0:D], scalar=r.gates[:, 2:3],
                                                          in1=r.X[:, b, :], op0=ALU.mult, op1=ALU.add)
                last.then_inc(acc_sb, 1)

            def turn(i, last_turn):
                for v in range(2):
                    e = i * 2 + v
                    more = not (last_turn and v == 1)
                    if more:
                        one_hots(e + 1)
                    for f in range(NF):
                        n = e * NF + f
                        dve.wait_ge(u_ps, n + 1)
                        dve.wait_ge(sg_sb, n + 1 + A_SG)
                        nc.vector.tensor_tensor(hid[f % 2][:, :], sg[f % 2][:, :], U_BANK[:, :], ALU.mult
                                                ).then_inc(hid_sb, 1)
                        dve.wait_ge(hi_sb, n + 1)
                        nc.vector.tensor_tensor(hidden[1][:, f, :], hid[f % 2][:, :], hidden[0][:, f, :].bitcast(F32),
                                                ALU.subtract).then_inc(hidden_sb, 1)
                    for q in range(NQ):
                        if more and q in (0, 2):
                            take_tokens(e + 1, q // 2)
                        if more and q == 4:
                            take_one_hots(e + 1, 1 - v)
                        n = e * NQ + q
                        dve.wait_ge(eo_hi, n + 1)
                        nc.vector.scalar_tensor_tensor(out=eo[q % 2][1][:, :], in0=EO[q % 2][:, 0:D],
                                                       scalar=weight[v][:, q:q + 1], in1=eo[q % 2][0][:, :].bitcast(F32),
                                                       op0=ALU.mult, op1=ALU.subtract).then_inc(eo_sb, 1)
                        if q > 0:
                            add(e, q - 1)
                    add(e, NQ - 1)
                    dve.wait_ge(acc_sb, (e + 1) * NQ + A_ACC)

            one_hots(0)
            take_tokens(0, 0)
            take_tokens(0, 1)
            take_one_hots(0, 0)
            with dve.Fori(0, E0 // 2 - 1) as i:
                turn(i, False)
            turn(E0 // 2 - 1, True)


E1, F1, TOPK, FS = 32, 192, 4, 512
FH = F1 // 2
KFS = FS // 128
TT = 128
TILES = -(-((B * S * TOPK + E1 * (TT - 1)) // TT) // 4) * 4


def router1_phase(nc, r, a, LG, SH):
    NB, NT = 4, B // 4
    with ExitStack() as ctx:
        def sb(name, shape, dt=F32):
            return ctx.enter_context(nc.sbuf_tensor("r1_" + name, shape, dt))

        def sem(name):
            return ctx.enter_context(nc.semaphore("r1_" + name))

        wr = sb("wr", [128, KD, E1 + 1])
        wg = sb("wg", [128, KD, FS])
        wu = sb("wu", [128, KD, FS])
        wd = sb("wd", [128, KFS, D])
        xb = sb("xb", [128, NB, D])
        xT = sb("xT", [128, KD, NB * S])
        sg = [sb(f"sg{n}", [128, NB * S]) for n in range(2)]
        hidden = sb("hidden", [128, KFS, NB * S])
        names = ("w_in", "xb_sb", "xt_ps", "xt_sb", "l_ps", "l_sb", "g_ps", "sg_sb", "u_ps", "hid_sb", "y_ps", "y_sb")
        w_in, xb_sb, xt_ps, xt_sb, l_ps, l_sb, g_ps, sg_sb, u_ps, hid_sb, y_ps, y_sb = (sem(n) for n in names)
        A_SG, A_HID, A_Y, A_XT, A_L = 1, 2, 2, 1, 1
        XK, LOG, G_BANK, U_BANK, Y = r.banks[0:2], r.banks[2], r.banks[3], r.banks[4], r.banks[5:7]
        block = ctx.enter_context(nc.Block())

        @block.sync
        def _(sp):
            def load(dst, name):
                sp.dma_start(dst, a[name].rearrange("(k p) n -> p k n", p=128)).then_inc(w_in, 16)

            load(wr[:, :, :], "L1_router_and_gate_w")
            load(wg[:, :, :], "L1_ffn_sh_gate")
            load(wu[:, :, :], "L1_ffn_sh_up")
            load(wd[:, :, :], "L1_ffn_sh_down")

        @block.tensor
        def _(pe):
            pe.wait_ge(w_in, 16 * 4)
            with pe.Fori(0, NT) as i:
                pe.wait_ge(xb_sb, i + 1)
                for k in range(KD):
                    for n in range(NB):
                        last = nc.tensor.transpose(XK[k][:, n * S:(n + 1) * S], xb[:, n, k * 128:(k + 1) * 128], r.ident[:, :])
                last.then_inc(xt_ps, 1)
                pe.wait_ge(xt_sb, i + 1 + A_XT)
                pe.wait_ge(l_sb, i + A_L)
                for n in range(NB):
                    for k in range(KD):
                        last = nc.tensor.matmul(LOG[:, n * (E1 + 1):(n + 1) * (E1 + 1)], xT[:, k, n * S:(n + 1) * S],
                                                wr[:, k, :], start=k == 0, stop=k == KD - 1)
                last.then_inc(l_ps, 1)
                for f in range(KFS):
                    m = i * KFS + f
                    pe.wait_ge(sg_sb, m + A_SG)
                    for k in range(KD):
                        last = nc.tensor.matmul(G_BANK[:, :], wg[:, k, f * 128:(f + 1) * 128], xT[:, k, :],
                                                start=k == 0, stop=k == KD - 1)
                    last.then_inc(g_ps, 1)
                    pe.wait_ge(hid_sb, m + A_HID)
                    for k in range(KD):
                        last = nc.tensor.matmul(U_BANK[:, :], wu[:, k, f * 128:(f + 1) * 128], xT[:, k, :],
                                                start=k == 0, stop=k == KD - 1)
                    last.then_inc(u_ps, 1)
                pe.wait_ge(hid_sb, i * KFS + KFS + A_HID)
                for n in range(NB):
                    pe.wait_ge(y_sb, i * NB + n - 1 + A_Y)
                    for f in range(KFS):
                        last = nc.tensor.matmul(Y[n % 2][:, 0:D], hidden[:, f, n * S:(n + 1) * S], wd[:, f, :],
                                                start=f == 0, stop=f == KFS - 1)
                    last.then_inc(y_ps, 1)

        @block.scalar
        def _(act):
            for s, ahead in ((sg_sb, A_SG), (hid_sb, A_HID), (y_sb, A_Y), (xt_sb, A_XT), (l_sb, A_L)):
                act.sem_inc(s, ahead)
            with act.Fori(0, NT) as i:
                for f in range(KFS):
                    m = i * KFS + f
                    act.wait_ge(g_ps, m + 1)
                    act.wait_ge(hid_sb, m - 1 + A_HID)
                    nc.scalar.activation(sg[f % 2][:, :], G_BANK[:, :], ACT.Silu).then_inc(sg_sb, 1)
                for n in range(NB):
                    act.wait_ge(y_ps, i * NB + n + 1)
                    nc.scalar.copy(SH[:, bass.ds(i * NB + n, 1), :].rearrange("p o d -> p (o d)"), Y[n % 2][:, 0:D]
                                   ).then_inc(y_sb, 1)

        @block.vector
        def _(dve):
            with dve.Fori(0, NT) as i:
                for n in range(NB):
                    b = i * NB + n
                    last = nc.vector.tensor_scalar(xb[:, n, :], r.X[:, bass.ds(b, 1), :].rearrange("p o d -> p (o d)"),
                                                   r.mv[:, bass.ds(b, 1), 0:1].rearrange("p o s -> p (o s)"),
                                                   r.rstd[:, bass.ds(b, 1)], ALU.subtract, ALU.mult)
                last.then_inc(xb_sb, 1)
                dve.wait_ge(xt_ps, i + 1)
                for k in range(KD):
                    last = nc.vector.tensor_copy(xT[:, k, :], XK[k][:, :])
                last.then_inc(xt_sb, 1)
                nc.vector.tensor_copy(r.XN[:, bass.ds(i * NB, NB), :], xb[:, :, :])
                dve.wait_ge(l_ps, i + 1)
                nc.vector.tensor_copy(LG[:, bass.ds(i * NB, NB), :],
                                      LOG[:, 0:NB * (E1 + 1)].rearrange("p (b e) -> p b e", b=NB)).then_inc(l_sb, 1)
                for f in range(KFS):
                    m = i * KFS + f
                    dve.wait_ge(u_ps, m + 1)
                    dve.wait_ge(sg_sb, m + 1 + A_SG)
                    nc.vector.tensor_tensor(hidden[:, f, :], sg[f % 2][:, :], U_BANK[:, :], ALU.mult).then_inc(hid_sb, 1)


def dispatch1_phase(nc, r, LG, w4, slots, sig, tile_expert, xs_dram):
    with ExitStack() as ctx:
        def sb(name, shape, dt=F32):
            return ctx.enter_context(nc.sbuf_tensor("d1_" + name, shape, dt))

        def sem(name):
            return ctx.enter_context(nc.semaphore("d1_" + name))

        negmax = sb("negmax", [128, B])
        ex = sb("ex", [128, B, E1])
        sums = sb("sums", [128, B])
        rs = sb("rs", [128, B])
        probs = sb("probs", [128, B, E1])
        ez = sb("ez", [128, B])
        ez1 = sb("ez1", [128, B])
        top = sb("top", [128, B, 8])
        top_at = sb("top_at", [128, B, 8], mybir.dt.uint32)
        at = sb("at", [128, B, TOPK])
        s4 = sb("s4", [128, B])
        i4 = sb("i4", [128, B])
        expert = sb("expert", [128, B, E1])
        choice = [sb(f"choice{k}", [128, B, E1]) for k in range(TOPK)]
        member = sb("member", [128, B, E1])
        earlier = sb("earlier", [128, 128])
        ones = sb("ones", [128, 128])
        before = sb("before", [128, B, E1])
        totals = sb("totals", [128, B, E1])
        upto = sb("upto", [128, B + 1, E1])
        edge = sb("edge", [128, E1, B * S // TT])
        over = sb("over", [128, E1, B * S // TT])
        ntiles = sb("ntiles", [128, E1])
        zeros = sb("zeros", [128, E1])
        ends = sb("ends", [128, E1])
        first = sb("first", [128, E1])
        slot = sb("slot", [128, B, E1])
        mine = sb("mine", [128, B, E1])
        slotf = sb("slotf", [128, TOPK, B])
        tile_at = sb("tile_at", [128, 1])
        done = sb("done", [128, E1])
        te = sb("te", [128, 1])
        (made, max_sb, ex_sb, mem_sb, cnt_ps, te_sb, te_ps, slots_sb, sent, chain) = (sem(n) for n in (
            "made", "max_sb", "ex_sb", "mem_sb", "cnt_ps", "te_sb", "te_ps", "slots_sb", "sent", "dve_chain"))
        BEFORE, TOTALS, TE = r.banks[0], r.banks[1], r.banks[2]
        block = ctx.enter_context(nc.Block())

        @block.gpsimd
        def _(pool):
            def iota(t, pattern, multiplier=0):
                nc.gpsimd.iota(t, pattern=pattern, base=0, channel_multiplier=multiplier,
                               allow_small_or_imprecise_dtypes=True).then_inc(made, 1)

            iota(expert[:, :, :], [[0, B], [1, E1]])
            iota(edge[:, :, :], [[0, E1], [TT, B * S // TT]])
            iota(tile_at[:, :], [[0, 1]], 1)
            nc.gpsimd.memset(ones[:, :], 1.0).then_inc(made, 1)
            nc.gpsimd.memset(earlier[:, :], 1.0).then_inc(made, 1)
            nc.gpsimd.memset(zeros[:, :], 0.0).then_inc(made, 1)
            pool.wait_ge(made, 6)
            nc.gpsimd.affine_select(out=earlier[:, :], in_=earlier[:, :], compare_op=ALU.is_gt, fill=0.0, base=0,
                                    pattern=[[1, 128]], channel_multiplier=-1).then_inc(made, 1)
            pool.wait_ge(slots_sb, 1)
            for b in range(B):
                for k in range(TOPK):
                    nc.gpsimd.indirect_dma_start(
                        out=xs_dram[:, :], out_offset=bass.IndirectOffsetOnAxis(ap=slots[:, b, k:k + 1], axis=0),
                        in_=r.XN[:, b, :], in_offset=None).then_inc(sent, 16)
            pool.wait_ge(sent, 16 * B * TOPK)

        @block.scalar
        def _(act):
            act.wait_ge(max_sb, 1)
            nc.scalar.activation(ex[:, :, :], ex[:, :, :], ACT.Exp)
            nc.scalar.activation(ez[:, :], LG[:, :, E1], ACT.Exp, scale=-1.0).then_inc(ex_sb, 1)

        @block.tensor
        def _(pe):
            pe.wait_ge(made, 7)
            pe.wait_ge(mem_sb, 1)
            m = member[:, :, :].rearrange("p b e -> p (b e)")
            nc.tensor.matmul(BEFORE[:, :], earlier[:, :], m, start=True, stop=True)
            nc.tensor.matmul(TOTALS[:, :], ones[:, :], m, start=True, stop=True).then_inc(cnt_ps, 1)
            pe.wait_ge(te_sb, 1)
            nc.tensor.matmul(TE[0:1, 0:128], te[:, :], r.ident[:, :], start=True, stop=True).then_inc(te_ps, 1)

        @block.vector
        def _(dve):
            ch = Chain(dve, chain)
            logits = LG[:, :, 0:E1]

            def along(t, n):
                return t.rearrange("p (b o) -> p b o", o=1).broadcast_to((128, B, n))

            dve.wait_ge(made, 7)
            ch.link(nc.vector.tensor_reduce(negmax[:, :], logits, AX_X, ALU.max, negate=True))
            nc.vector.tensor_tensor(ex[:, :, :], logits, along(negmax[:, :], E1), ALU.add).then_inc(max_sb, 1)
            dve.wait_ge(ex_sb, 1)
            ch.link(nc.vector.tensor_reduce(sums[:, :], ex[:, :, :], AX_X, ALU.add))
            ch.link(nc.vector.reciprocal(rs[:, :], sums[:, :]))
            nc.vector.tensor_scalar(ez1[:, :], ez[:, :], 1.0, None, ALU.add)
            ch.link(nc.vector.tensor_tensor(probs[:, :, :], ex[:, :, :], along(rs[:, :], E1), ALU.mult))
            nc.vector.reciprocal(sig[:, :], ez1[:, :])
            for b in range(B):
                last = nc.vector.max(top[:, b, :], probs[:, b, :])
            ch.link(last)
            for b in range(B):
                last = nc.vector.max_index(top_at[:, b, :], top[:, b, :], probs[:, b, :])
            ch.link(last)
            nc.vector.tensor_reduce(s4[:, :], top[:, :, 0:TOPK], AX_X, ALU.add)
            ch.link(nc.vector.tensor_copy(at[:, :, :], top_at[:, :, 0:TOPK]))
            nc.vector.reciprocal(i4[:, :], s4[:, :])
            for k in range(TOPK):
                last = nc.vector.tensor_tensor(choice[k][:, :, :], expert[:, :, :],
                                               at[:, :, k:k + 1].broadcast_to((128, B, E1)), ALU.is_equal)
            ch.link(last)
            nc.vector.tensor_tensor(w4[:, :, :], top[:, :, 0:TOPK], along(i4[:, :], TOPK), ALU.mult)
            ch.link(nc.vector.tensor_tensor(member[:, :, :], choice[0][:, :, :], choice[1][:, :, :], ALU.add))
            ch.link(nc.vector.tensor_tensor(member[:, :, :], member[:, :, :], choice[2][:, :, :], ALU.add))
            nc.vector.tensor_tensor(member[:, :, :], member[:, :, :], choice[3][:, :, :], ALU.add).then_inc(mem_sb, 1)
            ch.link(nc.vector.tensor_copy(upto[:, 0, :], zeros[:, :]))
            dve.wait_ge(cnt_ps, 1)
            nc.vector.tensor_copy(before[:, :, :].rearrange("p b e -> p (b e)"), BEFORE[:, :])
            ch.link(nc.vector.tensor_copy(totals[:, :, :].rearrange("p b e -> p (b e)"), TOTALS[:, :]))
            for b in range(B):
                ch.link(nc.vector.tensor_tensor(upto[:, b + 1, :], upto[:, b, :], totals[:, b, :], ALU.add))
            count = upto[:, B, :].rearrange("p (e o) -> p e o", o=1).broadcast_to((128, E1, B * S // TT))
            ch.link(nc.vector.tensor_tensor(over[:, :, :], count, edge[:, :, :], ALU.is_gt))
            ch.link(nc.vector.tensor_reduce(ntiles[:, :], over[:, :, :], AX_X, ALU.add))
            ch.link(nc.vector.tensor_tensor_scan(ends[:, :], ntiles[:, :], zeros[:, :], 0.0, ALU.add, ALU.add))
            ch.link(nc.vector.tensor_scalar(done[:, :], ends[:, :], tile_at[:, 0:1], None, ALU.is_le))
            ch.link(nc.vector.tensor_reduce(te[:, :], done[:, :], AX_X, ALU.add))
            nc.vector.tensor_scalar(te[:, :], te[:, :], float(E1 - 1), None, ALU.min).then_inc(te_sb, 1)
            ch.link(nc.vector.tensor_tensor(first[:, :], ends[:, :], ntiles[:, :], ALU.subtract))
            ch.link(nc.vector.tensor_scalar(first[:, :], first[:, :], float(TT), None, ALU.mult))
            ch.link(nc.vector.tensor_tensor(slot[:, :, :], before[:, :, :], upto[:, 0:B, :], ALU.add))
            ch.link(nc.vector.tensor_tensor(slot[:, :, :], slot[:, :, :],
                                            first[:, :].rearrange("p (o e) -> p o e", o=1).broadcast_to((128, B, E1)), ALU.add))
            for k in range(TOPK):
                ch.link(nc.vector.tensor_tensor(mine[:, :, :], choice[k][:, :, :], slot[:, :, :], ALU.mult))
                ch.link(nc.vector.tensor_reduce(slotf[:, k, :], mine[:, :, :], AX_X, ALU.add))
            nc.vector.tensor_copy(slots[:, :, :], slotf[:, :, :].rearrange("p k b -> p b k")).then_inc(slots_sb, 1)
            dve.wait_ge(te_ps, 1)
            ch.link(nc.vector.tensor_copy(tile_expert[:, :], TE[0:1, 0:TILES]))


def experts1_phase(nc, r, a, tile_expert, xs_dram, ys_dram):
    NBUF = 4
    with ExitStack() as ctx:
        def sb(name, shape, dt=F32):
            return ctx.enter_context(nc.sbuf_tensor("e1_" + name, shape, dt))

        def sem(name):
            return ctx.enter_context(nc.semaphore("e1_" + name))

        wgu = [sb(f"wgu{v}", [128, KD, 2, F1]) for v in range(NBUF)]
        wd = [sb(f"wd{v}", [FH, 2, D]) for v in range(NBUF)]
        xt = [sb(f"xt{v}", [128, D]) for v in range(NBUF)]
        xT = [sb(f"xT{v}", [128, KD, TT]) for v in range(2)]
        sg = [sb(f"sg{v}", [FH, 2, TT]) for v in range(2)]
        hidden = [sb(f"hidden{v}", [FH, 2, TT]) for v in range(2)]
        yt = [sb(f"yt{v}", [128, D]) for v in range(NBUF)]
        x_in, w_in, y_out = ([sem(f"{n}{v}") for v in range(NBUF)] for n in ("x_in", "w_in", "y_out"))
        xt_ps, xt_sb, g_ps, sg_sb, u_ps, hid_sb, y_ps, y_sb = (sem(n) for n in (
            "xt_ps", "xt_sb", "g_ps", "sg_sb", "u_ps", "hid_sb", "y_ps", "y_sb"))
        AHEAD = 2
        XT, G, U, Y = r.banks[0:2], r.banks[2:4], r.banks[4:6], r.banks[6:8]
        block = ctx.enter_context(nc.Block())

        def later(i, v):
            return i + v // NBUF, v % NBUF

        @block.sync
        def _(sp):
            def load(i, v):
                i, v = later(i, v)
                t = i * NBUF + v
                sp.dma_start(xt[v][:, :], xs_dram[bass.ds(t * TT, TT), :]).then_inc(x_in[v], 16)
                e = sp.value_load(tile_expert[0:1, bass.ds(t, 1)], min_val=0, max_val=E1 - 1)
                sp.dma_start(wgu[v][:, :, :, :].rearrange("p k m n -> p (k m n)"),
                             a["L1_gate_up"][bass.ds(e, 1), :, :].rearrange("o p n -> p (o n)")).then_inc(w_in[v], 16)
                sp.dma_start(wd[v][:, :, :].rearrange("p k n -> p (k n)"),
                             a["L1_down"][bass.ds(e, 1), :, :].rearrange("o p n -> p (o n)")).then_inc(w_in[v], 16)

            def turn(i, last_turn):
                for v in range(NBUF):
                    t = i * NBUF + v
                    sp.wait_ge(y_sb, t + 1 + AHEAD)
                    sp.sem_inc(r.held, 1)
                    sp.dma_start(ys_dram[bass.ds(t * TT, TT), :], yt[v][:, :]).then_inc(y_out[v], 16)
                    if not last_turn:
                        load(i, v + NBUF)

            for v in range(NBUF):
                load(0, v)
            with sp.Fori(0, TILES // NBUF - 1) as i:
                turn(i, False)
            turn(TILES // NBUF - 1, True)
            for v in range(NBUF):
                sp.wait_ge(y_out[v], (1 + TILES // NBUF) * 16)

        @block.tensor
        def _(pe):
            def turn_over(i, v):
                i, v = later(i, v)
                t = i * NBUF + v
                pe.wait_ge(x_in[v], i * 16 + 16)
                pe.wait_ge(xt_sb, t - 1 + AHEAD)
                for k in range(KD):
                    last = nc.tensor.transpose(XT[v % 2][:, k * TT:(k + 1) * TT], xt[v][:, k * 128:(k + 1) * 128], r.ident[:, :])
                last.then_inc(xt_ps, 1)

            def up(i, v):
                i, v = later(i, v)
                t = i * NBUF + v
                pe.wait_ge(xt_sb, t + 1 + AHEAD)
                pe.wait_ge(w_in[v], i * 32 + 32)
                for n, (free, bank, full) in enumerate(((sg_sb, G, g_ps), (hid_sb, U, u_ps))):
                    pe.wait_ge(free, t - 1 + AHEAD)
                    for m in range(2):
                        for k in range(KD):
                            last = nc.tensor.matmul(bank[v % 2][0:FH, m * TT:(m + 1) * TT], wgu[v][:, k, n, m * FH:(m + 1) * FH],
                                                    xT[v % 2][:, k, :], start=k == 0, stop=k == KD - 1)
                    last.then_inc(full, 1)

            def down(i, v):
                t = i * NBUF + v
                pe.wait_ge(hid_sb, t + 1 + AHEAD)
                pe.wait_ge(y_sb, t - 1 + AHEAD)
                for m in range(2):
                    last = nc.tensor.matmul(Y[v % 2][:, 0:D], hidden[v % 2][:, m, :], wd[v][:, m, :], start=m == 0, stop=m == 1)
                last.then_inc(y_ps, 1)

            def turn(i, last_turn):
                for v in range(NBUF):
                    if not (last_turn and v + 1 >= NBUF):
                        up(i, v + 1)
                    if not (last_turn and v + 2 >= NBUF):
                        turn_over(i, v + 2)
                    down(i, v)

            turn_over(0, 0)
            up(0, 0)
            turn_over(0, 1)
            with pe.Fori(0, TILES // NBUF - 1) as i:
                turn(i, False)
            turn(TILES // NBUF - 1, True)

        @block.scalar
        def _(act):
            for s in (xt_sb, sg_sb, hid_sb, y_ps, y_sb):
                act.sem_inc(s, AHEAD)
            for v in range(NBUF):
                act.sem_inc(y_out[v], 16)

            def gate(i, v):
                t = i * NBUF + v
                act.wait_ge(g_ps, t + 1)
                act.wait_ge(hid_sb, t - 1 + AHEAD)
                nc.scalar.activation(sg[v % 2][:, :, :].rearrange("p m t -> p (m t)"), G[v % 2][0:FH, 0:2 * TT], ACT.Silu
                                     ).then_inc(sg_sb, 1)

            def turn(i, last_turn):
                for v in range(NBUF):
                    if not (last_turn and v + 1 >= NBUF):
                        gate(i, v + 1)
                    t = i * NBUF + v
                    act.wait_ge(y_ps, t + 1 + AHEAD)
                    act.wait_ge(y_out[v], i * 16 + 16)
                    nc.scalar.copy(yt[v][:, :], Y[v % 2][:, 0:D]).then_inc(y_sb, 1)

            gate(0, 0)
            with act.Fori(0, TILES // NBUF - 1) as i:
                turn(i, False)
            turn(TILES // NBUF - 1, True)

        @block.vector
        def _(dve):
            def take_tokens(i, v):
                t = i * NBUF + v
                dve.wait_ge(xt_ps, t + 1)
                nc.vector.tensor_copy(xT[v % 2][:, :, :].rearrange("p k t -> p (k t)"), XT[v % 2][:, 0:D]).then_inc(xt_sb, 1)

            def gated(i, v):
                t = i * NBUF + v
                dve.wait_ge(u_ps, t + 1)
                dve.wait_ge(sg_sb, t + 1 + AHEAD)
                nc.vector.tensor_tensor(hidden[v % 2][:, :, :].rearrange("p m t -> p (m t)"),
                                        sg[v % 2][:, :, :].rearrange("p m t -> p (m t)"), U[v % 2][0:FH, 0:2 * TT], ALU.mult
                                        ).then_inc(hid_sb, 1)

            def turn(i, last_turn):
                for v in range(NBUF):
                    if not (last_turn and v + 1 >= NBUF):
                        gated(i, v + 1)
                    if not (last_turn and v + 2 >= NBUF):
                        take_tokens(i, v + 2)

            take_tokens(0, 0)
            gated(0, 0)
            take_tokens(0, 1)
            with dve.Fori(0, TILES // NBUF - 1) as i:
                turn(i, False)
            turn(TILES // NBUF - 1, True)


def combine1_phase(nc, r, w4, slots, sig, SH, ys_dram, out):
    NBUF = 4
    with ExitStack() as ctx:
        def sb(name, shape, dt=F32):
            return ctx.enter_context(nc.sbuf_tensor("c1_" + name, shape, dt))

        def sem(name):
            return ctx.enter_context(nc.semaphore("c1_" + name))

        y = [sb(f"y{n}", [128, TOPK, D]) for n in range(NBUF)]
        y_in = [sem(f"y_in{n}") for n in range(NBUF)]
        x_sb, stored, chain = sem("x_sb"), sem("stored"), sem("dve_chain")
        block = ctx.enter_context(nc.Block())

        @block.gpsimd
        def _(pool):
            for b in range(B):
                if b >= NBUF:
                    pool.wait_ge(x_sb, b - NBUF + 1)
                for k in range(TOPK):
                    nc.gpsimd.indirect_dma_start(
                        out=y[b % NBUF][:, k, :], out_offset=None, in_=ys_dram[:, :],
                        in_offset=bass.IndirectOffsetOnAxis(ap=slots[:, b, k:k + 1], axis=0)).then_inc(y_in[b % NBUF], 16)

        @block.vector
        def _(dve):
            ch = Chain(dve, chain)
            for b in range(B):
                acc = SH[:, b, :]
                ch.link(nc.vector.tensor_scalar(acc, acc, sig[:, b:b + 1], None, ALU.mult))
                dve.wait_ge(y_in[b % NBUF], (b // NBUF + 1) * 16 * TOPK)
                for k in range(TOPK):
                    ch.link(nc.vector.scalar_tensor_tensor(out=acc, in0=y[b % NBUF][:, k, :], scalar=w4[:, b, k:k + 1],
                                                           in1=acc, op0=ALU.mult, op1=ALU.add))
                nc.vector.scalar_tensor_tensor(out=r.X[:, b, :], in0=acc, scalar=r.gates[:, 3:4], in1=r.X[:, b, :],
                                               op0=ALU.mult, op1=ALU.add).then_inc(x_sb, 1)

        @block.sync
        def _(sp):
            for b in range(B):
                sp.wait_ge(x_sb, b + 1)
                sp.dma_start(out[b, :, :], r.X[:, b, :]).then_inc(stored, 16)
            sp.wait_ge(stored, 16 * B)


def build(nc, a, out):
    with ExitStack() as ctx:
        r = Resident(nc, ctx)
        signals = AttentionSignals(nc, ctx)
        xs_dram = nc.dram_tensor("xs_dram", (TILES * TT, D), F32, kind="Internal").ap()
        load_phase(nc, r, a)
        stats_phase(nc, r, "ln_xattn0")
        with nc.sbuf_tensor("attended", [128, B, D], F32) as r.XN:
            attention_phase(nc, r, a, 0, signals)
            stats_phase(nc, r, "ln_ffn0", added=r.XN, gate=r.gates[:, 0:1], clear=signals)
        with ExitStack() as ffn:
            xn_hi, xn_lo = (ffn.enter_context(nc.sbuf_tensor(n, [128, B, D], F32R)) for n in ("xn_hi", "xn_lo"))
            R = ffn.enter_context(nc.sbuf_tensor("R", [128, B, E0 + 1], F32))
            W = ffn.enter_context(nc.sbuf_tensor("W", [128, B, E0 + 1], F32))
            router0_phase(nc, r, a, R, W, xn_hi, xn_lo)
            experts0_phase(nc, r, a, R, W, xn_hi, xn_lo, xs_dram)
        stats_phase(nc, r, "ln_xattn1")
        attention_phase(nc, r, a, 1, signals)
        stats_phase(nc, r, "ln_ffn1")
        r.XN = ctx.enter_context(nc.sbuf_tensor("XN", [128, B, D], F32))
        LG, SH, w4, sig = (ctx.enter_context(nc.sbuf_tensor(n, s, F32)) for n, s in (
            ("LG", [128, B, E1 + 1]), ("SH", [128, B, D]), ("w4", [128, B, TOPK]), ("sig", [128, B])))
        slots = ctx.enter_context(nc.sbuf_tensor("slots", [128, B, TOPK], I32))
        tile_expert = ctx.enter_context(nc.sbuf_tensor("tile_expert", [1, TILES], I32))
        ys_dram = nc.dram_tensor("ys_dram", (TILES * TT, D), F32, kind="Internal").ap()
        router1_phase(nc, r, a, LG, SH)
        dispatch1_phase(nc, r, LG, w4, slots, sig, tile_expert, xs_dram)
        experts1_phase(nc, r, a, tile_expert, xs_dram, ys_dram)
        combine1_phase(nc, r, w4, slots, sig, SH, ys_dram, out)


def kernel(**inputs):
    import numpy as np
    import concourse.bacc as bacc
    from concourse.bass_utils import run_bass_kernel_spmd as run

    laid_out = {
        "x": inputs["x"],
        "ctx_t": np.asarray(inputs["ctx_1024"]).transpose(0, 2, 1),
        "mask_pad": np.asarray(inputs["mask_BxS2_bf0"]),
        "mask_BxSxS2_ik0": inputs["mask_BxSxS2_ik0"],
        "L0_wq_t": np.asarray(inputs["L0_xattn_Wq"]).T,
        "L0_wk_t": np.asarray(inputs["L0_xattn_Wk"]).T,
        "L0_wv_t": np.asarray(inputs["L0_xattn_Wv"]).T,
        "L1_wq_t": np.asarray(inputs["L1_xattn_w_q"]).T,
        "L1_wk_t": np.asarray(inputs["L1_xattn_w_k"]).T,
        "L1_wv_t": np.asarray(inputs["L1_xattn_w_v"]).T,
        "L1_router_and_gate_w": np.concatenate([np.asarray(inputs["L1_ffn_router_w"]),
                                                np.asarray(inputs["L1_ffn_sh_gate_w"])], axis=1),
        "L1_gate_up": np.stack([np.asarray(inputs["L1_ffn_w_gate"]), np.asarray(inputs["L1_ffn_w_up"])], axis=2)
                      .reshape(E1, KD, 128, 2 * F1).transpose(0, 2, 1, 3).reshape(E1, 128, KD * 2 * F1),
        "L1_down": np.asarray(inputs["L1_ffn_w_down"]).reshape(E1, 2, FH, D).transpose(0, 2, 1, 3).reshape(E1, FH, 2 * D),
        "L1_wo_t": np.asarray(inputs["L1_xattn_w_o"]).T,
    }
    for name in ("g_xattn", "g_ffn", "L0_xattn_bq", "L0_xattn_bk", "L0_xattn_bv", "L1_xattn_b_o", "L0_ffn_router_w1", "L0_ffn_router_w2",
                 "L0_ffn_w1", "L0_ffn_w2", "L0_ffn_w3",
                 "L1_ffn_sh_gate", "L1_ffn_sh_up", "L1_ffn_sh_down"):
        laid_out[name] = inputs[name]

    nc = bacc.Bacc("TRN2", target_bir_lowering=False, num_devices=1)
    arrays, args = {}, {}
    for name, value in laid_out.items():
        value = np.ascontiguousarray(value)
        arrays[f"in_{name}"] = value
        args[name] = nc.dram_tensor(f"in_{name}", value.shape, U8 if value.dtype == bool else mybir.dt.from_np(value.dtype), kind="ExternalInput").ap()
    out = nc.dram_tensor("out", (B, S, D), F32, kind="ExternalOutput").ap()
    build(nc, args, out)
    return run(nc, [arrays], core_ids=[0]).results[0]["out"]
```

```python
import concourse.bass as bass
from concourse import mybir
from contextlib import ExitStack

ACT = mybir.ActivationFunctionType
ALU = mybir.AluOpType
AX_X = mybir.AxisListType.X
F32 = mybir.dt.float32
BF16 = mybir.dt.bfloat16
F32R = mybir.dt.float32r
I32 = mybir.dt.int32
U8 = mybir.dt.uint8

B, S, D = 16, 128, 256
H, DH = 16, 16
KD = D // 128
STRIPS = 4
HS = H // STRIPS
EPS = 1e-5
MASKED = -2.0 ** 120


class Chain:

    def __init__(self, eng, sem, base=0):
        self.eng, self.sem, self.n, self.base = eng, sem, 0, base

    def link(self, ins):
        self.n += 1
        ins.then_inc(self.sem, 1)
        self.eng.wait_ge(self.sem, self.base + self.n)


class Resident:

    def __init__(self, nc, ctx):
        def sb(name, shape, dt=F32):
            return ctx.enter_context(nc.sbuf_tensor(name, shape, dt))

        self.X = sb("X", [128, B, D])
        self.XN = None
        self.ident = sb("ident", [128, 128])
        self.ident_bf = sb("ident_bf", [128, 128], BF16)
        self.gates = sb("gates", [128, 4])
        self.stats = sb("stats", [128, B, 6])
        self.mv = sb("mv", [128, B, 2])
        self.var = sb("var", [128, B])
        self.std = sb("std", [128, B])
        self.rstd = sb("rstd", [128, B])
        self.held = ctx.enter_context(nc.semaphore("held"))
        self.banks = [ctx.enter_context(nc.psum_tensor(f"bank{i}", [128, 512], F32)) for i in range(8)]


def load_phase(nc, r, a):
    with ExitStack() as ctx:
        s_x, s_g, s_zero, s_ident, s_gates = (ctx.enter_context(nc.semaphore(n)) for n in (
            "x_loaded", "g_loaded", "ident_zeroed", "ident_made", "gates_made"))
        block = ctx.enter_context(nc.Block())

        @block.sync
        def _(sp):
            sp.dma_start(r.X[:, :, :], a["x"].rearrange("b s d -> s b d")).then_inc(s_x, 16)
            sp.dma_start(r.gates[:, 0:2], a["g_xattn"].partition_broadcast(128)).then_inc(s_g, 16)
            sp.dma_start(r.gates[:, 2:4], a["g_ffn"].partition_broadcast(128)).then_inc(s_g, 16)
            sp.wait_ge(s_x, 16)

        @block.gpsimd
        def _(pool):
            nc.gpsimd.memset(r.ident[:, :], 0.0).then_inc(s_zero, 1)
            nc.gpsimd.memset(r.ident_bf[:, :], 0.0).then_inc(s_zero, 1)
            pool.wait_ge(s_zero, 2)
            for t in (r.ident, r.ident_bf):
                nc.gpsimd.affine_select(out=t[:, :], in_=t[:, :], compare_op=ALU.not_equal, fill=1.0, base=0,
                                        pattern=[[-1, 128]], channel_multiplier=1).then_inc(s_ident, 1)
            pool.wait_ge(s_ident, 2)

        @block.scalar
        def _(act):
            act.wait_ge(s_g, 32)
            nc.scalar.activation(r.gates[:, :], r.gates[:, :], ACT.Tanh).then_inc(s_gates, 1)
            act.wait_ge(s_gates, 1)


def stats_phase(nc, r, name, added=None, gate=None, clear=None):
    with ExitStack() as ctx:
        s_chain, s_var, s_std = (ctx.enter_context(nc.semaphore(f"{name}_{n}")) for n in
                                 ("dve_chain", "var_ready", "std_ready"))
        block = ctx.enter_context(nc.Block())

        @block.vector
        def _(dve):
            ch = Chain(dve, s_chain)
            if added is not None:
                for b in range(B):
                    last = nc.vector.scalar_tensor_tensor(out=r.X[:, b, :], in0=added[:, b, :], scalar=gate,
                                                          in1=r.X[:, b, :], op0=ALU.mult, op1=ALU.add)
                ch.link(last)
            for b in range(B):
                last = nc.vector.bn_stats(r.stats[:, b, :], r.X[:, b, :])
            ch.link(last)
            for b in range(B):
                last = nc.vector.bn_aggr(r.mv[:, b, :], r.stats[:, b, :])
            ch.link(last)
            nc.vector.tensor_scalar(r.var[:, :], r.mv[:, :, 1], EPS, None, ALU.add).then_inc(s_var, 1)
            dve.wait_ge(s_std, 1)
            ch.link(nc.vector.reciprocal(r.rstd[:, :], r.std[:, :]))

        @block.scalar
        def _(act):
            act.wait_ge(s_var, 1)
            nc.scalar.activation(r.std[:, :], r.var[:, :], ACT.Sqrt).then_inc(s_std, 1)

        if clear is not None:
            @block.sync
            def _(sp):
                sp.sem_clear(range(min(clear.numbers), max(clear.numbers) + 1))


class AttentionSignals:

    def __init__(self, nc, ctx):
        self.numbers = []

        def sem(name):
            s = ctx.enter_context(nc.semaphore("attn_" + name))
            self.numbers.append(s.num)
            return s

        def pair(name):
            return [sem(name + "0"), sem(name + "1")]

        self.w_in = sem("w_in")
        self.w_made = sem("w_made")
        self.causal_made = sem("causal_made")
        self.zeroed = sem("zeroed")
        self.mask_sb = sem("mask_sb")
        self.k_tok_sb = sem("k_tok_sb")
        self.q_tok_sb = sem("q_tok_sb")
        self.k_hi_sb = sem("k_hi_sb")
        self.q_hi_sb = sem("q_hi_sb")
        self.xb_sb = sem("xb_sb")
        self.xt_ps = sem("xt_ps")
        self.xt_sb = sem("xt_sb")
        self.q_ps = sem("q_ps")
        self.kv_ps = sem("kv_ps")
        self.q_sb = sem("q_sb")
        self.qk_sb = sem("qk_sb")
        self.v_sb = sem("v_sb")
        self.s_ps = sem("s_ps")
        self.max_sb = sem("max_sb")
        self.p_sb = sem("p_sb")
        self.pt_ps = sem("pt_ps")
        self.pt_sb = sem("pt_sb")
        self.pv_ps = sem("pv_ps")
        self.o_sb = sem("o_sb")
        self.o_in = sem("o_in")
        self.k_ps = sem("k_ps")
        self.ot_ps = sem("ot_ps")
        self.ot_sb = sem("ot_sb")
        self.y_ps = sem("y_ps")
        self.y_sb = sem("y_sb")
        self.chain = sem("chain")
        self.v_out = pair("v_out")
        self.v_in = pair("v_in")
        self.o_out = pair("o_out")


def attention_phase(nc, r, a, layer, signals):
    pre = f"a{layer}_"
    S_BANKS, PT_BANKS, KV, XQ = r.banks[0:4], r.banks[4:6], r.banks[6], r.banks[7]
    Q1, V1 = PT_BANKS[1], PT_BANKS[0]
    O = S_BANKS[0]
    BANK_ORDER = (1, 2, 3, 0)
    NJ = STRIPS
    AHEAD = 5
    FIRST, FIRST_DMA = 1, 16

    def head(j, g):
        return HS * j + g if layer == 0 else STRIPS * g + j

    with ExitStack() as ctx:
        def sb(name, shape, dt=F32):
            return ctx.enter_context(nc.sbuf_tensor(pre + name, shape, dt))

        xb = [sb(f"xb{u}", [128, D]) for u in range(2)]
        xT = [sb(f"xT{u}", [128, KD, S]) for u in range(2)]
        cT = [sb(f"cT{u}", [128, KD, S]) for u in range(2)]
        qT = [sb(f"qT{u}", [128, HS, S], F32R) for u in range(2)]
        kA = [sb(f"kA{u}", [128, HS, S], F32R) for u in range(2)]
        kB = [sb(f"kB{u}", [128, HS, S], F32R) for u in range(2)]
        vtok = [sb(f"vtok{u}", [128, H, DH + 1]) for u in range(2)]
        mask = [sb(f"mask{u}", [128, S], BF16) for u in range(2)]
        negmax = [sb(f"negmax{u}", [128, NJ, HS]) for u in range(2)]
        rinv = [sb(f"rinv{u}", [128, H]) for u in range(2)]
        osb = [sb(f"osb{u}", [128, H, DH]) for u in range(2)]
        P = sb("P", [128, NJ, HS, S])
        pT = [sb(f"pT{u}", [128, HS, S]) for u in range(2)]
        qhi = sb("qhi", [128, HS, S], F32R)
        low_cols = sb("low_cols", [128, STRIPS, DH])
        low_rows = sb("low_rows", [128, 1])
        if layer == 0:
            padmask = [sb(f"padmask{u}", [128, S], U8) for u in range(2)]
            causal = sb("causal", [128, S])
            q_tok = sb("q_tok", [128, H, 2, DH])
            k_tok = sb("k_tok", [128, H, 2, DH])
            q_strips = sb("q_strips", [128, HS, S])
            k_strips = sb("k_strips", [128, HS, S])
            vs = [sb(f"vs{u}", [128, H, DH + 1]) for u in range(2)]
            wq = sb("wq", [128, KD, D])
            wkv = sb("wkv", [128, KD, 2 * D])
            bq = sb("bq", [128, D])
            bkv = sb("bkv", [128, 2 * D])
            v_dram = nc.dram_tensor(pre + "v_dram", (B * S * D,), F32, kind="Internal").ap()
            o_dram = nc.dram_tensor(pre + "o_dram", (B * S * D,), F32, kind="Internal").ap()
        else:
            imask = [sb(f"imask{u}", [128, S], I32) for u in range(2)]
            wdense = sb("wdense", [128, KD, 2 * D])
            wqp = sb("wqp", [128, KD, H, 2 * DH])
            wkp = sb("wkp", [128, KD, H, 2 * DH])
            wv = sb("wv", [128, KD, D])
            wo = sb("wo", [128, KD, D])
            bo = sb("bo", [128, D])
            oT = [sb(f"oT{u}", [128, KD, S]) for u in range(2)]
            proj = [sb(f"proj{u}", [128, D]) for u in range(2)]
            vs = vtok

        q = signals
        mask_in, ctx_in = ([ctx.enter_context(nc.semaphore(f"{pre}{n}{u}")) for u in range(2)] for n in ("mask_in", "ctx_in"))
        block = ctx.enter_context(nc.Block())

        @block.sync
        def _(sp):
            def hold(sp, sem, value):
                sp.wait_ge(sem, value)
                sp.sem_inc(r.held, 1)

            def weights(dst, name):
                sp.dma_start(dst, a[name].rearrange("(k p) n -> p k n", p=128)).then_inc(q.w_in, 16)

            if layer == 0:
                weights(wq[:, :, :], "L0_wq_t")
                weights(wkv[:, :, 0:D], "L0_wk_t")
                weights(wkv[:, :, D:2 * D], "L0_wv_t")
                sp.dma_start(bq[:, :], a["L0_xattn_bq"].partition_broadcast(128)).then_inc(q.w_in, 16)
                sp.dma_start(bkv[:, 0:D], a["L0_xattn_bk"].partition_broadcast(128)).then_inc(q.w_in, 16)
                sp.dma_start(bkv[:, D:2 * D], a["L0_xattn_bv"].partition_broadcast(128)).then_inc(q.w_in, 16)
                sp.wait_ge(q.zeroed, 2)
                with sp.Fori(0, B // 2) as i:
                    for u in range(2):
                        b = i * 2 + u
                        vd = v_dram[bass.ds(sp.snap(b * (S * D)), S * D)]
                        hold(sp, q.v_sb, b + 1)
                        sp.dma_start(vd.rearrange("(s h e) -> s h e", h=H, e=DH), vtok[u][:, :, 0:DH]).then_inc(q.v_out[u], 16)
                        hold(sp, q.v_out[u], i * 16 + 16 + FIRST_DMA)
                        hold(sp, q.pv_ps, (b - 1) * NJ + AHEAD)
                        sp.dma_start(vs[u][:, :, 0:DH], vd.rearrange("(h p e) -> p h e", h=H, e=DH)).then_inc(q.v_in[u], 16)
                    for u in range(2):
                        b = i * 2 + u
                        od = o_dram[bass.ds(sp.snap(b * (S * D)), S * D)]
                        hold(sp, q.o_sb, b + 1 + FIRST)
                        sp.dma_start(od.rearrange("(h p e) -> p h e", h=H, e=DH), osb[u][:, :, :]).then_inc(q.o_out[u], 16)
                for u in range(2):
                    sp.wait_ge(q.o_out[u], 16 * B // 2 + FIRST_DMA)
                sp.dma_start(r.XN[:, :, :], o_dram.rearrange("(b s d) -> s b d", b=B, s=S)).then_inc(q.o_in, 16)
                sp.wait_ge(q.o_in, 16)
            else:
                weights(wdense[:, :, 0:D], "L1_wq_t")
                weights(wdense[:, :, D:2 * D], "L1_wk_t")
                weights(wv[:, :, :], "L1_wv_t")
                weights(wo[:, :, :], "L1_wo_t")
                sp.dma_start(bo[:, :], a["L1_xattn_b_o"].partition_broadcast(128)).then_inc(q.w_in, 16)

        @block.gpsimd
        def _(pool):
            for u in range(2):
                nc.gpsimd.memset(vs[u][:, :, :], 1.0).then_inc(q.zeroed, 1)
            nc.gpsimd.tensor_copy(low_cols[:, :, :], r.ident[:, :].rearrange("p (j n) -> p j n", j=STRIPS)[:, :, DH:2 * DH]
                                  ).then_inc(q.zeroed, 1)
            if layer == 0:
                nc.gpsimd.memset(causal[:, :], 0.0).then_inc(q.zeroed, 1)
                pool.wait_ge(q.zeroed, 4)
                nc.gpsimd.affine_select(out=causal[:, :], in_=causal[:, :], compare_op=ALU.is_ge, fill=MASKED, base=0,
                                        pattern=[[-1, S]], channel_multiplier=1).then_inc(q.causal_made, 1)

            def load(i, u):
                b = i * 2 + u
                if layer == 0:
                    src = a["mask_pad"][bass.ds(b, 1), :].rearrange("o s -> (o s)").partition_broadcast(128)
                    pool.dma_start(padmask[u][:, :], src).then_inc(mask_in[u], 16)
                else:
                    src = a["mask_BxSxS2_ik0"][bass.ds(b, 1), :, :].rearrange("o q k -> (o q) k")
                    pool.dma_start(imask[u][:, :], src).then_inc(mask_in[u], 16)
                src = a["ctx_t"][bass.ds(b, 1), :, :].rearrange("o (k p) s -> p (o k) s", p=128)
                pool.dma_start(cT[u][:, :, :], src).then_inc(ctx_in[u], 16)

            def turn(i, last_turn):
                for u in range(2):
                    b = i * 2 + u
                    if not last_turn:
                        pool.wait_ge(q.mask_sb, b + 1 + FIRST)
                        pool.wait_ge(q.kv_ps, b + 1 + FIRST)
                        load(i + 1, u)
                    if layer == 0:
                        pool.wait_ge(q.k_tok_sb, b + 1)
                        pool.sem_inc(r.held, 1)
                        nc.gpsimd.tensor_copy(kA[u][:, :, :].rearrange("p g s -> p (g s)"),
                                              k_strips[:, :, :].rearrange("p g s -> p (g s)")).then_inc(q.k_hi_sb, 1)
                        pool.wait_ge(q.q_tok_sb, b + 1)
                        pool.sem_inc(r.held, 1)
                        nc.gpsimd.tensor_copy(qhi[:, :, :].rearrange("p g s -> p (g s)"),
                                              q_strips[:, :, :].rearrange("p g s -> p (g s)")).then_inc(q.q_hi_sb, 1)

            load(0, 0)
            load(0, 1)
            with pool.Fori(0, B // 2 - 1) as i:
                turn(i, False)
            if layer == 0:
                turn(B // 2 - 1, True)

        @block.tensor
        def _(pe):
            pe.wait_ge(q.w_in, 16 * (6 if layer == 0 else 5))
            pe.wait_ge(q.w_made, 1 if layer == 0 else 4 * KD)

            def turn_x(i, u):
                b = i * 2 + u
                pe.wait_ge(q.xb_sb, b + 1)
                pe.wait_ge(q.qk_sb, b + FIRST)
                if layer == 1 and not (isinstance(b, int) and b < 2):
                    pe.wait_ge(q.y_sb, b - 2 + FIRST)
                for k in range(KD):
                    last = nc.tensor.transpose(XQ[:, k * S:(k + 1) * S], xb[u][:, k * 128:(k + 1) * 128], r.ident[:, :])
                last.then_inc(q.xt_ps, 1)

            def project_context(i, u, n):
                b = i * 2 + u
                if n == 0:
                    pe.wait_ge(ctx_in[u], i * 16 + 16)
                if layer == 0 and n % 2 == 0:
                    k = n // 2
                    last = nc.tensor.matmul(KV[:, :], cT[u][:, k, :], wkv[:, k, :], start=k == 0, stop=k == KD - 1)
                if layer == 1:
                    for k in range(KD):
                        w = wkp[:, k, STRIPS * n:STRIPS * n + STRIPS, :].rearrange("p h e -> p (h e)")
                        last = nc.tensor.matmul(KV[:, n * S:(n + 1) * S], w, cT[u][:, k, :], start=k == 0, stop=k == KD - 1)
                    if n == HS - 1:
                        last.then_inc(q.k_ps, 1)
                        pe.wait_ge(q.pt_sb, (b - 1) * NJ + AHEAD)
                        for k in range(KD):
                            last = nc.tensor.matmul(V1[:, 0:D], cT[u][:, k, :], wv[:, k, :], start=k == 0, stop=k == KD - 1)
                if n == (2 if layer == 0 else 3):
                    last.then_inc(q.kv_ps, 1)

            def project_tokens(i, u):
                b = i * 2 + u
                pe.wait_ge(q.xt_sb, b + 1)
                if layer == 0:
                    for k in range(KD):
                        last = nc.tensor.matmul(XQ[:, D:2 * D], xT[u][:, k, :], wq[:, k, :], start=k == 0, stop=k == KD - 1)
                else:
                    for g in range(HS):
                        for k in range(KD):
                            w = wqp[:, k, STRIPS * g:STRIPS * g + STRIPS, :].rearrange("p h e -> p (h e)")
                            last = nc.tensor.matmul(Q1[:, g * S:(g + 1) * S], w, xT[u][:, k, :],
                                                    start=k == 0, stop=k == KD - 1)
                last.then_inc(q.q_ps, 1)

            def scores(i, u):
                b = i * 2 + u
                pe.wait_ge(q.mask_sb, b + 1 + FIRST)
                pe.wait_ge(q.p_sb, b * NJ + FIRST)
                for j in BANK_ORDER:
                    if j == 0:
                        pe.wait_ge(q.o_sb, b + FIRST)
                    m = mask[u][:, :].rearrange("p (o s) -> p o s", o=1).broadcast_to((128, HS, S))
                    nc.tensor.matmul(S_BANKS[j][:, :], r.ident_bf[:, :], m, start=True, stop=False)
                pe.wait_ge(q.qk_sb, b + 1 + FIRST)
                for g in range(HS):
                    for part in (kA, kB):
                        for j in BANK_ORDER:
                            rows = slice(32 * j, 32 * j + 2 * DH)
                            last = nc.tensor.matmul(S_BANKS[j][:, g * S:(g + 1) * S], qT[u][rows, g, :],
                                                    part[u][rows, g, :], start=False, stop=g == HS - 1 and part is kB)
                            if g == HS - 1 and part is kB:
                                last.then_inc(q.s_ps, 1)

            def attend(i, u, more):
                b = i * 2 + u

                def transpose_p(m):
                    n, j = b * NJ + m, BANK_ORDER[m]
                    pe.wait_ge(q.p_sb, n + 1 + FIRST)
                    pe.wait_ge(q.pt_sb, n - 1 + AHEAD)
                    for g in range(HS):
                        last = nc.tensor.transpose(PT_BANKS[m % 2][:, g * S:(g + 1) * S], P[:, j, g, :], r.ident[:, :])
                    last.then_inc(q.pt_ps, 1)

                def values(m):
                    n, j = b * NJ + m, BANK_ORDER[m]
                    pe.wait_ge(q.pt_sb, n + 1 + AHEAD)
                    for g in range(HS):
                        h = head(j, g)
                        last = nc.tensor.matmul(O[:, h * (DH + 1):(h + 1) * (DH + 1)], pT[m % 2][:, g, :], vs[u][:, h, :],
                                                start=True, stop=True)
                    last.then_inc(q.pv_ps, 1)

                if layer == 1 and more:
                    pe.wait_ge(q.v_sb, b + 2)
                transpose_p(0)
                if layer == 1 and more:
                    pe.wait_ge(q.q_sb, b + 2 + FIRST)
                if layer == 0:
                    pe.wait_ge(q.v_in[u], i * 16 + 16)
                pe.wait_ge(q.p_sb, b * NJ + NJ + FIRST)
                for m in range(1, NJ):
                    transpose_p(m)
                    values(m - 1)
                values(NJ - 1)

            def turn_out(i, u, more):
                b = i * 2 + u
                pe.wait_ge(q.o_sb, b + 1 + FIRST)
                pe.wait_ge(q.y_sb, b + FIRST)
                if more:
                    pe.wait_ge(q.xt_sb, b + 3)
                for k in range(KD):
                    last = nc.tensor.transpose(XQ[:, k * S:(k + 1) * S],
                                               osb[u][:, :, :].rearrange("p h e -> p (h e)")[:, k * 128:(k + 1) * 128],
                                               r.ident[:, :])
                last.then_inc(q.ot_ps, 1)

            def project_out(i, u):
                b = i * 2 + u
                pe.wait_ge(q.ot_sb, b + 1)
                for k in range(KD):
                    last = nc.tensor.matmul(XQ[:, D:2 * D], oT[u][:, k, :], wo[:, k, :], start=k == 0, stop=k == KD - 1)
                last.then_inc(q.y_ps, 1)

            def turn(i, first_turn=False, last_turn=False):
                for u in range(2):
                    more = not (last_turn and u == 1)
                    out = layer == 1 and not (first_turn and u == 0)
                    after, before = (i + u, 1 - u), (i - 1 + u, 1 - u)
                    if more:
                        turn_x(*after)
                    scores(i, u)
                    if more:
                        for n in range(4):
                            project_context(*after, n)
                    if out:
                        turn_out(*before, more)
                    if more:
                        project_tokens(*after)
                    if out:
                        project_out(*before)
                    attend(i, u, more)

            turn_x(0, 0)
            for n in range(4):
                project_context(0, 0, n)
            project_tokens(0, 0)
            turn(0, first_turn=True)
            with pe.Fori(1, B // 2 - 1) as i:
                turn(i)
            turn(B // 2 - 1, last_turn=True)
            if layer == 1:
                turn_out(B // 2 - 1, 1, False)
                project_out(B // 2 - 1, 1)

        @block.scalar
        def _(act):
            for s in (q.pt_ps, q.pt_sb, q.pv_ps):
                act.sem_inc(s, AHEAD)
            for s in (q.mask_sb, q.kv_ps, q.o_sb, q.qk_sb, q.y_sb, q.p_sb, q.q_sb):
                act.sem_inc(s, FIRST)
            for s in (*q.v_out, *q.o_out):
                act.sem_inc(s, FIRST_DMA)

            def high_parts(i, u):
                b = i * 2 + u
                act.wait_ge(q.q_ps, b + 1)
                act.wait_ge(q.q_sb, b + FIRST)
                nc.scalar.copy(qhi[:, :, :].rearrange("p g s -> p (g s)"), Q1[:, :]).then_inc(q.q_hi_sb, 1)
                act.wait_ge(q.k_ps, b + 1)
                nc.scalar.copy(kA[u][:, :, :].rearrange("p g s -> p (g s)"), KV[:, :]).then_inc(q.k_hi_sb, 1)

            def turn(i, last_turn):
                for u in range(2):
                    b = i * 2 + u
                    for m, j in enumerate(BANK_ORDER):
                        n = b * NJ + m
                        act.wait_ge(q.max_sb, n + 1)
                        act.wait_ge(q.pt_ps, n - NJ + 1 + AHEAD)
                        for g in range(HS):
                            last = nc.scalar.activation(P[:, j, g, :], S_BANKS[j][:, g * S:(g + 1) * S], ACT.Exp,
                                                        bias=negmax[u][:, j, g:g + 1])
                        last.then_inc(q.p_sb, 1)
                    if layer == 1 and not (last_turn and u == 1):
                        high_parts(i + u, 1 - u)
                    for m, j in enumerate(BANK_ORDER):
                        n = b * NJ + m
                        act.wait_ge(q.pt_ps, n + 1 + AHEAD)
                        act.wait_ge(q.pv_ps, n - 1 + AHEAD)
                        nc.scalar.copy(pT[m % 2][:, :, :].rearrange("p g s -> p (g s)"), PT_BANKS[m % 2][:, :]
                                       ).then_inc(q.pt_sb, 1)

            if layer == 1:
                high_parts(0, 0)
            with act.Fori(0, B // 2 - 1) as i:
                turn(i, False)
            turn(B // 2 - 1, True)

        @block.vector
        def _(dve):
            if layer == 0:
                dve.wait_ge(q.w_in, 16 * 6)
                dve.wait_ge(q.causal_made, 1)
                ch = Chain(dve, q.chain)
                nc.vector.tensor_scalar(bq[:, :], bq[:, :], DH ** 0.5, None, ALU.mult)
                ch.link(nc.vector.tensor_scalar(wq[:, :, :], wq[:, :, :], DH ** 0.5, None, ALU.mult))
                dve.sem_inc(q.w_made, 1)
            else:
                ch = Chain(dve, q.chain)
                dve.wait_ge(q.w_in, 16 * 5)
                for k in range(KD):
                    for half in range(2):
                        for n, (t, scale) in enumerate(((wqp, DH ** -0.5), (wkp, 1.0))):
                            src = wdense[:, k, n * D:(n + 1) * D].rearrange("p (h e) -> p h e", h=H)
                            nc.vector.tensor_scalar(t[:, k, :, half * DH:(half + 1) * DH], src, scale, None, ALU.mult
                                                    ).then_inc(q.w_made, 1)
            dve.wait_ge(q.zeroed, 3)
            ch.link(nc.vector.tensor_reduce(low_rows[:, :], low_cols[:, :, :].rearrange("p j e -> p (j e)"), AX_X,
                                            ALU.add, negate=True))
            setup = ch.n

            def prepare_early(i, u, ch):
                b = i * 2 + u
                dve.wait_ge(mask_in[u], i * 16 + 16)
                if layer == 0:
                    nc.vector.scalar_tensor_tensor(out=mask[u][:, :], in0=padmask[u][:, :], scalar=MASKED,
                                                   in1=causal[:, :], op0=ALU.mult, op1=ALU.add).then_inc(q.mask_sb, 1)
                else:
                    nc.vector.tensor_scalar(mask[u][:, :], imask[u][:, :], 0.0, MASKED, ALU.is_equal, ALU.mult
                                            ).then_inc(q.mask_sb, 1)
                nc.vector.tensor_scalar(xb[u][:, :], r.X[:, bass.ds(b, 1), :].rearrange("p o d -> p (o d)"),
                                        r.mv[:, bass.ds(b, 1), 0:1].rearrange("p o s -> p (o s)"),
                                        r.rstd[:, bass.ds(b, 1)], ALU.subtract, ALU.mult).then_inc(q.xb_sb, 1)

            def strips(t):
                return t[:, :, :].rearrange("p g s -> p (g s)").rearrange("p (s c) -> p c s", c=H)

            def twice(t):
                return t.rearrange("p (c o e) -> p c o e", o=1, e=DH).broadcast_to((128, H, 2, DH))

            def padded(t):
                return t[:, :, :, :].rearrange("p c o e -> p c (o e)")

            def take_x(i, u):
                b = i * 2 + u
                dve.wait_ge(q.xt_ps, b + 1)
                nc.vector.tensor_copy(xT[u][:, :, :].rearrange("p k s -> p (k s)"), XQ[:, 0:D]).then_inc(q.xt_sb, 1)

            def take_context(i, u, ch):
                b = i * 2 + u
                if layer == 0:
                    dve.wait_ge(q.kv_ps, b + 1 + FIRST)
                    ch.link(nc.vector.tensor_tensor(k_tok[:, :, :, :], twice(KV[:, 0:D]), twice(bkv[:, 0:D]), ALU.add))
                    nc.vector.transpose(strips(k_strips), padded(k_tok)).then_inc(q.k_tok_sb, 1)
                    dve.wait_ge(q.v_out[u], i * 16 + FIRST_DMA)
                    nc.vector.tensor_tensor(vtok[u][:, :, 0:DH], KV[:, D:2 * D].rearrange("p (h e) -> p h e", h=H),
                                            bkv[:, D:2 * D].rearrange("p (h e) -> p h e", h=H), ALU.add).then_inc(q.v_sb, 1)
                else:
                    dve.wait_ge(q.kv_ps, b + 1 + FIRST)
                    nc.vector.tensor_copy(vtok[u][:, :, 0:DH], V1[:, 0:D].rearrange("p (h e) -> p h e", h=H)
                                          ).then_inc(q.v_sb, 1)

            def take_tokens(i, u, ch):
                b = i * 2 + u
                if layer == 0:
                    dve.wait_ge(q.q_ps, b + 1)
                    ch.link(nc.vector.tensor_tensor(q_tok[:, :, :, :], twice(XQ[:, D:2 * D]), twice(bq[:, :]), ALU.add))
                    nc.vector.transpose(strips(q_strips), padded(q_tok)).then_inc(q.q_tok_sb, 1)
                    dve.wait_ge(q.k_hi_sb, b + 1)
                    nc.vector.tensor_tensor(kB[u][:, :, :].rearrange("p g s -> p (g s)"),
                                            k_strips[:, :, :].rearrange("p g s -> p (g s)"),
                                            kA[u][:, :, :].rearrange("p g s -> p (g s)").bitcast(F32), ALU.subtract)
                    dve.wait_ge(q.q_hi_sb, b + 1)
                    nc.vector.scalar_tensor_tensor(out=qT[u][:, :, :].rearrange("p g s -> p (g s)"),
                                                   in0=qhi[:, :, :].rearrange("p g s -> p (g s)").bitcast(F32),
                                                   scalar=low_rows[:, 0:1],
                                                   in1=q_strips[:, :, :].rearrange("p g s -> p (g s)"),
                                                   op0=ALU.mult, op1=ALU.add).then_inc(q.qk_sb, 1)
                else:
                    dve.wait_ge(q.q_hi_sb, b + 1)
                    nc.vector.scalar_tensor_tensor(out=qT[u][:, :, :].rearrange("p g s -> p (g s)"),
                                                   in0=qhi[:, :, :].rearrange("p g s -> p (g s)").bitcast(F32),
                                                   scalar=low_rows[:, 0:1], in1=Q1[:, :], op0=ALU.mult, op1=ALU.add
                                                   ).then_inc(q.q_sb, 1)
                    dve.wait_ge(q.k_hi_sb, b + 1)
                    nc.vector.tensor_tensor(kB[u][:, :, :].rearrange("p g s -> p (g s)"), KV[:, :],
                                            kA[u][:, :, :].rearrange("p g s -> p (g s)").bitcast(F32), ALU.subtract
                                            ).then_inc(q.qk_sb, 1)

            def maxima(i, u, ch):
                b = i * 2 + u
                for m, j in enumerate(BANK_ORDER):
                    dve.wait_ge(q.s_ps, b * NJ + m + 1)
                    nc.vector.tensor_reduce(negmax[u][:, j, :], S_BANKS[j][:, :].rearrange("p (g s) -> p g s", g=HS),
                                            AX_X, ALU.max, negate=True).then_inc(q.max_sb, 1)

            def output(i, u, ch):
                b = i * 2 + u
                dve.wait_ge(q.pv_ps, b * NJ + NJ + AHEAD)
                sums = O[:, 0:H * (DH + 1)].rearrange("p (h e) -> p h e", h=H)
                ch.link(nc.vector.reciprocal(rinv[u][:, :], sums[:, :, DH]))
                if layer == 0:
                    dve.wait_ge(q.o_out[u], i * 16 + FIRST_DMA)
                nc.vector.tensor_tensor(osb[u][:, :, :], sums[:, :, 0:DH],
                                        rinv[u][:, :].rearrange("p (h o) -> p h o", o=1).broadcast_to((128, H, DH)),
                                        ALU.mult).then_inc(q.o_sb, 1)

            def take_turned_out(i, u):
                b = i * 2 + u
                dve.wait_ge(q.ot_ps, b + 1)
                nc.vector.tensor_copy(oT[u][:, :, :].rearrange("p k s -> p (k s)"), XQ[:, 0:D]).then_inc(q.ot_sb, 1)

            def take_out(i, u):
                b = i * 2 + u
                dve.wait_ge(q.y_ps, b + 1)
                nc.vector.tensor_tensor(proj[u][:, :], XQ[:, D:2 * D], bo[:, :], ALU.add).then_inc(q.y_sb, 1)
                dve.wait_ge(q.y_sb, b + 1 + FIRST)
                xrow = r.X[:, bass.ds(b, 1), :].rearrange("p o d -> p (o d)")
                nc.vector.scalar_tensor_tensor(out=xrow, in0=proj[u][:, :], scalar=r.gates[:, 1:2], in1=xrow,
                                               op0=ALU.mult, op1=ALU.add)

            per_batch = 3 if layer == 0 else 1

            def turn(i, first_turn=False, last_turn=False):
                for u in range(2):
                    ch = Chain(dve, q.chain, (i * 2 + u) * per_batch + setup + prepared)
                    more = not (last_turn and u == 1)
                    out = layer == 1 and not (first_turn and u == 0)
                    after, before = (i + u, 1 - u), (i - 1 + u, 1 - u)
                    if more:
                        take_x(*after)
                    maxima(i, u, ch)
                    if more:
                        take_context(*after, ch)
                    if out:
                        take_turned_out(*before)
                    if more:
                        take_tokens(*after, ch)
                    if out:
                        take_out(*before)
                    if not last_turn:
                        prepare_early(i + 1, u, ch)
                    output(i, u, ch)
                    assert last_turn or ch.n == per_batch

            ch = Chain(dve, q.chain, setup)
            prepare_early(0, 0, ch)
            take_x(0, 0)
            take_context(0, 0, ch)
            take_tokens(0, 0, ch)
            prepare_early(0, 1, ch)
            prepared = ch.n
            turn(0, first_turn=True)
            with dve.Fori(1, B // 2 - 1) as i:
                turn(i)
            turn(B // 2 - 1, last_turn=True)
            if layer == 0:
                dve.wait_ge(q.o_sb, B + FIRST)
            else:
                take_turned_out(B // 2 - 1, 1)
                take_out(B // 2 - 1, 1)


E0, F0, CAP, RH = 16, 512, 64, 128
KF0 = F0 // 128
TIE = 2.0 ** -100


def router0_phase(nc, r, a, R, W):
    NB, NT = 4, B // 4
    with ExitStack() as ctx:
        def sb(name, shape, dt=F32):
            return ctx.enter_context(nc.sbuf_tensor("r0_" + name, shape, dt))

        def sem(name):
            return ctx.enter_context(nc.semaphore("r0_" + name))

        w1 = sb("w1", [128, KD, RH])
        w2 = sb("w2", [RH, E0])
        tie = sb("tie", [128, S])
        ones = sb("ones", [128, 128])
        xb = sb("xb", [128, NB, D])
        xT = sb("xT", [128, KD, NB * S])
        hid = sb("hid", [RH, NB * S])
        negmax = sb("negmax", [E0, NB])
        ex = sb("ex", [E0, NB, S])
        sums = sb("sums", [E0, NB])
        rs = sb("rs", [E0, NB])
        probs = sb("probs", [E0, NB, S])
        row = [sb(f"row{v}", [128, E0, NB * S]) for v in range(2)]
        col = [sb(f"col{v}", [128, NB, E0]) for v in range(2)]
        taken = sb("taken", [128, NB, E0])
        total = sb("total", [128, NB, E0])
        inv = sb("inv", [128, NB, E0])
        p_dram = nc.dram_tensor("r0_p_dram", (NT * E0 * NB * S,), F32, kind="Internal").ap()
        (w_in, consts, xb_sb, xt_ps, xt_sb, h_ps, h_sb, l_ps, max_sb, ex_sb, probs_sb, p_out, row_in, col_ps, taken_sb,
         total_ps, chain, copied) = (sem(n) for n in (
             "w_in", "consts", "xb_sb", "xt_ps", "xt_sb", "h_ps", "h_sb", "l_ps", "max_sb", "ex_sb", "probs_sb",
             "p_out", "row_in", "col_ps", "taken_sb", "total_ps", "dve_chain", "copied"))
        banks = r.banks
        block = ctx.enter_context(nc.Block())

        @block.sync
        def _(sp):
            sp.dma_start(w1[:, :, :], a["L0_ffn_router_w1"].rearrange("(k p) n -> p k n", p=128)).then_inc(w_in, 16)
            sp.dma_start(w2[:, :], a["L0_ffn_router_w2"]).then_inc(w_in, 16)
            for t in range(NT):
                sp.wait_ge(probs_sb, t + 1)
                pd = p_dram[t * E0 * NB * S:(t + 1) * E0 * NB * S]
                sp.dma_start(pd.rearrange("(e n) -> e n", e=E0), probs[:, :, :].rearrange("e b s -> e (b s)")
                             ).then_inc(p_out, 16)
                sp.wait_ge(p_out, t * 16 + 16)
                if t >= 2:
                    sp.wait_ge(taken_sb, t - 1)
                sp.dma_start(row[t % 2][:, :, :].rearrange("p e n -> p (e n)"), pd.partition_broadcast(128)
                             ).then_inc(row_in, 16)

        @block.gpsimd
        def _(pool):
            nc.gpsimd.memset(tie[:, :], -TIE).then_inc(consts, 1)
            nc.gpsimd.memset(ones[:, :], 1.0).then_inc(consts, 1)
            nc.gpsimd.memset(R[:, :, :], 0.0).then_inc(consts, 1)
            nc.gpsimd.memset(W[:, :, :], 0.0).then_inc(consts, 1)
            pool.wait_ge(consts, 4)
            nc.gpsimd.affine_select(out=tie[:, :], in_=tie[:, :], compare_op=ALU.is_gt, fill=0.0, base=0,
                                    pattern=[[-1, S]], channel_multiplier=1).then_inc(consts, 1)
            for t in range(NT):
                pool.wait_ge(xb_sb, t + 1)
                nc.gpsimd.tensor_copy(r.XN[:, t * NB:(t + 1) * NB, :], xb[:, :, :]).then_inc(copied, 1)

        @block.tensor
        def _(pe):
            pe.wait_ge(w_in, 32)
            pe.wait_ge(consts, 5)

            def sum_taken(t):
                pe.wait_ge(taken_sb, t + 1)
                nc.tensor.matmul(banks[5][:, 0:NB * E0], ones[:, :], taken[:, :, :].rearrange("p b e -> p (b e)"),
                                 start=True, stop=True).then_inc(total_ps, 1)

            for t in range(NT):
                pe.wait_ge(xb_sb, t + 1)
                for k in range(KD):
                    for n in range(NB):
                        last = nc.tensor.transpose(banks[k][:, n * S:(n + 1) * S], xb[:, n, k * 128:(k + 1) * 128],
                                                   r.ident[:, :])
                last.then_inc(xt_ps, 1)
                pe.wait_ge(xt_sb, t + 1)
                for k in range(KD):
                    last = nc.tensor.matmul(banks[2][:, :], w1[:, k, :], xT[:, k, :], start=k == 0, stop=k == KD - 1)
                last.then_inc(h_ps, 1)
                pe.wait_ge(h_sb, t + 1)
                nc.tensor.matmul(banks[3][0:E0, :], w2[:, :], hid[:, :], start=True, stop=True).then_inc(l_ps, 1)
                pe.wait_ge(probs_sb, t + 1)
                for n in range(NB):
                    last = nc.tensor.transpose(banks[4][:, n * E0:(n + 1) * E0], probs[:, n, :], r.ident[0:E0, 0:E0])
                last.then_inc(col_ps, 1)
                if t >= 2:
                    sum_taken(t - 2)
            sum_taken(NT - 2)
            sum_taken(NT - 1)

        @block.scalar
        def _(act):
            for t in range(NT):
                act.wait_ge(h_ps, t + 1)
                nc.scalar.activation(hid[:, :], banks[2][:, :], ACT.Silu).then_inc(h_sb, 1)
                act.wait_ge(max_sb, t + 1)
                for n in range(NB):
                    last = nc.scalar.activation(ex[:, n, :], banks[3][0:E0, n * S:(n + 1) * S], ACT.Exp,
                                                bias=negmax[:, n:n + 1], accum_out=sums[:, n:n + 1])
                last.then_inc(ex_sb, 1)

        @block.vector
        def _(dve):
            dve.wait_ge(consts, 5)
            ch = Chain(dve, chain)

            def layernorm(t):
                if t > 0:
                    dve.wait_ge(copied, t)
                for n in range(NB):
                    b = t * NB + n
                    last = nc.vector.tensor_scalar(xb[:, n, :], r.X[:, b, :], r.mv[:, b, 0:1], r.rstd[:, b:b + 1],
                                                   ALU.subtract, ALU.mult)
                last.then_inc(xb_sb, 1)

            def take_transpose(t):
                dve.wait_ge(xt_ps, t + 1)
                for k in range(KD):
                    last = nc.vector.tensor_copy(xT[:, k, :], banks[k][:, :])
                last.then_inc(xt_sb, 1)

            def maxima(t):
                dve.wait_ge(l_ps, t + 1)
                nc.vector.tensor_reduce(negmax[:, :], banks[3][0:E0, :].rearrange("e (b s) -> e b s", b=NB), AX_X,
                                        ALU.max, negate=True).then_inc(max_sb, 1)

            def probabilities(t):
                dve.wait_ge(ex_sb, t + 1)
                ch.link(nc.vector.reciprocal(rs[:, :], sums[:, :]))
                if t > 0:
                    dve.wait_ge(p_out, t * 16)
                nc.vector.tensor_tensor(probs[:, :, :], ex[:, :, :], rs[:, :].rearrange("e (b o) -> e b o", o=1)
                                        .broadcast_to((E0, NB, S)), ALU.mult).then_inc(probs_sb, 1)

            def ranks(t, pairs):
                dve.wait_ge(row_in, t * 16 + 16)
                for n, e in pairs:
                    cell = row[t % 2][:, e, n * S:(n + 1) * S]
                    last = nc.vector.scalar_tensor_tensor(
                        out=cell, in0=cell, scalar=col[t % 2][:, n, e:e + 1], in1=tie[:, :],
                        op0=ALU.subtract, op1=ALU.is_gt, accum_out=R[:, t * NB + n, e:e + 1])
                return last

            def take(t):
                batches = slice(t * NB, (t + 1) * NB)
                nc.vector.scalar_tensor_tensor(out=taken[:, :, :], in0=R[:, batches, 0:E0],
                                               scalar=float(CAP), in1=col[t % 2][:, :, :], op0=ALU.is_lt, op1=ALU.mult
                                               ).then_inc(taken_sb, 1)

            def weights(t):
                batches = slice(t * NB, (t + 1) * NB)
                dve.wait_ge(total_ps, t + 1)
                ch.link(nc.vector.tensor_scalar(total[:, :, :].rearrange("p b e -> p (b e)"), banks[5][:, 0:NB * E0],
                                                1e-9, None, ALU.add))
                ch.link(nc.vector.reciprocal(inv[:, :, :], total[:, :, :]))
                nc.vector.tensor_tensor(W[:, batches, 0:E0], taken[:, :, :], inv[:, :, :], ALU.mult)

            pairs = [(n, e) for n in range(NB) for e in range(E0)]
            shares = (pairs[0:8], pairs[8:16], pairs[16:24], pairs[24:])
            for t in range(-2, NT):
                for share, stage in zip(shares, (layernorm, take_transpose, maxima, probabilities)):
                    if t + 2 < NT:
                        stage(t + 2)
                    if t >= 0:
                        counted = ranks(t, share)
                if t >= 0:
                    ch.link(counted)
                    take(t)
                if t + 2 < NT:
                    dve.wait_ge(col_ps, t + 3)
                    if t >= 0:
                        dve.wait_ge(taken_sb, t + 1)
                    ch.link(nc.vector.tensor_copy(col[t % 2][:, :, :].rearrange("p b e -> p (b e)"),
                                                  banks[4][:, 0:NB * E0]))
                if t >= 0:
                    weights(t)


def experts0_phase(nc, r, a, R, W, xs_dram):
    NH, NPAIR, SLOTS = 2, 4, 8 * CAP
    NQ, NF = NH * NPAIR, NH * KF0
    NEO = 4
    NG = 4
    NB = B // NG
    GATHER_AT = (0, 2, 4, 6)
    with ExitStack() as ctx:
        def sb(name, shape, dt=F32):
            return ctx.enter_context(nc.sbuf_tensor("e0_" + name, shape, dt))

        def sem(name):
            return ctx.enter_context(nc.semaphore("e0_" + name))

        def parts(name, shape):
            return [sb(f"{name}_{part}", shape, F32R) for part in ("hi", "lo")]

        w_raw = [sb(f"w{n}", [128, KD * F0]) for n in range(3)]
        w_parts = [[parts(f"w{n}_{v}", [128, KD * F0]) for n in range(3)] for v in range(2)]
        slot = sb("slot", [128, 1, CAP])
        pick = sb("pick", [128, 2, B, CAP])
        pickT = [sb(f"pickT{v}", [128, NQ, S], F32R) for v in range(2)]
        weight = [sb(f"weight{v}", [128, NQ]) for v in range(2)]
        xg = parts("xg", [128, KD, B * 2 * CAP])
        sg = [sb(f"sg{n}", [128, SLOTS]) for n in range(2)]
        hid = [sb(f"hid{n}", [128, SLOTS]) for n in range(2)]
        hidden = parts("hidden", [128, NF, SLOTS])
        eo = [parts(f"eo{n}", [128, D]) for n in range(NEO)]
        zero = sb("zero", [128, D])
        (made, pick_sb, xg_ps, xg_hi, xg_sb, put_ps, putT_sb, g_ps, sg_sb, u_ps, hid_sb, hi_sb, hidden_sb, eo_ps, eo_hi, eo_sb,
         sum_ps, acc_sb, w_in, w_hi, w_sb) = (sem(n) for n in (
             "made", "pick_sb", "xg_ps", "xg_hi", "xg_sb", "put_ps", "putT_sb", "g_ps", "sg_sb", "u_ps", "hid_sb", "hi_sb",
             "hidden_sb", "eo_ps", "eo_hi", "eo_sb", "sum_ps", "acc_sb", "w_in", "w_hi", "w_sb"))
        zero_made, cleared = sem("zero_made"), sem("cleared")
        A_SG, A_HID, A_EO, A_SUM, A_ACC, A_EOPS, A_PUT = 1, 1, 2, NEO, 1, 2 * NQ, 1
        G_BANK, U_BANK, XK, EO, OUT = r.banks[2], r.banks[3], r.banks[0:2], r.banks[4:6], r.banks[6:8]
        WEIGHTS = U_BANK[:, 0:2 * NQ]
        block = ctx.enter_context(nc.Block())

        @block.sync
        def _(sp):
            def load(e):
                for t, name in zip(w_raw, ("L0_ffn_w1", "L0_ffn_w2", "L0_ffn_w3")):
                    src = a[name][bass.ds(e, 1), :, :].rearrange("o (k p) n -> p (o k) n", p=128)
                    sp.dma_start(t[:, :].rearrange("p (k n) -> p k n", n=src.shape[2]), src).then_inc(w_in, 16)

            load(0)
            with sp.Fori(0, E0 - 1) as e:
                sp.wait_ge(w_sb, e * 3 + 3)
                sp.sem_inc(r.held, 1)
                load(e + 1)

        @block.gpsimd
        def _(pool):
            nc.gpsimd.iota(slot[:, :, :], pattern=[[0, 1], [1, CAP]], base=0, channel_multiplier=0,
                           allow_small_or_imprecise_dtypes=True).then_inc(made, 1)
            nc.gpsimd.memset(zero[:, :], 0.0).then_inc(zero_made, 1)
            pool.wait_ge(zero_made, 1)
            pool.dma_start(xs_dram.rearrange("(t p) d -> p t d", p=TT),
                           zero[:, :].rearrange("p (o d) -> p o d", o=1).broadcast_to((128, TILES, D))).then_inc(cleared, 16)
            with pool.Fori(0, E0 // 2) as i:
                for v in range(2):
                    e = i * 2 + v
                    pool.wait_ge(w_in, e * 48 + 48)
                    pool.wait_ge(eo_ps, (e - 1) * NQ + A_EOPS)
                    pool.sem_inc(r.held, 1)
                    for n in range(3):
                        nc.gpsimd.tensor_copy(w_parts[v][n][0][:, :], w_raw[n][:, :]).then_inc(w_hi, 1)
                    for n in range(3):
                        pool.wait_ge(w_hi, e * 3 + n + 1)
                        nc.gpsimd.tensor_tensor(w_parts[v][n][1][:, :], w_raw[n][:, :], w_parts[v][n][0][:, :].bitcast(F32),
                                                ALU.subtract).then_inc(w_sb, 1)
            pool.wait_ge(cleared, 16)

        @block.tensor
        def _(pe):
            def gather(i, g):
                if g == 0:
                    pe.wait_ge(pick_sb, i * 2 + 2)
                else:
                    pe.wait_ge(xg_sb, i * 2 * NG + 2 * g)
                for k in range(KD):
                    for n in range(NB):
                        b = g * NB + n
                        last = nc.tensor.matmul(XK[k][:, n * 2 * CAP:(n + 1) * 2 * CAP].rearrange("p (v c) -> p v c", v=2),
                                                r.XN[:, b, k * 128:(k + 1) * 128], pick[:, :, b, :], start=True, stop=True)
                last.then_inc(xg_ps, 1)

            def slot_weights(i, v):
                e = i * 2 + v
                pe.wait_ge(hid_sb, e * NF + A_HID)
                for q in range(NQ):
                    pair = pick[:, v, 2 * q:2 * q + 2, :].rearrange("p b c -> p (b c)")
                    nc.tensor.matmul(WEIGHTS[:, 2 * q:2 * q + 2], pair,
                                     W[:, 2 * q:2 * q + 2, bass.ds(e, 1)].rearrange("p b o -> p (b o)"),
                                     start=True, stop=True)

            def turn_over(i, v):
                if v == 0:
                    pe.wait_ge(xg_sb, (i + 1) * 2 * NG)
                for q in range(NQ):
                    pair = pick[:, v, 2 * q:2 * q + 2, :].rearrange("p b c -> p (b c)")
                    last = nc.tensor.transpose(XK[q // 4][:, (q % 4) * S:(q % 4 + 1) * S], pair, r.ident[:, :])
                last.then_inc(put_ps, 1)

            def up(e, v, h):
                for f in range(KF0):
                    n = e * NF + h * KF0 + f
                    for m, (free, bank, full) in enumerate(((sg_sb, G_BANK, g_ps), (hid_sb, U_BANK, u_ps))):
                        pe.wait_ge(free, n + A_SG)
                        if h == 0 and f == 0 and m == 1:
                            pe.wait_ge(putT_sb, e * 4 + 4 + A_PUT)
                        hi, lo = w_parts[v][m]
                        terms = [(w, x, k) for w, x in ((hi, xg[0]), (lo, xg[0]), (hi, xg[1])) for k in range(KD)]
                        for w, x, k in terms:
                            tokens = x[:, k, :].rearrange("p (b v c) -> p b v c", v=2, c=CAP)
                            last = nc.tensor.matmul(bank[:, :].rearrange("p (b c) -> p b c", c=CAP),
                                                    w[:, k * F0 + f * 128:k * F0 + (f + 1) * 128],
                                                    tokens[:, h * 2 * NPAIR:(h + 1) * 2 * NPAIR, v, :],
                                                    start=(w, x, k) == terms[0], stop=(w, x, k) == terms[-1])
                        last.then_inc(full, 1)

            def down(e, v, q):
                h, p = q // NPAIR, q % NPAIR
                n = e * NQ + q
                if p == 0:
                    pe.wait_ge(hidden_sb, e * NF + (h + 1) * KF0)
                pe.wait_ge(eo_sb, n - 1 + A_EO)
                hi, lo = w_parts[v][2]
                terms = [(x, w, f) for x, w in ((hidden[0], hi), (hidden[1], hi), (hidden[0], lo)) for f in range(KF0)]
                for x, w, f in terms:
                    last = nc.tensor.matmul(EO[q % 2][:, 0:D], x[:, h * KF0 + f, p * 128:(p + 1) * 128],
                                            w[:, f * D:(f + 1) * D],
                                            start=(x, w, f) == terms[0], stop=(x, w, f) == terms[-1])
                last.then_inc(eo_ps, 1)

            def scatter(e, v, q):
                n = e * NQ + q
                pe.wait_ge(eo_sb, n + 1 + A_EO)
                pe.wait_ge(acc_sb, n + A_ACC)
                for t in range(2):
                    rows = slice(t * CAP, (t + 1) * CAP)
                    hi, lo = eo[q % NEO]
                    for part in (hi, lo):
                        last = nc.tensor.matmul(OUT[t][:, 0:D], pickT[v][rows, q, :], part[rows, :],
                                                start=part is hi, stop=part is lo)
                last.then_inc(sum_ps, 1)

            def turn(i, last_turn):
                for v in range(2):
                    e = i * 2 + v
                    more = not (last_turn and v == 1)
                    pe.wait_ge(w_sb, e * 3 + 3)
                    if v == 0:
                        pe.wait_ge(xg_sb, (i + 1) * 2 * NG)
                    for h in range(NH):
                        up(e, v, h)
                    for q in range(NQ):
                        if more and v == 1 and q in GATHER_AT:
                            gather(i + 1, GATHER_AT.index(q))
                        down(e, v, q)
                        if q >= 2:
                            scatter(e, v, q - 2)
                    if more:
                        slot_weights(i + v, 1 - v)
                    scatter(e, v, NQ - 2)
                    if more:
                        turn_over(i + v, 1 - v)
                    scatter(e, v, NQ - 1)

            pe.wait_ge(made, 1)
            pe.sem_inc(putT_sb, A_PUT)
            for g in range(NG):
                gather(0, g)
            slot_weights(0, 0)
            turn_over(0, 0)
            with pe.Fori(0, E0 // 2 - 1) as i:
                turn(i, False)
            turn(E0 // 2 - 1, True)

        @block.scalar
        def _(act):
            for s, ahead in ((sg_sb, A_SG), (eo_sb, A_EO), (hid_sb, A_HID), (sum_ps, A_SUM), (acc_sb, A_ACC),
                             (eo_ps, A_EOPS)):
                act.sem_inc(s, ahead)

            def take_tokens(i, g):
                act.wait_ge(xg_ps, i * NG + g + 1)
                for k in range(KD):
                    nc.scalar.copy(xg[0][:, k, g * SLOTS:(g + 1) * SLOTS], XK[k][:, :]).then_inc(xg_hi, 1)

            def take_one_hots(e, v):
                act.wait_ge(put_ps, e + 1)
                nc.scalar.copy(pickT[v][:, 0:4, :].rearrange("p q s -> p (q s)"), XK[0][:, :]).then_inc(putT_sb, 1)

            def turn(i, last_turn):
                for v in range(2):
                    e = i * 2 + v
                    more = not (last_turn and v == 1)
                    for f in range(NF):
                        n = e * NF + f
                        act.wait_ge(g_ps, n + 1)
                        nc.scalar.activation(sg[f % 2][:, :], G_BANK[:, :], ACT.Silu).then_inc(sg_sb, 1)
                        act.wait_ge(hid_sb, n + 1 + A_HID)
                        nc.scalar.copy(hidden[0][:, f, :], hid[f % 2][:, :]).then_inc(hi_sb, 1)
                    for q in range(NQ):
                        if more and v == 1 and q in GATHER_AT:
                            take_tokens(i + 1, GATHER_AT.index(q))
                        n = e * NQ + q
                        act.wait_ge(eo_ps, n + 1 + A_EOPS)
                        act.wait_ge(sum_ps, n - NEO + 1 + A_SUM)
                        nc.scalar.activation(eo[q % NEO][0][:, :], EO[q % 2][:, 0:D], ACT.Copy, scale=weight[v][:, q:q + 1]
                                             ).then_inc(eo_hi, 1)
                    if more:
                        take_one_hots(e + 1, 1 - v)

            for g in range(NG):
                take_tokens(0, g)
            take_one_hots(0, 0)
            with act.Fori(0, E0 // 2 - 1) as i:
                turn(i, False)
            turn(E0 // 2 - 1, True)

        @block.vector
        def _(dve):
            dve.wait_ge(made, 1)

            def one_hots(i):
                for v in range(2):
                    rank = R[:, :, bass.ds(i * 2 + v, 1)].broadcast_to((128, B, CAP))
                    nc.vector.tensor_tensor(pick[:, v, :, :], slot[:, :, :].broadcast_to((128, B, CAP)), rank, ALU.is_equal
                                            ).then_inc(pick_sb, 1)

            def take_tokens(i, g):
                part = slice(g * SLOTS, (g + 1) * SLOTS)
                for k in range(KD):
                    dve.wait_ge(xg_hi, i * 2 * NG + g * 2 + k + 1)
                    nc.vector.tensor_tensor(xg[1][:, k, part], XK[k][:, :], xg[0][:, k, part].bitcast(F32), ALU.subtract
                                            ).then_inc(xg_sb, 1)

            def take_one_hots(e, v):
                dve.wait_ge(put_ps, e + 1)
                nc.vector.tensor_copy(pickT[v][:, 4:8, :].rearrange("p q s -> p (q s)"), XK[1][:, :]).then_inc(putT_sb, 1)
                for t in range(2):
                    rows = slice(t * CAP, (t + 1) * CAP)
                    nc.vector.tensor_copy(weight[v][rows, :], WEIGHTS[rows, :].rearrange("p (q t) -> p q t", t=2)[:, :, t]
                                          ).then_inc(putT_sb, 1)

            def add(e, q):
                dve.wait_ge(sum_ps, e * NQ + q + 1 + A_SUM)
                for t in range(2):
                    b = 2 * q + t
                    last = nc.vector.scalar_tensor_tensor(out=r.X[:, b, :], in0=OUT[t][:, 0:D], scalar=r.gates[:, 2:3],
                                                          in1=r.X[:, b, :], op0=ALU.mult, op1=ALU.add)
                last.then_inc(acc_sb, 1)

            def turn(i, last_turn):
                for v in range(2):
                    e = i * 2 + v
                    more = not (last_turn and v == 1)
                    if more and v == 1:
                        one_hots(i + 1)
                    for f in range(NF):
                        n = e * NF + f
                        dve.wait_ge(u_ps, n + 1)
                        dve.wait_ge(sg_sb, n + 1 + A_SG)
                        nc.vector.tensor_tensor(hid[f % 2][:, :], sg[f % 2][:, :], U_BANK[:, :], ALU.mult
                                                ).then_inc(hid_sb, 1)
                        dve.wait_ge(hi_sb, n + 1)
                        nc.vector.tensor_tensor(hidden[1][:, f, :], hid[f % 2][:, :], hidden[0][:, f, :].bitcast(F32),
                                                ALU.subtract).then_inc(hidden_sb, 1)
                    for q in range(NQ):
                        if more and v == 1 and q in GATHER_AT:
                            take_tokens(i + 1, GATHER_AT.index(q))
                        n = e * NQ + q
                        if q >= 2:
                            add(e, q - 2)
                        dve.wait_ge(eo_hi, n + 1)
                        nc.vector.scalar_tensor_tensor(out=eo[q % NEO][1][:, :], in0=EO[q % 2][:, 0:D],
                                                       scalar=weight[v][:, q:q + 1], in1=eo[q % NEO][0][:, :].bitcast(F32),
                                                       op0=ALU.mult, op1=ALU.subtract).then_inc(eo_sb, 1)
                    add(e, NQ - 2)
                    if more:
                        take_one_hots(e + 1, 1 - v)
                    add(e, NQ - 1)
                    dve.wait_ge(acc_sb, (e + 1) * NQ + A_ACC)

            one_hots(0)
            for g in range(NG):
                take_tokens(0, g)
            take_one_hots(0, 0)
            with dve.Fori(0, E0 // 2 - 1) as i:
                turn(i, False)
            turn(E0 // 2 - 1, True)


E1, F1, TOPK, FS = 32, 192, 4, 512
FH = F1 // 2
KFS = FS // 128
TT = 128
TILES = -(-((B * S * TOPK + E1 * (TT - 1)) // TT) // 4) * 4


def router1_phase(nc, r, a, LG, xT):
    NB, NT = 4, B // 4
    with ExitStack() as ctx:
        wr = ctx.enter_context(nc.sbuf_tensor("r1_wr", [128, KD, E1 + 1], F32))
        w_in, xb_sb, xt_ps, xt0_sb, xt1_sb, l_ps = (ctx.enter_context(nc.semaphore("r1_" + n)) for n in (
            "w_in", "xb_sb", "xt_ps", "xt0_sb", "xt1_sb", "l_ps"))
        XK, LOG = (r.banks[0:2], r.banks[2:4]), r.banks[4:8]
        block = ctx.enter_context(nc.Block())

        @block.sync
        def _(sp):
            sp.dma_start(wr[:, :, :], a["L1_router_and_gate_w"].rearrange("(k p) n -> p k n", p=128)).then_inc(w_in, 16)

        @block.tensor
        def _(pe):
            def turn_over(t):
                pe.wait_ge(xb_sb, t + 1)
                if t >= 2:
                    pe.wait_ge(xt0_sb, t - 1)
                    pe.wait_ge(xt1_sb, t - 1)
                for k in range(KD):
                    for n in range(NB):
                        last = nc.tensor.transpose(XK[t % 2][k][:, n * S:(n + 1) * S],
                                                   r.XN[:, t * NB + n, k * 128:(k + 1) * 128], r.ident[:, :])
                last.then_inc(xt_ps, 1)

            turn_over(0)
            pe.wait_ge(w_in, 16)
            for t in range(NT):
                if t + 1 < NT:
                    turn_over(t + 1)
                pe.wait_ge(xt0_sb, t + 1)
                pe.wait_ge(xt1_sb, t + 1)
                for n in range(NB):
                    for k in range(KD):
                        last = nc.tensor.matmul(LOG[t][:, n * (E1 + 1):(n + 1) * (E1 + 1)],
                                                xT[:, k, (t * NB + n) * S:(t * NB + n + 1) * S],
                                                wr[:, k, :], start=k == 0, stop=k == KD - 1)
                last.then_inc(l_ps, 1)

        @block.scalar
        def _(act):
            for t in range(NT):
                act.wait_ge(xt_ps, t + 1)
                nc.scalar.copy(xT[:, 1, t * NB * S:(t + 1) * NB * S], XK[t % 2][1][:, :]).then_inc(xt1_sb, 1)

        @block.vector
        def _(dve):
            for t in range(NT):
                for n in range(NB):
                    b = t * NB + n
                    last = nc.vector.tensor_scalar(r.XN[:, b, :], r.X[:, b, :], r.mv[:, b, 0:1], r.rstd[:, b:b + 1],
                                                   ALU.subtract, ALU.mult)
                last.then_inc(xb_sb, 1)
                if t > 0:
                    dve.wait_ge(xt_ps, t)
                    nc.vector.tensor_copy(xT[:, 0, (t - 1) * NB * S:t * NB * S], XK[(t - 1) % 2][0][:, :]).then_inc(xt0_sb, 1)
            dve.wait_ge(xt_ps, NT)
            nc.vector.tensor_copy(xT[:, 0, (NT - 1) * NB * S:], XK[(NT - 1) % 2][0][:, :]).then_inc(xt0_sb, 1)
            for t in range(NT):
                dve.wait_ge(l_ps, t + 1)
                nc.vector.tensor_copy(LG[:, t * NB:(t + 1) * NB, :],
                                      LOG[t][:, 0:NB * (E1 + 1)].rearrange("p (b e) -> p b e", b=NB))


def dispatch1_phase(nc, r, a, LG, xT, w4, slots, sig, tile_expert, xs_dram, SH):
    with ExitStack() as ctx:
        def sb(name, shape, dt=F32):
            return ctx.enter_context(nc.sbuf_tensor("d1_" + name, shape, dt))

        def sem(name):
            return ctx.enter_context(nc.semaphore("d1_" + name))

        negmax = sb("negmax", [128, B])
        ex = sb("ex", [128, B, E1])
        sums = sb("sums", [128, B])
        rs = sb("rs", [128, B])
        probs = sb("probs", [128, B, E1])
        ez = sb("ez", [128, B])
        ez1 = sb("ez1", [128, B])
        top = sb("top", [128, B, 8])
        top_at = sb("top_at", [128, B, 8], mybir.dt.uint32)
        at = sb("at", [128, B, TOPK])
        s4 = sb("s4", [128, B])
        i4 = sb("i4", [128, B])
        expert = sb("expert", [128, B, E1])
        choice = [sb(f"choice{k}", [128, B, E1]) for k in range(TOPK)]
        member = sb("member", [128, B, E1])
        earlier = sb("earlier", [128, 128])
        ones = sb("ones", [128, 128])
        before = sb("before", [128, B, E1])
        totals = sb("totals", [128, B, E1])
        upto = sb("upto", [128, B + 1, E1])
        edge = sb("edge", [128, E1, B * S // TT])
        over = sb("over", [128, E1, B * S // TT])
        ntiles = sb("ntiles", [128, E1])
        zeros = sb("zeros", [128, E1])
        ends = sb("ends", [128, E1])
        first = sb("first", [128, E1])
        slot = sb("slot", [128, B, E1])
        mine = sb("mine", [128, B, E1])
        slotf = sb("slotf", [128, TOPK, B])
        tile_at = sb("tile_at", [128, 1])
        done = sb("done", [128, E1])
        te = sb("te", [128, 1])
        (made, max_sb, ex_sb, mem_sb, cnt_ps, te_sb, te_ps, slots_sb, sent, chain) = (sem(n) for n in (
            "made", "max_sb", "ex_sb", "mem_sb", "cnt_ps", "te_sb", "te_ps", "slots_sb", "sent", "dve_chain"))
        BEFORE, TOTALS, TE = r.banks[0], r.banks[1], r.banks[2]
        NB, NT = 4, B // 4
        wg = sb("wg", [128, KD, FS])
        wu = sb("wu", [128, KD, FS])
        wd = sb("wd", [128, KFS, D])
        sg = [sb(f"sg{n}", [128, NB * S]) for n in range(2)]
        hidden = sb("hidden", [128, KFS, NB * S])
        w_in, g_ps, sg_sb, u_ps, hid_sb, y_ps, y_sb = (sem(n) for n in (
            "w_in", "g_ps", "sg_sb", "u_ps", "hid_sb", "y_ps", "y_sb"))
        A_SG, A_HID, A_Y = 1, 2, 2
        G_BANK, U_BANK, Y = r.banks[3], r.banks[4], r.banks[5:7]
        block = ctx.enter_context(nc.Block())

        @block.gpsimd
        def _(pool):
            def iota(t, pattern, multiplier=0):
                nc.gpsimd.iota(t, pattern=pattern, base=0, channel_multiplier=multiplier,
                               allow_small_or_imprecise_dtypes=True).then_inc(made, 1)

            iota(expert[:, :, :], [[0, B], [1, E1]])
            iota(edge[:, :, :], [[0, E1], [TT, B * S // TT]])
            iota(tile_at[:, :], [[0, 1]], 1)
            nc.gpsimd.memset(ones[:, :], 1.0).then_inc(made, 1)
            nc.gpsimd.memset(earlier[:, :], 1.0).then_inc(made, 1)
            nc.gpsimd.memset(zeros[:, :], 0.0).then_inc(made, 1)
            pool.wait_ge(made, 6)
            nc.gpsimd.affine_select(out=earlier[:, :], in_=earlier[:, :], compare_op=ALU.is_gt, fill=0.0, base=0,
                                    pattern=[[1, 128]], channel_multiplier=-1).then_inc(made, 1)
            pool.wait_ge(slots_sb, 1)
            for b in range(B):
                for k in range(TOPK):
                    nc.gpsimd.indirect_dma_start(
                        out=xs_dram[:, :], out_offset=bass.IndirectOffsetOnAxis(ap=slots[:, b, k:k + 1], axis=0),
                        in_=r.XN[:, b, :], in_offset=None).then_inc(sent, 16)
            pool.wait_ge(sent, 16 * B * TOPK)

        @block.sync
        def _(sp):
            for t, name in ((wg, "L1_ffn_sh_gate"), (wu, "L1_ffn_sh_up"), (wd, "L1_ffn_sh_down")):
                sp.dma_start(t[:, :, :], a[name].rearrange("(k p) n -> p k n", p=128)).then_inc(w_in, 16)

        @block.scalar
        def _(act):
            for s, ahead in ((sg_sb, A_SG), (hid_sb, A_HID), (y_sb, A_Y)):
                act.sem_inc(s, ahead)
            act.wait_ge(max_sb, 1)
            nc.scalar.activation(ex[:, :, :], ex[:, :, :], ACT.Exp)
            nc.scalar.activation(ez[:, :], LG[:, :, E1], ACT.Exp, scale=-1.0).then_inc(ex_sb, 1)

            def turn(i):
                for f in range(KFS):
                    m = i * KFS + f
                    act.wait_ge(g_ps, m + 1)
                    act.wait_ge(hid_sb, m - 1 + A_HID)
                    nc.scalar.activation(sg[f % 2][:, :], G_BANK[:, :], ACT.Silu).then_inc(sg_sb, 1)
                for n in range(NB):
                    act.wait_ge(y_ps, i * NB + n + 1)
                    nc.scalar.copy(SH[:, bass.ds(i * NB + n, 1), :].rearrange("p o d -> p (o d)"), Y[n % 2][:, 0:D]
                                   ).then_inc(y_sb, 1)

            turn(0)
            with act.Fori(1, NT) as i:
                turn(i)

        @block.tensor
        def _(pe):
            def up(i):
                tokens = bass.ds(i * (NB * S), NB * S)
                for f in range(KFS):
                    m = i * KFS + f
                    pe.wait_ge(sg_sb, m + A_SG)
                    for k in range(KD):
                        last = nc.tensor.matmul(G_BANK[:, :], wg[:, k, f * 128:(f + 1) * 128], xT[:, k, tokens],
                                                start=k == 0, stop=k == KD - 1)
                    last.then_inc(g_ps, 1)
                    pe.wait_ge(hid_sb, m + A_HID)
                    for k in range(KD):
                        last = nc.tensor.matmul(U_BANK[:, :], wu[:, k, f * 128:(f + 1) * 128], xT[:, k, tokens],
                                                start=k == 0, stop=k == KD - 1)
                    last.then_inc(u_ps, 1)

            def down(i):
                pe.wait_ge(hid_sb, i * KFS + KFS + A_HID)
                for n in range(NB):
                    pe.wait_ge(y_sb, i * NB + n - 1 + A_Y)
                    for f in range(KFS):
                        last = nc.tensor.matmul(Y[n % 2][:, 0:D], hidden[:, f, n * S:(n + 1) * S], wd[:, f, :],
                                                start=f == 0, stop=f == KFS - 1)
                    last.then_inc(y_ps, 1)

            pe.wait_ge(w_in, 16 * 3)
            up(0)
            pe.wait_ge(made, 7)
            pe.wait_ge(mem_sb, 1)
            m = member[:, :, :].rearrange("p b e -> p (b e)")
            nc.tensor.matmul(BEFORE[:, :], earlier[:, :], m, start=True, stop=True)
            nc.tensor.matmul(TOTALS[:, :], ones[:, :], m, start=True, stop=True).then_inc(cnt_ps, 1)
            down(0)
            pe.wait_ge(te_sb, 1)
            nc.tensor.matmul(TE[0:1, 0:128], te[:, :], r.ident[:, :], start=True, stop=True).then_inc(te_ps, 1)
            with pe.Fori(1, NT) as i:
                up(i)
                down(i)

        @block.vector
        def _(dve):
            ch = Chain(dve, chain)
            logits = LG[:, :, 0:E1]

            def along(t, n):
                return t.rearrange("p (b o) -> p b o", o=1).broadcast_to((128, B, n))

            def gated(i, f):
                m = i * KFS + f
                dve.wait_ge(u_ps, m + 1)
                dve.wait_ge(sg_sb, m + 1 + A_SG)
                nc.vector.tensor_tensor(hidden[:, f, :], sg[f % 2][:, :], U_BANK[:, :], ALU.mult).then_inc(hid_sb, 1)

            dve.wait_ge(made, 7)
            ch.link(nc.vector.tensor_reduce(negmax[:, :], logits, AX_X, ALU.max, negate=True))
            nc.vector.tensor_tensor(ex[:, :, :], logits, along(negmax[:, :], E1), ALU.add).then_inc(max_sb, 1)
            dve.wait_ge(ex_sb, 1)
            ch.link(nc.vector.tensor_reduce(sums[:, :], ex[:, :, :], AX_X, ALU.add))
            ch.link(nc.vector.reciprocal(rs[:, :], sums[:, :]))
            nc.vector.tensor_scalar(ez1[:, :], ez[:, :], 1.0, None, ALU.add)
            ch.link(nc.vector.tensor_tensor(probs[:, :, :], ex[:, :, :], along(rs[:, :], E1), ALU.mult))
            nc.vector.reciprocal(sig[:, :], ez1[:, :])
            for b in range(B):
                last = nc.vector.max(top[:, b, :], probs[:, b, :])
            gated(0, 0)
            ch.link(last)
            for b in range(B):
                last = nc.vector.max_index(top_at[:, b, :], top[:, b, :], probs[:, b, :])
            gated(0, 1)
            ch.link(last)
            nc.vector.tensor_reduce(s4[:, :], top[:, :, 0:TOPK], AX_X, ALU.add)
            ch.link(nc.vector.tensor_copy(at[:, :, :], top_at[:, :, 0:TOPK]))
            nc.vector.reciprocal(i4[:, :], s4[:, :])
            for k in range(TOPK):
                last = nc.vector.tensor_tensor(choice[k][:, :, :], expert[:, :, :],
                                               at[:, :, k:k + 1].broadcast_to((128, B, E1)), ALU.is_equal)
            ch.link(last)
            nc.vector.tensor_tensor(w4[:, :, :], top[:, :, 0:TOPK], along(i4[:, :], TOPK), ALU.mult)
            ch.link(nc.vector.tensor_tensor(member[:, :, :], choice[0][:, :, :], choice[1][:, :, :], ALU.add))
            ch.link(nc.vector.tensor_tensor(member[:, :, :], member[:, :, :], choice[2][:, :, :], ALU.add))
            nc.vector.tensor_tensor(member[:, :, :], member[:, :, :], choice[3][:, :, :], ALU.add).then_inc(mem_sb, 1)
            gated(0, 2)
            gated(0, 3)
            ch.link(nc.vector.tensor_copy(upto[:, 0, :], zeros[:, :]))
            dve.wait_ge(cnt_ps, 1)
            nc.vector.tensor_copy(before[:, :, :].rearrange("p b e -> p (b e)"), BEFORE[:, :])
            ch.link(nc.vector.tensor_copy(totals[:, :, :].rearrange("p b e -> p (b e)"), TOTALS[:, :]))
            for b in range(B):
                ch.link(nc.vector.tensor_tensor(upto[:, b + 1, :], upto[:, b, :], totals[:, b, :], ALU.add))
            count = upto[:, B, :].rearrange("p (e o) -> p e o", o=1).broadcast_to((128, E1, B * S // TT))
            ch.link(nc.vector.tensor_tensor(over[:, :, :], count, edge[:, :, :], ALU.is_gt))
            ch.link(nc.vector.tensor_reduce(ntiles[:, :], over[:, :, :], AX_X, ALU.add))
            ch.link(nc.vector.tensor_tensor_scan(ends[:, :], ntiles[:, :], zeros[:, :], 0.0, ALU.add, ALU.add))
            ch.link(nc.vector.tensor_scalar(done[:, :], ends[:, :], tile_at[:, 0:1], None, ALU.is_le))
            ch.link(nc.vector.tensor_reduce(te[:, :], done[:, :], AX_X, ALU.add))
            nc.vector.tensor_scalar(te[:, :], te[:, :], float(E1 - 1), None, ALU.min).then_inc(te_sb, 1)
            ch.link(nc.vector.tensor_tensor(first[:, :], ends[:, :], ntiles[:, :], ALU.subtract))
            ch.link(nc.vector.tensor_scalar(first[:, :], first[:, :], float(TT), None, ALU.mult))
            ch.link(nc.vector.tensor_tensor(slot[:, :, :], before[:, :, :], upto[:, 0:B, :], ALU.add))
            ch.link(nc.vector.tensor_tensor(slot[:, :, :], slot[:, :, :],
                                            first[:, :].rearrange("p (o e) -> p o e", o=1).broadcast_to((128, B, E1)), ALU.add))
            for k in range(TOPK):
                ch.link(nc.vector.tensor_tensor(mine[:, :, :], choice[k][:, :, :], slot[:, :, :], ALU.mult))
                ch.link(nc.vector.tensor_reduce(slotf[:, k, :], mine[:, :, :], AX_X, ALU.add))
            nc.vector.tensor_copy(slots[:, :, :], slotf[:, :, :].rearrange("p k b -> p b k")).then_inc(slots_sb, 1)
            dve.wait_ge(te_ps, 1)
            ch.link(nc.vector.tensor_copy(tile_expert[:, :], TE[0:1, 0:TILES]))
            with dve.Fori(1, NT) as i:
                for f in range(KFS):
                    gated(i, f)


def experts1_phase(nc, r, a, tile_expert, xs_dram, ys_dram):
    NBUF = 4
    with ExitStack() as ctx:
        def sb(name, shape, dt=F32):
            return ctx.enter_context(nc.sbuf_tensor("e1_" + name, shape, dt))

        def sem(name):
            return ctx.enter_context(nc.semaphore("e1_" + name))

        wgu = [sb(f"wgu{v}", [128, KD, 2, F1]) for v in range(NBUF)]
        wd = [sb(f"wd{v}", [FH, 2, D]) for v in range(NBUF)]
        xt = [sb(f"xt{v}", [128, D]) for v in range(NBUF)]
        xT = [sb(f"xT{v}", [128, KD, TT]) for v in range(2)]
        sg = [sb(f"sg{v}", [FH, 2, TT]) for v in range(2)]
        hidden = [sb(f"hidden{v}", [FH, 2, TT]) for v in range(2)]
        yt = [sb(f"yt{v}", [128, D]) for v in range(NBUF)]
        x_in, w_in, y_out = ([sem(f"{n}{v}") for v in range(NBUF)] for n in ("x_in", "w_in", "y_out"))
        xt_ps, xt_sb, g_ps, sg_sb, u_ps, hid_sb, y_ps, y_sb = (sem(n) for n in (
            "xt_ps", "xt_sb", "g_ps", "sg_sb", "u_ps", "hid_sb", "y_ps", "y_sb"))
        AHEAD = 2
        XT, G, U, Y = r.banks[0:2], r.banks[2:4], r.banks[4:6], r.banks[6:8]
        block = ctx.enter_context(nc.Block())

        def later(i, v):
            return i + v // NBUF, v % NBUF

        @block.sync
        def _(sp):
            def load(i, v):
                i, v = later(i, v)
                t = i * NBUF + v
                sp.dma_start(xt[v][:, :], xs_dram[bass.ds(t * TT, TT), :]).then_inc(x_in[v], 16)
                e = sp.value_load(tile_expert[0:1, bass.ds(t, 1)], min_val=0, max_val=E1 - 1)
                sp.dma_start(wgu[v][:, :, :, :].rearrange("p k m n -> p (k m n)"),
                             a["L1_gate_up"][bass.ds(e, 1), :, :].rearrange("o p n -> p (o n)")).then_inc(w_in[v], 16)
                sp.dma_start(wd[v][:, :, :].rearrange("p k n -> p (k n)"),
                             a["L1_down"][bass.ds(e, 1), :, :].rearrange("o p n -> p (o n)")).then_inc(w_in[v], 16)

            def turn(i, last_turn):
                for v in range(NBUF):
                    t = i * NBUF + v
                    sp.wait_ge(y_sb, t + 1 + AHEAD)
                    sp.sem_inc(r.held, 1)
                    sp.dma_start(ys_dram[bass.ds(t * TT, TT), :], yt[v][:, :]).then_inc(y_out[v], 16)
                    if not last_turn:
                        load(i, v + NBUF)

            for v in range(NBUF):
                load(0, v)
            with sp.Fori(0, TILES // NBUF - 1) as i:
                turn(i, False)
            turn(TILES // NBUF - 1, True)
            for v in range(NBUF):
                sp.wait_ge(y_out[v], (1 + TILES // NBUF) * 16)

        @block.tensor
        def _(pe):
            def turn_over(i, v):
                i, v = later(i, v)
                t = i * NBUF + v
                pe.wait_ge(x_in[v], i * 16 + 16)
                pe.wait_ge(xt_sb, t - 1 + AHEAD)
                for k in range(KD):
                    last = nc.tensor.transpose(XT[v % 2][:, k * TT:(k + 1) * TT], xt[v][:, k * 128:(k + 1) * 128], r.ident[:, :])
                last.then_inc(xt_ps, 1)

            def up(i, v):
                i, v = later(i, v)
                t = i * NBUF + v
                pe.wait_ge(xt_sb, t + 1 + AHEAD)
                pe.wait_ge(w_in[v], i * 32 + 32)
                for n, (free, bank, full) in enumerate(((sg_sb, G, g_ps), (hid_sb, U, u_ps))):
                    pe.wait_ge(free, t - 1 + AHEAD)
                    for m in range(2):
                        for k in range(KD):
                            last = nc.tensor.matmul(bank[v % 2][0:FH, m * TT:(m + 1) * TT], wgu[v][:, k, n, m * FH:(m + 1) * FH],
                                                    xT[v % 2][:, k, :], start=k == 0, stop=k == KD - 1)
                    last.then_inc(full, 1)

            def down(i, v):
                t = i * NBUF + v
                pe.wait_ge(hid_sb, t + 1 + AHEAD)
                pe.wait_ge(y_sb, t - 1 + AHEAD)
                for m in range(2):
                    last = nc.tensor.matmul(Y[v % 2][:, 0:D], hidden[v % 2][:, m, :], wd[v][:, m, :], start=m == 0, stop=m == 1)
                last.then_inc(y_ps, 1)

            def turn(i, last_turn):
                for v in range(NBUF):
                    if not (last_turn and v + 1 >= NBUF):
                        up(i, v + 1)
                    if not (last_turn and v + 2 >= NBUF):
                        turn_over(i, v + 2)
                    down(i, v)

            turn_over(0, 0)
            up(0, 0)
            turn_over(0, 1)
            with pe.Fori(0, TILES // NBUF - 1) as i:
                turn(i, False)
            turn(TILES // NBUF - 1, True)

        @block.scalar
        def _(act):
            for s in (xt_sb, sg_sb, hid_sb, y_ps, y_sb):
                act.sem_inc(s, AHEAD)
            for v in range(NBUF):
                act.sem_inc(y_out[v], 16)

            def gate(i, v):
                t = i * NBUF + v
                act.wait_ge(g_ps, t + 1)
                act.wait_ge(hid_sb, t - 1 + AHEAD)
                nc.scalar.activation(sg[v % 2][:, :, :].rearrange("p m t -> p (m t)"), G[v % 2][0:FH, 0:2 * TT], ACT.Silu
                                     ).then_inc(sg_sb, 1)

            def turn(i, last_turn):
                for v in range(NBUF):
                    if not (last_turn and v + 1 >= NBUF):
                        gate(i, v + 1)
                    t = i * NBUF + v
                    act.wait_ge(y_ps, t + 1 + AHEAD)
                    act.wait_ge(y_out[v], i * 16 + 16)
                    nc.scalar.copy(yt[v][:, :], Y[v % 2][:, 0:D]).then_inc(y_sb, 1)

            gate(0, 0)
            with act.Fori(0, TILES // NBUF - 1) as i:
                turn(i, False)
            turn(TILES // NBUF - 1, True)

        @block.vector
        def _(dve):
            def take_tokens(i, v):
                t = i * NBUF + v
                dve.wait_ge(xt_ps, t + 1)
                nc.vector.tensor_copy(xT[v % 2][:, :, :].rearrange("p k t -> p (k t)"), XT[v % 2][:, 0:D]).then_inc(xt_sb, 1)

            def gated(i, v):
                t = i * NBUF + v
                dve.wait_ge(u_ps, t + 1)
                dve.wait_ge(sg_sb, t + 1 + AHEAD)
                nc.vector.tensor_tensor(hidden[v % 2][:, :, :].rearrange("p m t -> p (m t)"),
                                        sg[v % 2][:, :, :].rearrange("p m t -> p (m t)"), U[v % 2][0:FH, 0:2 * TT], ALU.mult
                                        ).then_inc(hid_sb, 1)

            def turn(i, last_turn):
                for v in range(NBUF):
                    if not (last_turn and v + 1 >= NBUF):
                        gated(i, v + 1)
                    if not (last_turn and v + 2 >= NBUF):
                        take_tokens(i, v + 2)

            take_tokens(0, 0)
            gated(0, 0)
            take_tokens(0, 1)
            with dve.Fori(0, TILES // NBUF - 1) as i:
                turn(i, False)
            turn(TILES // NBUF - 1, True)


def combine1_phase(nc, r, w4, slots, sig, SH, ys_dram, out):
    NBUF = 4
    with ExitStack() as ctx:
        def sb(name, shape, dt=F32):
            return ctx.enter_context(nc.sbuf_tensor("c1_" + name, shape, dt))

        def sem(name):
            return ctx.enter_context(nc.semaphore("c1_" + name))

        y = [sb(f"y{n}", [128, TOPK, D]) for n in range(NBUF)]
        y_in = [sem(f"y_in{n}") for n in range(NBUF)]
        x_sb, stored, chain = sem("x_sb"), sem("stored"), sem("dve_chain")
        block = ctx.enter_context(nc.Block())

        @block.gpsimd
        def _(pool):
            for b in range(B):
                if b >= NBUF:
                    pool.wait_ge(x_sb, b - NBUF + 1)
                for k in range(TOPK):
                    nc.gpsimd.indirect_dma_start(
                        out=y[b % NBUF][:, k, :], out_offset=None, in_=ys_dram[:, :],
                        in_offset=bass.IndirectOffsetOnAxis(ap=slots[:, b, k:k + 1], axis=0)).then_inc(y_in[b % NBUF], 16)

        @block.vector
        def _(dve):
            ch = Chain(dve, chain)
            for b in range(B):
                acc = SH[:, b, :]
                ch.link(nc.vector.tensor_scalar(acc, acc, sig[:, b:b + 1], None, ALU.mult))
                dve.wait_ge(y_in[b % NBUF], (b // NBUF + 1) * 16 * TOPK)
                for k in range(TOPK):
                    ch.link(nc.vector.scalar_tensor_tensor(out=acc, in0=y[b % NBUF][:, k, :], scalar=w4[:, b, k:k + 1],
                                                           in1=acc, op0=ALU.mult, op1=ALU.add))
                nc.vector.scalar_tensor_tensor(out=r.X[:, b, :], in0=acc, scalar=r.gates[:, 3:4], in1=r.X[:, b, :],
                                               op0=ALU.mult, op1=ALU.add).then_inc(x_sb, 1)

        @block.sync
        def _(sp):
            for b in range(B):
                sp.wait_ge(x_sb, b + 1)
                sp.dma_start(out[b, :, :], r.X[:, b, :]).then_inc(stored, 16)
            sp.wait_ge(stored, 16 * B)


def build(nc, a, out):
    with ExitStack() as ctx:
        r = Resident(nc, ctx)
        signals = AttentionSignals(nc, ctx)
        xs_dram = nc.dram_tensor("xs_dram", (TILES * TT, D), F32, kind="Internal").ap()
        load_phase(nc, r, a)
        stats_phase(nc, r, "ln_xattn0")
        with nc.sbuf_tensor("attended", [128, B, D], F32) as r.XN:
            attention_phase(nc, r, a, 0, signals)
            stats_phase(nc, r, "ln_ffn0", added=r.XN, gate=r.gates[:, 0:1], clear=signals)
        with ExitStack() as ffn:
            r.XN = ffn.enter_context(nc.sbuf_tensor("XN0", [128, B, D], F32))
            R = ffn.enter_context(nc.sbuf_tensor("R", [128, B, E0 + 1], F32))
            W = ffn.enter_context(nc.sbuf_tensor("W", [128, B, E0 + 1], F32))
            router0_phase(nc, r, a, R, W)
            experts0_phase(nc, r, a, R, W, xs_dram)
        stats_phase(nc, r, "ln_xattn1")
        attention_phase(nc, r, a, 1, signals)
        stats_phase(nc, r, "ln_ffn1")
        r.XN = ctx.enter_context(nc.sbuf_tensor("XN", [128, B, D], F32))
        LG, SH, w4, sig = (ctx.enter_context(nc.sbuf_tensor(n, s, F32)) for n, s in (
            ("LG", [128, B, E1 + 1]), ("SH", [128, B, D]), ("w4", [128, B, TOPK]), ("sig", [128, B])))
        slots = ctx.enter_context(nc.sbuf_tensor("slots", [128, B, TOPK], I32))
        tile_expert = ctx.enter_context(nc.sbuf_tensor("tile_expert", [1, TILES], I32))
        ys_dram = nc.dram_tensor("ys_dram", (TILES * TT, D), F32, kind="Internal").ap()
        with nc.sbuf_tensor("xT", [128, KD, B * S], F32) as xT:
            router1_phase(nc, r, a, LG, xT)
            dispatch1_phase(nc, r, a, LG, xT, w4, slots, sig, tile_expert, xs_dram, SH)
        experts1_phase(nc, r, a, tile_expert, xs_dram, ys_dram)
        combine1_phase(nc, r, w4, slots, sig, SH, ys_dram, out)


def kernel(**inputs):
    import numpy as np
    import concourse.bacc as bacc
    from concourse.bass_utils import run_bass_kernel_spmd as run

    laid_out = {
        "x": inputs["x"],
        "ctx_t": np.asarray(inputs["ctx_1024"]).transpose(0, 2, 1),
        "mask_pad": np.asarray(inputs["mask_BxS2_bf0"]),
        "mask_BxSxS2_ik0": inputs["mask_BxSxS2_ik0"],
        "L0_wq_t": np.asarray(inputs["L0_xattn_Wq"]).T,
        "L0_wk_t": np.asarray(inputs["L0_xattn_Wk"]).T,
        "L0_wv_t": np.asarray(inputs["L0_xattn_Wv"]).T,
        "L1_wq_t": np.asarray(inputs["L1_xattn_w_q"]).T,
        "L1_wk_t": np.asarray(inputs["L1_xattn_w_k"]).T,
        "L1_wv_t": np.asarray(inputs["L1_xattn_w_v"]).T,
        "L1_router_and_gate_w": np.concatenate([np.asarray(inputs["L1_ffn_router_w"]),
                                                np.asarray(inputs["L1_ffn_sh_gate_w"])], axis=1),
        "L1_gate_up": np.stack([np.asarray(inputs["L1_ffn_w_gate"]), np.asarray(inputs["L1_ffn_w_up"])], axis=2)
                      .reshape(E1, KD, 128, 2 * F1).transpose(0, 2, 1, 3).reshape(E1, 128, KD * 2 * F1),
        "L1_down": np.asarray(inputs["L1_ffn_w_down"]).reshape(E1, 2, FH, D).transpose(0, 2, 1, 3).reshape(E1, FH, 2 * D),
        "L1_wo_t": np.asarray(inputs["L1_xattn_w_o"]).T,
    }
    for name in ("g_xattn", "g_ffn", "L0_xattn_bq", "L0_xattn_bk", "L0_xattn_bv", "L1_xattn_b_o", "L0_ffn_router_w1", "L0_ffn_router_w2",
                 "L0_ffn_w1", "L0_ffn_w2", "L0_ffn_w3",
                 "L1_ffn_sh_gate", "L1_ffn_sh_up", "L1_ffn_sh_down"):
        laid_out[name] = inputs[name]

    nc = bacc.Bacc("TRN2", target_bir_lowering=False, num_devices=1)
    arrays, args = {}, {}
    for name, value in laid_out.items():
        value = np.ascontiguousarray(value)
        arrays[f"in_{name}"] = value
        args[name] = nc.dram_tensor(f"in_{name}", value.shape, U8 if value.dtype == bool else mybir.dt.from_np(value.dtype), kind="ExternalInput").ap()
    out = nc.dram_tensor("out", (B, S, D), F32, kind="ExternalOutput").ap()
    build(nc, args, out)
    return run(nc, [arrays], core_ids=[0]).results[0]["out"]
```
